# Optimizing a Trainium2 kernel written in Bass

```python
import numpy as np
import jax
import jax.numpy as jnp

def _softmax(x, axis=-1):
    return jax.nn.softmax(x, axis=axis)

def _gelu(x):
    return jax.nn.gelu(x, approximate=True)

def _silu(x):
    return jax.nn.silu(x)

def _sigmoid(x):
    return jax.nn.sigmoid(x)

def _layernorm(x, axis=-1, eps=1e-05):
    m = jnp.mean(x, axis=axis, keepdims=True)
    v = jnp.var(x, axis=axis, keepdims=True)
    return (x - m) / jnp.sqrt(v + eps)

def _scatter_add(tgt, idx, src, axis=0):
    return tgt.at[idx].add(src)

def _segment_sum(src, seg, n):
    return jax.ops.segment_sum(src, seg, n)
kernel_name = 'mk_gps_d1_gnn_r8_0fdfbe'

def setup_inputs(seed: int=0):
    np.random.seed(seed)
    _w = jnp.asarray

    def _rec_inputs():
        import jax
        import jax.numpy as jnp
        _gk = jax.random.key(seed)
        x = -0.0005963 + 1.001 * jax.random.normal(jax.random.fold_in(_gk, 1), (384, 1024), jnp.float32)
        src = jax.random.randint(jax.random.fold_in(_gk, 2), (12288,), 0, 384, jnp.int32)
        dst = jax.random.randint(jax.random.fold_in(_gk, 3), (12288,), 0, 384, jnp.int32)
        _o = jnp.argsort(dst, stable=True)
        src = src[_o]
        dst = dst[_o]
        edge_type_5 = jax.random.randint(jax.random.fold_in(_gk, 12), (12288,), 0, 5, jnp.int32)
        return (x, src, dst, edge_type_5)
    x, src, dst, edge_type_5 = _rec_inputs()

    def _L0_gnn_setup():
        import jax, jax.numpy as jnp
        import numpy as np
        N = 384
        E = 12288
        IN_F = 1024
        OUT_F = 1024
        H = 16
        D = OUT_F // H
        NUM_ETYPES = 4

        def _build_mask(edge_index, edge_type, edge_type_weights, dtype):
            src, dst = (edge_index[0], edge_index[1])
            w = jax.nn.softplus(edge_type_weights)
            mask = jnp.full((N, N), -jnp.inf, dtype=dtype)
            mask = mask.at[src, dst].set(w[edge_type - 1])
            diag = jnp.diagonal(mask)
            idx = jnp.arange(N)
            mask = mask.at[idx, idx].set(jnp.where(jnp.isneginf(diag), w[3], diag))
            return mask
        key = jax.random.key(seed)
        ks = jax.random.split(key, 20)
        p = lambda k, shape: jax.random.normal(k, shape, dtype=jnp.float32) * 0.02
        return {'x': jax.random.normal(ks[0], (N, IN_F), dtype=jnp.float32), 'edge_index': jax.random.randint(ks[1], (2, E), 0, N), 'edge_type': jax.random.randint(ks[2], (E,), 1, NUM_ETYPES + 1), 'edge_type_weights': jnp.ones((NUM_ETYPES,), jnp.float32) + 0.1 * jax.random.normal(ks[3], (NUM_ETYPES,), dtype=jnp.float32), 'wq': p(ks[4], (OUT_F, IN_F)), 'bq': p(ks[5], (OUT_F,)), 'wk': p(ks[6], (OUT_F, IN_F)), 'bk': p(ks[7], (OUT_F,)), 'wv': p(ks[8], (OUT_F, IN_F)), 'bv': p(ks[9], (OUT_F,)), 'wiq': p(ks[10], (OUT_F, OUT_F)), 'biq': p(ks[11], (OUT_F,)), 'wik': p(ks[12], (OUT_F, OUT_F)), 'bik': p(ks[13], (OUT_F,)), 'wiv': p(ks[14], (OUT_F, OUT_F)), 'biv': p(ks[15], (OUT_F,)), 'wo': p(ks[16], (OUT_F, OUT_F)), 'bo': p(ks[17], (OUT_F,))}
    _L0_gnn_all = _L0_gnn_setup()
    _L0_gnn_in = {k: v for k, v in _L0_gnn_all.items() if k in ('edge_type_weights', 'wq', 'bq', 'wk', 'bk', 'wv', 'bv', 'wiq', 'biq', 'wik', 'bik', 'wiv', 'biv', 'wo', 'bo')}
    del _L0_gnn_all

    def _L0_mix_setup():
        import jax, jax.numpy as jnp
        import numpy as np
        NUM_HEADS = 16
        EPS = 1e-06

        def _split_heads(t, h):
            b, s, d = t.shape
            return t.reshape(b, s, h, d // h).transpose(0, 2, 1, 3)
        key = jax.random.key(seed)
        ks = jax.random.split(key, 6)
        b, s, d = (4, 512, 1024)
        scale = 1.0 / np.sqrt(d)
        return {'x': jax.random.normal(ks[0], (b, s, d), dtype=jnp.float32), 'wq': jax.random.normal(ks[1], (d, d), dtype=jnp.float32) * scale, 'wk': jax.random.normal(ks[2], (d, d), dtype=jnp.float32) * scale, 'wv': jax.random.normal(ks[3], (d, d), dtype=jnp.float32) * scale, 'wo': jax.random.normal(ks[4], (d, d), dtype=jnp.float32) * scale, 'bo': jnp.zeros((d,), dtype=jnp.float32)}
    _L0_mix_all = _L0_mix_setup()
    _L0_mix_in = {k: v for k, v in _L0_mix_all.items() if k in ('wq', 'wk', 'wv', 'wo', 'bo')}
    del _L0_mix_all

    def _L0_ffn_setup():
        import jax, jax.numpy as jnp
        import numpy as np
        DMODEL = 1024
        N_EXPERTS = 32
        EXPERT_SIZE = 512
        N_HEADS = 4
        WEIGHT_SCALE = 1.0
        key = jax.random.key(seed)
        k0, k1, k2, k3 = jax.random.split(key, 4)
        x = jax.random.normal(k0, (2, 256, DMODEL), dtype=jnp.float32)
        expert_sel = jax.random.normal(k1, (N_EXPERTS, DMODEL), dtype=jnp.float32) * DMODEL ** (-0.5)
        keys = jax.random.normal(k2, (N_EXPERTS, DMODEL, EXPERT_SIZE), dtype=jnp.float32) * DMODEL ** (-0.5)
        values = jax.random.normal(k3, (N_EXPERTS, EXPERT_SIZE, DMODEL), dtype=jnp.float32) * (N_EXPERTS * EXPERT_SIZE) ** (-0.5)
        return {'x': x, 'expert_sel': expert_sel, 'keys': keys, 'values': values}
    _L0_ffn_all = _L0_ffn_setup()
    _L0_ffn_in = {k: v for k, v in _L0_ffn_all.items() if k in ('expert_sel', 'keys', 'values')}
    del _L0_ffn_all
    return {'x': x, 'src': src, 'dst': dst, 'edge_type_5': edge_type_5, 'L0_gnn_edge_type_weights': _L0_gnn_in['edge_type_weights'], 'L0_gnn_wq': _L0_gnn_in['wq'], 'L0_gnn_bq': _L0_gnn_in['bq'], 'L0_gnn_wk': _L0_gnn_in['wk'], 'L0_gnn_bk': _L0_gnn_in['bk'], 'L0_gnn_wv': _L0_gnn_in['wv'], 'L0_gnn_bv': _L0_gnn_in['bv'], 'L0_gnn_wiq': _L0_gnn_in['wiq'], 'L0_gnn_biq': _L0_gnn_in['biq'], 'L0_gnn_wik': _L0_gnn_in['wik'], 'L0_gnn_bik': _L0_gnn_in['bik'], 'L0_gnn_wiv': _L0_gnn_in['wiv'], 'L0_gnn_biv': _L0_gnn_in['biv'], 'L0_gnn_wo': _L0_gnn_in['wo'], 'L0_gnn_bo': _L0_gnn_in['bo'], 'L0_mix_wq': _L0_mix_in['wq'], 'L0_mix_wk': _L0_mix_in['wk'], 'L0_mix_wv': _L0_mix_in['wv'], 'L0_mix_wo': _L0_mix_in['wo'], 'L0_mix_bo': _L0_mix_in['bo'], 'L0_ffn_expert_sel': _L0_ffn_in['expert_sel'], 'L0_ffn_keys': _L0_ffn_in['keys'], 'L0_ffn_values': _L0_ffn_in['values']}

def reference(x, src, dst, edge_type_5, L0_gnn_edge_type_weights, L0_gnn_wq, L0_gnn_bq, L0_gnn_wk, L0_gnn_bk, L0_gnn_wv, L0_gnn_bv, L0_gnn_wiq, L0_gnn_biq, L0_gnn_wik, L0_gnn_bik, L0_gnn_wiv, L0_gnn_biv, L0_gnn_wo, L0_gnn_bo, L0_mix_wq, L0_mix_wk, L0_mix_wv, L0_mix_wo, L0_mix_bo, L0_ffn_expert_sel, L0_ffn_keys, L0_ffn_values):
    import jax
    import jax.numpy as jnp

    def _L0_gnn_ref(x, edge_index, edge_type, edge_type_weights, wq, bq, wk, bk, wv, bv, wiq, biq, wik, bik, wiv, biv, wo, bo):
        import jax, jax.numpy as jnp
        import numpy as np
        N = 384
        E = 12288
        IN_F = 1024
        OUT_F = 1024
        H = 16
        D = OUT_F // H
        NUM_ETYPES = 4

        def _build_mask(edge_index, edge_type, edge_type_weights, dtype):
            src, dst = (edge_index[0], edge_index[1])
            w = jax.nn.softplus(edge_type_weights)
            mask = jnp.full((N, N), -jnp.inf, dtype=dtype)
            mask = mask.at[src, dst].set(w[edge_type - 1])
            diag = jnp.diagonal(mask)
            idx = jnp.arange(N)
            mask = mask.at[idx, idx].set(jnp.where(jnp.isneginf(diag), w[3], diag))
            return mask
        q = x @ wq.T + bq
        k = x @ wk.T + bk
        v = x @ wv.T + bv
        q2 = (q @ wiq.T + biq).reshape(N, H, D).transpose(1, 0, 2)
        k2 = (k @ wik.T + bik).reshape(N, H, D).transpose(1, 0, 2)
        v2 = (v @ wiv.T + biv).reshape(N, H, D).transpose(1, 0, 2)
        mask = _build_mask(edge_index, edge_type, edge_type_weights, x.dtype)
        scale = 1.0 / np.sqrt(D).astype(np.float32)
        scores = jnp.einsum('hnd,hmd->hnm', q2, k2) * scale + mask[None]
        attn = jax.nn.softmax(scores, axis=-1)
        out = jnp.einsum('hnm,hmd->hnd', attn, v2)
        out = out.transpose(1, 0, 2).reshape(N, OUT_F)
        return out @ wo.T + bo

    def _L0_mix_ref(x, wq, wk, wv, wo, bo):
        import jax, jax.numpy as jnp
        import numpy as np
        NUM_HEADS = 16
        EPS = 1e-06

        def _split_heads(t, h):
            b, s, d = t.shape
            return t.reshape(b, s, h, d // h).transpose(0, 2, 1, 3)
        h = NUM_HEADS
        q = _split_heads(x @ wq.T, h)
        k = _split_heads(x @ wk.T, h)
        v = _split_heads(x @ wv.T, h)
        qf = jax.nn.elu(q) + 1.0
        kf = jax.nn.elu(k) + 1.0
        k_sum = jnp.sum(kf, axis=-2)
        denom = jnp.sum(qf * k_sum[:, :, None, :], axis=-1, keepdims=True) + EPS
        kv = jnp.einsum('bhsd,bhse->bhde', kf, v)
        q_kv = jnp.einsum('bhsd,bhde->bhse', qf, kv)
        out = q_kv / denom
        b, _, s, dh = out.shape
        out = out.transpose(0, 2, 1, 3).reshape(b, s, h * dh)
        return out @ wo.T + bo

    def _L0_ffn_ref(x, expert_sel, keys, values):
        import jax, jax.numpy as jnp
        import numpy as np
        DMODEL = 1024
        N_EXPERTS = 32
        EXPERT_SIZE = 512
        N_HEADS = 4
        WEIGHT_SCALE = 1.0
        B, S, D = x.shape
        xt = x.reshape(-1, D)
        N = xt.shape[0]
        sel_logits = jnp.einsum('nd,ed->ne', xt, expert_sel)
        gates = jax.nn.sigmoid(sel_logits)
        sel_val, sel_idx = jax.lax.top_k(gates, N_HEADS)
        gate_full = jnp.zeros_like(gates).at[jnp.arange(N)[:, None], sel_idx].set(sel_val)
        scores = jax.nn.relu(jnp.einsum('nd,edf->nef', xt, keys))
        scores = scores * gate_full[:, :, None]
        out = jnp.einsum('nef,efv->nv', scores, values)
        return out.reshape(B, S, -1)
    edge_index = jnp.stack([src, dst])
    xn = _layernorm(x, axis=-1)
    x = x + _L0_gnn_ref(xn, edge_index, edge_type_5, L0_gnn_edge_type_weights, L0_gnn_wq, L0_gnn_bq, L0_gnn_wk, L0_gnn_bk, L0_gnn_wv, L0_gnn_bv, L0_gnn_wiq, L0_gnn_biq, L0_gnn_wik, L0_gnn_bik, L0_gnn_wiv, L0_gnn_biv, L0_gnn_wo, L0_gnn_bo) + _L0_mix_ref(xn[None], L0_mix_wq, L0_mix_wk, L0_mix_wv, L0_mix_wo, L0_mix_bo)[0]
    x = x + _L0_ffn_ref(_layernorm(x, axis=-1)[None], L0_ffn_expert_sel, L0_ffn_keys, L0_ffn_values)[0]
    return x

_drawn_inputs = setup_inputs


def setup_inputs(seed=0):
    import zlib

    import numpy as np

    out = dict(_drawn_inputs(seed))
    spreads = {'L0_mix_bo': (0.0, 0.1)}
    factors = {'L0_gnn_edge_type_weights': 3.941,
     'L0_gnn_wq': 2.854,
     'L0_gnn_bq': 8.0,
     'L0_gnn_wk': 2.888,
     'L0_gnn_bk': 64.0,
     'L0_gnn_wiq': 3.92,
     'L0_gnn_biq': 8.0,
     'L0_gnn_wik': 2.929,
     'L0_gnn_bik': 64.0,
     'L0_mix_wq': 3.88,
     'L0_mix_wk': 2.995,
     'L0_gnn_bv': 3.105}
    for name, (base, spread) in spreads.items():
        noise = np.random.default_rng([zlib.crc32(name.encode()), seed]).standard_normal(out[name].shape)
        drawn = base * np.exp(spread * noise) if base else spread * noise
        out[name] = jnp.asarray(drawn.astype(out[name].dtype))
    for name, factor in factors.items():
        out[name] = (out[name] * factor).astype(out[name].dtype)
    return out
```

```python
from contextlib import ExitStack

import concourse.bass as bass
from concourse import mybir

F32 = mybir.dt.float32
FR = mybir.dt.float32r
BF16 = mybir.dt.bfloat16
F16 = mybir.dt.float16
I32 = mybir.dt.int32
U32 = mybir.dt.uint32
ACT = mybir.ActivationFunctionType
ALU = mybir.AluOpType
AX_X = mybir.AxisListType.X

P = 128
N = 384
NT = N // P
D = 1024
DC = D // P
H = 16
HD = D // H
E = 12288
EC = E // P
LAYERS = EC // 2
NE = 32
ES = 512
EF = ES // P
TOPK = 4
HALF = 512
SLOTS_MAX = (N * TOPK) // P + NE - 1
PAIRS_MIN, PAIRS_MAX = NE // 2, (SLOTS_MAX + 1) // 2
SLOTS = 2 * PAIRS_MAX + 1
FAR = 4096.0
NEG = -1.0e30
EPS_LN = 1e-5
EPS_MIX = 1e-6
RAW = 4
SUB = 4
XRAW = 8
XSUB = 8
XLEAD = 4
LEAD = 3

PROJ = [("mq", "F"), ("mk", "T"), ("mv", "T"), ("v", "F"), ("mo", "T"), ("q", "F"), ("v2", "T"),
        ("q2", "F"), ("k", "F"), ("k2", "F"), ("o", "T")]
CHUNKS = 4 * len(PROJ)
SUBS = 2 * CHUNKS
CONSTS = ["ident", "after", "ones", "pair", "iota", "iotah", "layer", "own"]


def plan_jobs():
    names = ["dup0", "dup1", "xT0", "xT1", "mq0", "mq1", "dup2", "dup3", "mk0", "mk1", "dup4", "dup5",
             "mv0", "mv1", "edge0", "edge1", "lin", "v0", "v1", "mix0", "mix1", "mix2", "mix3",
             "mo0", "mo1", "q0", "q1", "v20", "v21", "q20", "q21", "k0", "k1", "k20", "k21", "att", "o0", "o1"]
    proj = [n for n, _ in PROJ]
    kind = dict(PROJ)
    jobs, bank, signalled, sub, at = {}, 0, 0, 0, 0
    for n in names:
        base = n[:-1]
        if base in proj:
            banks = 4 if kind[base] == "F" else NT
        else:
            banks = {"edge": NT, "at": 0, "li": 3}.get(base, 4)
        subs = 4 if base in proj else 0
        jobs[n] = dict(set=at % 2, first=bank, signals=signalled, banks=banks, sub=sub, sub_end=sub + subs, kind=kind.get(base), base=base,
                       half=int(n[-1]) if n[-1].isdigit() else 0)
        bank += banks
        signalled += banks - 1 if subs or base == "edge" else banks
        sub += subs
        at += 1
    order = list(jobs)
    for k, n in enumerate(order):
        prev = order[k - 2] if k >= 2 else None
        jobs[n]["free"] = jobs[prev]["first"] + jobs[prev]["banks"] if prev else 0
    return jobs, order


def gps_layer_kernel(nc, x, src, dst, typ, etw, W, cols, rows, selT, keys, values, C, xt_dram, y_dram, out):
    jobs, order = plan_jobs()
    assert jobs["o1"]["sub_end"] == SUBS
    ctx = ExitStack()
    with ctx:
        def sb(name, shape, dt):
            return ctx.enter_context(nc.sbuf_tensor(name, shape, dt))

        def sem(name):
            return ctx.enter_context(nc.semaphore(name))

        arena0 = (nc.sbuf_base + 31) // 32 * 32
        arena = sb("arena", [P, 3 * 6144 + 3 * 3072], F32)

        def at(name, shape, dt, off):
            return nc.alloc_sbuf_tensor_at(name, shape, dt, offset=arena0 + off)

        KB = 1024
        A0, A1, A2, F0, F1, F2 = 0, 24 * KB, 48 * KB, 72 * KB, 84 * KB, 96 * KB
        xnh, xnl = at("xnh", [P, DC, N], FR, A0), at("xnl", [P, DC, N], FR, A0 + 12 * KB)
        mah, mal = at("mah", [P, DC, N], FR, A1), at("mal", [P, DC, N], FR, A1 + 12 * KB)
        mbh, mbl = at("mbh", [P, DC, N], FR, A2), at("mbl", [P, DC, N], FR, A2 + 12 * KB)
        xn = at("xn", [P, NT, D], F32, F0)
        mq = at("mq", [P, DC, N], F32, F0)
        q2 = at("q2", [P, DC, N], F32, F0)
        mk = at("mk", [P, NT, D], F32, F1)
        kvbd = at("kvbd", [P, DC, P], F32, F1)
        ksbd = at("ksbd", [P, DC, P], F32, F1 + 4 * KB)
        k2 = at("k2", [P, DC, N], F32, F1)
        mv = at("mv", [P, NT, D], F32, F2)
        v2 = at("v2", [P, NT, D], F32, F2)
        bo_b = at("bo_b", [P, D], F32, A2)
        mbo_b = at("mbo_b", [P, D], F32, A2 + 4 * KB)
        ohs = at("ohs", [P, 4, N], BF16, A2 + 8 * KB)
        ohd = at("ohd", [P, 4, N], BF16, A2 + 11 * KB)
        vcode = at("vcode", [P, NT, N], F32, A2 + 14 * KB)
        cellw = at("cellw", [P, NT, N], F32, A2 + 19 * KB)
        pT = at("pT", [P, 2, NT, N], F32, A0)
        sm = at("sm", [P, 3, N], F32, A0 + 10 * KB)
        pr = at("pr", [P, 3, N], F32, A0 + 15 * KB)
        raw_x = [at(f"raw_x{r}", [P, 4, HALF], F32, A1 + 8 * KB * r) for r in range(3)] + [at("raw_x3", [P, 4, HALF], F32, F2)]
        sub_x = [A0 + 8 * KB * r for r in range(3)] + [F1]
        wh_x = [at(f"wh_x{r}", [P, 2, HALF], FR, o) for r, o in enumerate(sub_x)]
        wl_x = [at(f"wl_x{r}", [P, 2, HALF], FR, o + 4 * KB) for r, o in enumerate(sub_x)]
        xgTh = [at(f"xgTh{p}", [P, DC, P], FR, A2 + 8 * KB * p) for p in range(2)]
        xgTl = [at(f"xgTl{p}", [P, DC, P], FR, A2 + 8 * KB * p + 4 * KB) for p in range(2)]
        hTh = [at(f"hTh{p}", [P, EF, P], FR, A2 + 16 * KB + 4 * KB * p) for p in range(2)]
        hTl = [at(f"hTl{p}", [P, EF, P], FR, A2 + 18 * KB + 4 * KB * p) for p in range(2)]
        xg = [at(f"xg{p}", [P, D], F32, F0 + 4 * KB * p) for p in range(2)]
        hsb = at("hsb", [P, ES], F32, F0 + 8 * KB)
        yk = [at(f"yk{t}", [P, TOPK, D], F32, A0 + 16 * KB * t) for t in range(NT)]
        xt = at("xt", [P, NT, D], F32, F0)
        xtT = at("xtT", [P, DC, N], F32, F1)
        route = A2
        gates = at("gates", [P, NT, NE], F32, route)
        oh = at("oh", [P, NT * TOPK, NE], F32, route + 1 * KB)
        member = at("member", [P, NT, NE], F32, route + 3 * KB)
        rank = at("rank", [P, NT + 1, NE], F32, route + 4 * KB)
        lane1h = at("lane1h", [P, 2, P], F32, route + 5 * KB)
        slot1h = at("slot1h", [P, 2, 3, SLOTS], F32, route + 6 * KB)
        cmp = at("cmp", [P, SLOTS, NE], F32, route + 8 * KB)

        m8 = at("m8", [P, NT, 8], F32, route + 14336)
        i8 = at("i8", [P, NT, 8], U32, route + 14464)
        i8f = at("i8f", [P, NT, 8], F32, route + 14592)
        small = at("small", [P, 8, NE], F32, route + 15360)
        pos = at("pos", [P, 4, NT * TOPK], F32, route + 16384)
        tabf = at("tabf", [P, 3, SLOTS], F32, F2 + 8 * KB)
        gidx, pidx = at("gidx", [P, SLOTS], I32, F2 + 9 * KB), at("pidx", [P, SLOTS], I32, F2 + 9 * KB + 512)
        acc = sb("acc", [P, NT, D], F32)
        raw = sb("raw", [P, RAW, 4, HALF], F32)
        wh = sb("wh", [P, SUB, 2, HALF], FR)
        wl = sb("wl", [P, SUB, 2, HALF], FR)
        mask = sb("mask", [P, NT, N], F32)
        etmp = sb("etmp", [P, 2, HALF], F32)
        biv_b = sb("biv_b", [P, D], F32)
        ysb = [at("ysb0", [P, D], F32, F1 + 8 * KB), etmp[:, :, :].rearrange("p a b -> p (a b)")]
        cst = {n: sb("c_" + n, list(C[n].shape), C[n].dtype) for n in CONSTS}
        ident, after, ones = cst["ident"], cst["after"], cst["ones"]
        col = sb("col", [P, len(cols), DC], F32)
        sel = sb("sel", [P, DC, NE], F32)
        ei = sb("ei", [P, 3, EC], I32)
        ef = sb("ef", [P, 4, EC], F32)
        code = sb("code", [P, EC], F32)
        dup = sb("dup", [P, EC], F32)
        junk = sb("junk", [P, P], F32)
        w4 = sb("w4", [P, 5, 4], F32)
        stats = sb("stats", [P, NT, 2, 6], F32)
        mv2 = sb("mv2", [P, NT, 4], F32)
        kss = sb("kss", [P, DC], F32)
        mx = sb("mx", [P, 4, H * NT], F32)
        gcol = [sb(f"gcol{p}", [P, 1], I32) for p in range(2)]
        pcol = sb("pcol", [P, 1], I32)
        slotx = sb("slotx", [P, SLOTS], I32)
        slots = sb("slots", [P, 1], I32)

        ps = [ctx.enter_context(nc.psum_tensor(f"ps{b}", [P, 512], F32)) for b in range(8)]

        s_x = sem("s_x")
        s_const = sem("s_const")
        s_load = [sem(f"s_load{r}") for r in range(XRAW)]
        s_hi = sem("s_hi")
        s_lo = sem("s_lo")
        s_used = sem("s_used")
        s_bank = sem("s_bank")
        s_free = sem("s_free")
        s_ahi = sem("s_ahi")
        s_dq = sem("s_dq")
        s_dch = sem("s_dch")
        s_ach = sem("s_ach")
        s_pch = sem("s_pch")
        s_seen = sem("s_seen")
        s_bias = sem("s_bias")
        s_xn = sem("s_xn")
        s_spl = sem("s_spl")
        s_oh = sem("s_oh")
        s_ohu = sem("s_ohu")
        s_key = sem("s_key")
        s_s = sem("s_s")
        s_sm = sem("s_sm")
        s_e = sem("s_e")
        s_p = sem("s_p")
        s_t = sem("s_t")
        s_pt = sem("s_pt")
        s_pv = sem("s_pv")
        s_oh_hi = sem("s_oh_hi")
        s_o = sem("s_o")
        s_x2 = sem("s_x2")
        s_xt = sem("s_xt")
        s_xtd = sem("s_xtd")
        s_r = sem("s_r")
        s_rv = sem("s_rv")
        s_ra = sem("s_ra")
        s_tab = sem("s_tab")
        s_g = [sem("s_g0"), sem("s_g1")]
        s_xT = sem("s_xT")
        s_xhi = sem("s_xhi")
        s_xlo = sem("s_xlo")
        s_h = sem("s_h")
        s_hT = sem("s_hT")
        s_hhi = sem("s_hhi")
        s_hlo = sem("s_hlo")
        s_ye0, s_ye1 = sem("s_ye0"), sem("s_ye1")
        s_sc = sem("s_sc")
        s_scd = sem("s_scd")
        s_end = sem("s_end")
        s_yl = [sem(f"s_yl{t}") for t in range(NT)]
        s_fin = sem("s_fin")
        s_out = sem("s_out")

        s_rv_a = sem("s_rv_a")
        n_const = len(CONSTS) + 4 + len(cols) + 4
        att_units = H * NT
        att_free = jobs["att"]["first"]
        MEMBERS_READY = DC + 2 + 2 * NT + 1 + NT * TOPK + 1
        POS_READY = MEMBERS_READY + 1 + NT + 3 + NT + NT * TOPK + 5
        elu_banks = []

        def attention_act(act):
            units = H * NT
            for t in range(units + 6):
                u = t - 1
                if 0 <= u < units:
                    act.wait_ge(s_sm, u + 1)
                    if u >= 3:
                        act.wait_ge(s_t, u - 2)
                    nc.scalar.activation(pr[:, u % 3, :], sm[:, u % 3, :], ACT.Exp, bias=mx[:, 1, u:u + 1],
                                         accum_out=mx[:, 2, u:u + 1]).then_inc(s_e, 1)
                u = t - 2
                if 0 <= u < units:
                    h, n = u // NT, u % NT
                    act.wait_ge(s_t, u + 1)
                    if h >= 2:
                        act.wait_ge(s_pv, h - 1)
                    nc.scalar.activation(pT[:, h % 2, :, n * P:(n + 1) * P],
                                         ps[3 + u % 3][:, 0:N].rearrange("p (c n) -> p c n", n=P), ACT.Copy).then_inc(s_pt, 1)
                u = t - 4
                if u >= 0 and u % NT == NT - 1:
                    h = u // NT
                    r = slice(HD * (h % 2), HD * (h % 2) + HD)
                    act.wait_ge(s_pv, h + 1)
                    nc.scalar.activation(mbh[r, h // 2, :], ps[6 + h % 2][r, 0:N], ACT.Copy).then_inc(s_oh_hi, 1)

        def link_q(dve, ins, count):
            ins.then_inc(s_dq, 1)
            dve.wait_ge(s_dq, count)

        def edge_mask(link):
            link(nc.vector.copy_predicated(vcode[:, :, :], cellw[:, :, :].bitcast(U32), cellw[:, :, :]))
            link(nc.vector.tensor_single_scalar(cellw[:, :, :].bitcast(I32), vcode[:, :, :].bitcast(I32), 23, ALU.logical_shift_right))
            link(nc.vector.tensor_single_scalar(cellw[:, :, :].bitcast(I32), cellw[:, :, :].bitcast(I32), 3, ALU.bitwise_and))
            link(nc.vector.tensor_copy(mask[:, :, :], cellw[:, :, :].bitcast(I32)))
            link(nc.vector.tensor_scalar(cellw[:, :, :], mask[:, :, :], 0.0, w4[:, 4, 0:1], ALU.is_equal, ALU.mult))
            for k in range(1, 4):
                link(nc.vector.tensor_scalar(mt[:, :, :], mask[:, :, :], float(k), w4[:, 4, k:k + 1], ALU.is_equal, ALU.mult))
                link(nc.vector.tensor_tensor(cellw[:, :, :], cellw[:, :, :], mt[:, :, :], ALU.add))
            link(nc.vector.memset(mask[:, :, :], NEG))
            for t in range(NT):
                link(nc.vector.tensor_scalar(mt[:, t, :], cst["iota"][:, :], cst["own"][:, 2 * NT * TOPK + t:2 * NT * TOPK + t + 1],
                                             None, ALU.is_equal))
            link(nc.vector.tensor_copy(mti[:, :, :], mt[:, :, :]))
            link(nc.vector.tensor_scalar(mt[:, :, :], mt[:, :, :], 0.0, w4[:, 4, 3:4], ALU.mult, ALU.add))
            link(nc.vector.copy_predicated(mask[:, :, :], mti[:, :, :], mt[:, :, :]))
            link(nc.vector.copy_predicated(mask[:, :, :], vcode[:, :, :].bitcast(U32), cellw[:, :, :]))

        mt = at("mt", [P, NT, N], F32, F2)
        mti = at("mti", [P, NT, N], U32, F2 + 5 * KB)
        sq = at("sq", [P, N], F32, F2 + 10 * KB)

        def attention_dve(dve):
            units = H * NT
            for t in range(units + 6):
                if t < units:
                    u = t
                    dve.wait_ge(s_s, u + 1)
                    if u >= 3:
                        dve.wait_ge(s_e, u - 2)
                    nc.vector.tensor_tensor_reduce(out=sm[:, u % 3, :], in0=ps[u % 3][:, 0:N], in1=mask[:, u % NT, :], scale=1.0,
                                                   scalar=-3.0e38, op0=ALU.add, op1=ALU.max, accum_out=mx[:, 0, u:u + 1])\
                        .then_inc(s_free, 1)
                    dve.wait_ge(s_free, att_free + u + 1)
                    nc.vector.tensor_scalar(mx[:, 1, u:u + 1], mx[:, 0, u:u + 1], -1.0, None, ALU.mult).then_inc(s_sm, 1)
                u = t - 1
                if 0 <= u < units:
                    dve.wait_ge(s_e, u + 1)
                    nc.vector.reciprocal(mx[:, 3, u:u + 1], mx[:, 2, u:u + 1]).then_inc(s_rv_a, 1)
                    dve.wait_ge(s_rv_a, u + 1)
                    nc.vector.tensor_scalar(pr[:, u % 3, :], pr[:, u % 3, :], mx[:, 3, u:u + 1], None, ALU.mult).then_inc(s_p, 1)
                u = t - 4
                if u >= 0 and u % NT == NT - 1:
                    h = u // NT
                    r = slice(HD * (h % 2), HD * (h % 2) + HD)
                    dve.wait_ge(s_oh_hi, h + 1)
                    nc.vector.tensor_tensor(mbl[r, h // 2, :], ps[6 + h % 2][r, 0:N], mbh[r, h // 2, :].bitcast(F32), ALU.subtract)\
                        .then_inc(s_o, 1)

        def attention_pe(pe):
            units = H * NT
            pe.wait_ge(s_free, att_free)
            for t in range(units + 5):
                if t < units:
                    h, n = t // NT, t % NT
                    r = slice(HD * (h % 2), HD * (h % 2) + HD)
                    if t >= 3:
                        pe.wait_ge(s_free, att_free + t - 2)
                    nc.tensor.matmul(ps[t % 3][:, 0:N], q2[r, h // 2, n * P:(n + 1) * P], k2[r, h // 2, :],
                                     start=True, stop=True).then_inc(s_s, 1)
                u = t - 2
                if 0 <= u < units:
                    pe.wait_ge(s_p, u + 1)
                    if u >= 3:
                        pe.wait_ge(s_pt, u - 2)
                    for c in range(NT):
                        last = nc.tensor.transpose(ps[3 + u % 3][:, c * P:(c + 1) * P], pr[:, u % 3, c * P:(c + 1) * P], ident[:, :])
                    last.then_inc(s_t, 1)
                u = t - 3
                if u >= 0 and u % NT == NT - 1:
                    h = u // NT
                    pe.wait_ge(s_pt, u + 1)
                    if h >= 2:
                        pe.wait_ge(s_o, h - 1)
                    for c in range(NT):
                        last = nc.tensor.matmul(ps[6 + h % 2][:, 0:N], v2[:, c, (h // 2) * P:(h // 2 + 1) * P], pT[:, h % 2, c, :],
                                                start=(c == 0), stop=(c == NT - 1))
                    last.then_inc(s_pv, 1)

        block = ctx.enter_context(nc.Block())

        def bank_filled(eng, j, b):
            if b == j["banks"] - 1 and j["sub_end"] > j["sub"]:
                eng.wait_ge(s_used, j["sub_end"])
            elif b == j["banks"] - 1 and j["base"] == "edge":
                eng.wait_ge(s_ohu, (j["half"] + 1) * LAYERS)
            else:
                eng.wait_ge(s_bank, j["signals"] + b + 1)

        def load_done(c):
            return 16 * (c // RAW + 1)

        raw_of = [raw[:, r, :, :] for r in range(RAW)] + [t[:, :, :] for t in raw_x]
        wh_of = [wh[:, r, :, :] for r in range(SUB)] + [t[:, :, :] for t in wh_x]
        wl_of = [wl[:, r, :, :] for r in range(SUB)] + [t[:, :, :] for t in wl_x]

        def x_load_done(c, j):
            r = c % XRAW
            return 16 * ((CHUNKS // RAW if r < RAW else 0) + c // XRAW + 1) + 16 * j

        @block.sync
        def _(sp):
            for t in range(NT):
                sp.dma_start(acc[:, t, :], x[t * P:(t + 1) * P, :]).then_inc(s_x, 16)
            for c in range(CHUNKS):
                if c >= RAW:
                    sp.wait_ge(s_lo, 2 * (c - RAW + 1))
                n = PROJ[c // 4][0]
                sp.dma_start(raw[:, c % RAW, :, :], W[n][c % 4]).then_inc(s_load[c % RAW], 16)

            def expert_half(src_ap, e, half, c):
                sp.dma_start(raw_of[c % XRAW], src_ap[bass.ds(e, 1), half].rearrange("a p k n -> p (a k) n"))\
                    .then_inc(s_load[c % XRAW], 16)

            def expert_chunks(src_ap, e, c, j):
                for half in range(2):
                    sp.wait_ge(s_lo, SUBS + 2 * (c + half - XRAW + 1) + 16 * j)
                    expert_half(src_ap, e, half, c + half)

            for half in range(2):
                sp.wait_ge(s_lo, 2 * (CHUNKS + half - RAW + 1))
                sp.dma_start(raw_of[half], keys[0, half]).then_inc(s_load[half], 16)
            sp.wait_ge(s_tab, 1)
            last = sp.value_load(slots[0:1, 0:1], min_val=PAIRS_MIN - 1, max_val=PAIRS_MAX - 1)
            with sp.Fori(0, last) as j:
                e = [sp.value_load(slotx[0:1, bass.ds(2 * j + q, 1)], min_val=0, max_val=NE - 1) for q in range(3)]
                for p in range(2):
                    expert_chunks(keys, e[p + 1], 2 + 4 * p, j)
                    expert_chunks(values, e[p], 4 + 4 * p, j)
            e = [sp.value_load(slotx[0:1, bass.ds(2 * last + q, 1)], min_val=0, max_val=NE - 1) for q in range(2)]
            expert_chunks(keys, e[1], 2, last)
            expert_chunks(values, e[0], 4, last)
            expert_chunks(values, e[1], 6, last)
            sp.wait_ge(s_end, 1)
            for t in range(NT):
                sp.dma_start(yk[t][:, :, :], y_dram.rearrange("(k t p) d -> t p k d", k=TOPK, t=NT)[t]).then_inc(s_yl[t], 16)
            for t in range(NT):
                sp.wait_ge(s_fin, t + 1)
                sp.dma_start(out[t * P:(t + 1) * P, :], acc[:, t, :]).then_inc(s_out, 16)
            sp.wait_ge(s_out, 16 * NT)

        @block.gpsimd
        def _(pool):
            pool.wait_ge(s_const, 16 * n_const)
            pool.wait_ge(s_xn, NT)
            for t in range(NT):
                nc.gpsimd.tensor_tensor(acc[:, t, :], acc[:, t, :], bo_b[:, :], ALU.add).then_inc(s_pch, 1)
                pool.wait_ge(s_pch, t + 1)
            for t in range(NT):
                nc.gpsimd.tensor_tensor(acc[:, t, :], acc[:, t, :], mbo_b[:, :], ALU.add).then_inc(s_bias, 1)

            def pool_wait(s, value):
                pool.wait_ge(s, value)
                pool.sem_inc(s_seen, 1)

            def gather(s, p, count):
                nc.gpsimd.tensor_copy(gcol[p][:, :], gidx[:, bass.ds(s, 1)]).then_inc(s_pch, 1)
                pool_wait(s_pch, count)
                nc.gpsimd.indirect_dma_start(xg[p][:, :], None, xt_dram, bass.IndirectOffsetOnAxis(gcol[p][:, :].bitcast(U32), 0),
                                             bounds_check=N - 1, oob_is_err=False).then_inc(s_g[p], 16)

            def pool_slot(j, p, count, ahead):
                s = 2 * j + p
                if ahead:
                    pool_wait(s_xT, s + 2)
                    gather(s + 3, 1 - p, count + 1)
                nc.gpsimd.tensor_copy(pcol[:, :], pidx[:, bass.ds(s, 1)]).then_inc(s_pch, 1)
                pool_wait(s_pch, count + (2 if ahead else 1))
                pool_wait(s_ye0, s + 3)
                pool_wait(s_ye1, s + 3)
                nc.gpsimd.indirect_dma_start(y_dram, bass.IndirectOffsetOnAxis(pcol[:, :].bitcast(U32), 0), ysb[p][:, :], None,
                                             bounds_check=TOPK * N - 1, oob_is_err=False).then_inc(s_sc, 16)
                pool_wait(s_sc, 16 * s + 16)
                pool.sem_inc(s_scd, 1)

            pool.wait_ge(s_xtd, 16 * NT)
            pool.wait_ge(s_t, H * NT + 8)
            for p in range(2):
                nc.gpsimd.memset(xg[p][:, :], 0.0).then_inc(s_pch, 1)
            pool.wait_ge(s_tab, 1)
            last = pool.value_load(slots[0:1, 0:1], min_val=PAIRS_MIN - 1, max_val=PAIRS_MAX - 1)
            pool.sem_inc(s_scd, 2)
            gather(0, 0, NT + 3)
            gather(1, 1, NT + 4)
            pool.wait_ge(s_xT, 1)
            gather(2, 0, NT + 5)
            with pool.Fori(0, last) as j:
                for p in range(2):
                    pool_slot(j, p, 4 * j + 2 * p + NT + 5, True)
            for p in range(2):
                pool_slot(last, p, 4 * last + p + NT + 5, False)
            pool_wait(s_g[0], 16 * last + 32)
            pool.sem_inc(s_end, 1)

        @block.scalar
        def _(act):
            for n in CONSTS:
                act.dma_start(cst[n][:], C[n]).then_inc(s_const, 16)
            act.dma_start(ei[:, 0, :], src).then_inc(s_const, 16)
            act.dma_start(ei[:, 1, :], dst).then_inc(s_const, 16)
            act.dma_start(ei[:, 2, :], typ).then_inc(s_const, 16)
            act.dma_start(w4[:, 0, :], etw.to_broadcast([P, 4])).then_inc(s_const, 16)
            for k, n in enumerate(cols):
                act.dma_start(col[:, k, :], cols[n]).then_inc(s_const, 16)
            act.dma_start(sel[:, :, :], selT).then_inc(s_const, 16)
            act.dma_start(bo_b[:, :], rows["bo"].to_broadcast([P, D])).then_inc(s_const, 16)
            act.dma_start(mbo_b[:, :], rows["mbo"].to_broadcast([P, D])).then_inc(s_const, 16)
            act.dma_start(biv_b[:, :], rows["biv"].to_broadcast([P, D])).then_inc(s_const, 16)

            done = [0]
            chain = [0]

            def link(ins):
                chain[0] += 1
                ins.then_inc(s_ach, 1)
                act.wait_ge(s_ach, chain[0])

            def split(upto):
                for s in range(done[0], min(upto, SUBS)):
                    c = s // 2
                    act.wait_ge(s_load[c % RAW], load_done(c))
                    if s >= SUB:
                        act.wait_ge(s_used, s - SUB + 1)
                    nc.scalar.activation(wh[:, s % SUB], raw[:, c % RAW, 2 * (s % 2):2 * (s % 2) + 2, :], ACT.Copy)\
                        .then_inc(s_hi, 1)
                done[0] = max(done[0], min(upto, SUBS))

            def bank_of(j, b):
                return ps[4 * j["set"] + b]

            colno = {n: k for k, n in enumerate(cols)}
            bias_of = {"v": "bv", "q": "bq", "k": "bk"}
            into = {"v": mah, "q": mbh, "k": mah}
            ahi = [0]
            act.wait_ge(s_spl, 1)
            link(nc.scalar.activation(w4[:, 2, :], w4[:, 1, :], ACT.Exp, scale=-1.0))
            nc.scalar.activation(w4[:, 3, :], w4[:, 2, :], ACT.Ln, bias=1.0).then_inc(s_ra, 1)
            split(2)
            for name in order:
                j = jobs[name]
                if name == "att":
                    attention_act(act)
                    continue
                split(j["sub_end"] + LEAD)
                oh_ = int(name[-1]) if name[-1].isdigit() else 0
                for b in range(j["banks"]):
                    pb = bank_of(j, b)
                    if b == 1:
                        split(j["sub_end"] + LEAD + 1)
                    base = j["base"]
                    if name.startswith("xT"):
                        bank_filled(act, j, b)
                        nc.scalar.activation(xnh[:, 4 * oh_ + b, :], pb[:, 0:N], ACT.Copy).then_inc(s_ahi, 1)
                    elif base in into:
                        bank_filled(act, j, b)
                        o = 4 * oh_ + b
                        nc.scalar.activation(into[base][:, o, :], pb[:, 0:N], ACT.Identity,
                                             bias=col[:, colno[bias_of[base]], o:o + 1]).then_inc(s_ahi, 1)
                    elif base in ("mq", "mk"):
                        width = N if base == "mq" else HALF
                        bank_filled(act, j, b)
                        if len(elu_banks) >= 2:
                            act.wait_ge(s_free, elu_banks[-2] + 1)
                        t = etmp[:, len(elu_banks) % 2, 0:width]
                        link(nc.scalar.activation(t, pb[:, 0:width], ACT.Relu, scale=-1.0))
                        nc.scalar.activation(t, t, ACT.Exp, scale=-1.0).then_inc(s_ahi, 1)
                        elu_banks.append(j["first"] + b)
                    elif base == "mix" and b % 2 == 0:
                        c = 2 * oh_ + b // 2
                        act.wait_ge(s_dq, c + 1)
                        nc.scalar.activation(mbh[:, c, :], etmp[:, c % 2, 0:N], ACT.Copy).then_inc(s_ahi, 1)
            for t in range(NT):
                act.wait_ge(s_xt, t + 1)
                act.dma_start(xt_dram[t * P:(t + 1) * P, :], xt[:, t, :]).then_inc(s_xtd, 16)
            def split_expert(k, j):
                c = k // 2
                act.wait_ge(s_load[c % XRAW], x_load_done(c, j))
                if k >= XSUB or k < SUB:
                    act.wait_ge(s_used, SUBS + k + 1 - (XSUB if k >= XSUB else SUB) + 16 * j)
                nc.scalar.activation(wh_of[k % XSUB], raw_of[c % XRAW][:, 2 * (k % 2):2 * (k % 2) + 2, :], ACT.Copy)\
                    .then_inc(s_hi, 1)

            for k in range(XLEAD):
                split_expert(k, 0)
            act.wait_ge(s_r, 1)
            nc.scalar.activation(gates[:, :, :], ps[0][:, 0:NT * NE].rearrange("p (t e) -> p t e", e=NE), ACT.Exp,
                                 scale=-1.0).then_inc(s_ra, 1)

            def x_hi(count, p):
                act.wait_ge(s_xT, count)
                for b in range(2):
                    ins = nc.scalar.activation(xgTh[p][:, 4 * b:4 * b + 4, :], ps[2 + b][:, :].rearrange("p (c t) -> p c t", t=P), ACT.Copy)
                ins.then_inc(s_xhi, 1)

            def h_out(used, s):
                act.wait_ge(s_used, used)
                nc.scalar.activation(hsb[:, :], ps[0][:, :], ACT.Relu, scale=tabf[:, 2, bass.ds(s, 1)]).then_inc(s_h, 1)

            def h_hi(count, p):
                act.wait_ge(s_hT, count)
                nc.scalar.activation(hTh[p][:, :, :], ps[1][:, :].rearrange("p (c t) -> p c t", t=P), ACT.Copy).then_inc(s_hhi, 1)

            def y_second(j, p, used):
                act.wait_ge(s_used, used)
                act.wait_ge(s_scd, 2 * j + p + 1)
                nc.scalar.activation(ysb[p][:, HALF:D], ps[5 + 2 * p][:, :], ACT.Copy).then_inc(s_ye1, 1)

            def act_slot(j, p, ahead):
                k = 8 * p
                used = SUBS + 8 * p + 16 * j
                for q in range(8, 10):
                    split_expert(k + q, j)
                h_out(used + 8, 2 * j + p + 1)
                split_expert(k + 10, j)
                if ahead:
                    x_hi(2 * j + p + 3, p)
                split_expert(k + 11, j)
                h_hi(2 * j + p + 2, 1 - p)
                for q in range(12, 14):
                    split_expert(k + q, j)
                y_second(j, p, used + 12)
                for q in range(14, 16):
                    split_expert(k + q, j)

            act.wait_ge(s_tab, 1)
            last = act.value_load(slots[0:1, 0:1], min_val=PAIRS_MIN - 1, max_val=PAIRS_MAX - 1)
            act.sem_inc(s_ye1, 2)
            x_hi(1, 0)
            for k in range(4, 6):
                split_expert(k, 0)
            x_hi(2, 1)
            for k in range(6, 4 + XLEAD):
                split_expert(k, 0)
            h_out(SUBS + 4, 0)
            h_hi(1, 0)
            with act.Fori(0, last) as j:
                for p in range(2):
                    act_slot(j, p, True)
            act_slot(last, 0, False)
            y_second(last, 1, SUBS + 16 + 16 * last)

        @block.vector
        def _(dve):
            chain = [0]

            def link(ins):
                chain[0] += 1
                ins.then_inc(s_dch, 1)
                dve.wait_ge(s_dch, chain[0])

            done = [0]

            def split(upto):
                for s in range(done[0], min(upto, SUBS)):
                    dve.wait_ge(s_hi, s + 1)
                    nc.vector.tensor_tensor(wl[:, s % SUB], raw[:, (s // 2) % RAW, 2 * (s % 2):2 * (s % 2) + 2, :],
                                            wh[:, s % SUB].bitcast(F32), ALU.subtract).then_inc(s_lo, 1)
                done[0] = max(done[0], min(upto, SUBS))

            def norms(out_tile, done_sem):
                for t in range(NT):
                    for k in range(2):
                        link(nc.vector.bn_stats(stats[:, t, k, :], acc[:, t, k * 512:(k + 1) * 512]))
                    link(nc.vector.bn_aggr(mv2[:, t, 0:2], stats[:, t, :, :].rearrange("p a b -> p (a b)")))
                v, y, z = mv2[:, :, 1], mv2[:, :, 2], mv2[:, :, 3]
                link(nc.vector.tensor_scalar(v, v, EPS_LN, None, ALU.add))
                link(nc.vector.tensor_single_scalar(z.bitcast(I32), v.bitcast(I32), 1, ALU.logical_shift_right))
                link(nc.vector.tensor_scalar(y.bitcast(I32), z.bitcast(I32), -1.0, float(0x5F3759DF), ALU.mult, ALU.add))
                for _ in range(3):
                    link(nc.vector.tensor_tensor(z, y, y, ALU.mult))
                    link(nc.vector.tensor_tensor(z, z, v, ALU.mult))
                    link(nc.vector.tensor_scalar(z, z, -0.5, 1.5, ALU.mult, ALU.add))
                    link(nc.vector.tensor_tensor(y, y, z, ALU.mult))
                for t in range(NT):
                    nc.vector.tensor_scalar(out_tile[:, t, :], acc[:, t, :], mv2[:, t, 0:1], mv2[:, t, 2:3],
                                            ALU.subtract, ALU.mult).then_inc(done_sem, 1)

            dve.wait_ge(s_x, 16 * NT)
            norms(xn, s_xn)
            dve.wait_ge(s_const, 16 * n_const)
            link(nc.vector.tensor_copy(ef[:, 0:3, :], ei[:, :, :]))
            nc.vector.scalar_tensor_tensor(ef[:, 3, :], ef[:, 0, :], float(N), ef[:, 1, :], ALU.mult, ALU.add).then_inc(s_key, 1)
            dve.wait_ge(s_key, 1)
            link(nc.vector.tensor_scalar(ei[:, 2, :], ef[:, 2, :], 3.0, None, ALU.add))
            link(nc.vector.tensor_single_scalar(ei[:, 2, :], ei[:, 2, :], 3, ALU.bitwise_and))
            link(nc.vector.tensor_tensor(ei[:, 2, :], ei[:, 2, :], cst["layer"][:, :], ALU.add))
            link(nc.vector.tensor_single_scalar(code[:, :].bitcast(I32), ei[:, 2, :], 23, ALU.logical_shift_left))
            nc.vector.scalar_tensor_tensor(w4[:, 1, :], w4[:, 0, :], -1.0, w4[:, 0, :], ALU.mult, ALU.max).then_inc(s_spl, 1)
            dve.wait_ge(s_ra, 1)
            link(nc.vector.scalar_tensor_tensor(w4[:, 4, :], w4[:, 0, :], 0.0, w4[:, 3, :], ALU.max, ALU.add))

            colno = {n: k for k, n in enumerate(cols)}
            bias_of = {"v": "bv", "q": "bq", "k": "bk", "q2": "biq", "k2": "bik"}
            parts = {"v": (mah, mal), "q": (mbh, mbl), "k": (mah, mal)}
            ahi = 0
            quotients = elus = 0
            for name in order:
                j = jobs[name]
                if name == "att":
                    attention_dve(dve)
                    continue
                split(j["sub_end"] + LEAD)
                half = int(name[-1]) if name[-1].isdigit() else 0
                base = j["base"]
                if name.startswith("edge"):
                    for c in range(LAYERS):
                        g = half * LAYERS + c
                        if g >= 4:
                            dve.wait_ge(s_ohu, g - 3)
                        nc.vector.tensor_scalar(ohs[:, g % 4, :], cst["iotah"][:, :], ef[:, 0, g:g + 1], None, ALU.is_equal)
                        nc.vector.tensor_scalar(ohd[:, g % 4, :], cst["iotah"][:, :], ef[:, 1, g:g + 1], ef[:, 2, g:g + 1],
                                                ALU.is_equal, ALU.mult).then_inc(s_oh, 1)
                for b in range(j["banks"]):
                    if b == 1:
                        split(j["sub_end"] + LEAD + 1)
                    pb = ps[4 * j["set"] + b]
                    if name != "lin":
                        bank_filled(dve, j, b)
                    if name.startswith("dup"):
                        for q in range(4):
                            g = 16 * half + 4 * b + q
                            last = nc.vector.scalar_tensor_tensor(junk[:, :], pb[:, q * P:(q + 1) * P], ef[:, 3, g:g + 1],
                                                                  after[:, :], ALU.is_equal, ALU.mult, accum_out=dup[:, g:g + 1])
                            if q < 3:
                                link(last)
                        last.then_inc(s_free, 1)
                        dve.wait_ge(s_free, j["first"] + b + 1)
                        if name == "dup5" and b == 3:
                            link(nc.vector.scalar_tensor_tensor(ef[:, 2, :], dup[:, :], 0.5, code[:, :], ALU.is_lt, ALU.mult))
                    elif name.startswith("xT"):
                        ahi += 1
                        dve.wait_ge(s_ahi, ahi)
                        nc.vector.tensor_tensor(xnl[:, 4 * half + b, :], pb[:, 0:N], xnh[:, 4 * half + b, :].bitcast(F32),
                                                ALU.subtract).then_inc(s_free, 1)
                    elif base in parts:
                        hi, lo = parts[base]
                        o = 4 * half + b
                        ahi += 1
                        dve.wait_ge(s_ahi, ahi)
                        nc.vector.scalar_tensor_tensor(lo[:, o, :], pb[:, 0:N], col[:, colno[bias_of[base]], o:o + 1],
                                                       hi[:, o, :].bitcast(F32), ALU.add, ALU.subtract).then_inc(s_free, 1)
                    elif base in ("mq", "mk"):
                        width = N if base == "mq" else HALF
                        to = mq[:, 4 * half + b, :] if base == "mq" else mk[:, b, half * HALF:(half + 1) * HALF]
                        t = etmp[:, elus % 2, 0:width]
                        ahi += 1
                        dve.wait_ge(s_ahi, ahi)
                        elus += 1
                        nc.vector.scalar_tensor_tensor(to, pb[:, 0:width], 0.0, t, ALU.max, ALU.add).then_inc(s_free, 1)
                    elif base in ("q2", "k2"):
                        o = 4 * half + b
                        to = q2 if base == "q2" else k2
                        nc.vector.tensor_scalar(to[:, o, :], pb[:, 0:N], col[:, colno[bias_of[base]], o:o + 1],
                                                float(HD) ** -0.5 if base == "q2" else 1.0, ALU.add, ALU.mult).then_inc(s_free, 1)
                    elif base == "mv":
                        nc.vector.tensor_copy(mv[:, b, half * HALF:(half + 1) * HALF], pb[:, :]).then_inc(s_free, 1)
                    elif base == "v2":
                        cs = slice(half * HALF, (half + 1) * HALF)
                        nc.vector.tensor_tensor(v2[:, b, cs], pb[:, :], biv_b[:, cs], ALU.add).then_inc(s_free, 1)
                    elif base in ("mo", "o"):
                        cs = slice(half * HALF, (half + 1) * HALF)
                        nc.vector.tensor_tensor(acc[:, b, cs], pb[:, :], acc[:, b, cs], ALU.add).then_inc(s_free, 1)
                    elif name.startswith("edge"):
                        to = vcode if half == 0 else cellw
                        nc.vector.tensor_copy(to[:, b, :], pb[:, 0:N]).then_inc(s_free, 1)
                    elif name == "lin":
                        if b == 0:
                            bank_filled(dve, j, 2)
                            link(nc.vector.tensor_copy(kss[:, :], ps[4 * j["set"] + 2][:, 0:DC]))
                        if b < 2:
                            last = nc.vector.tensor_tensor(kvbd[:, 4 * b:4 * b + 4, :], pb[:, :].rearrange("p (c e) -> p c e", e=P),
                                                           cst["pair"][:, None, :].to_broadcast([P, 4, P]), ALU.mult)
                        else:
                            for c in range(DC):
                                last = nc.vector.tensor_scalar(ksbd[:, c, :], cst["pair"][:, :], kss[:, c:c + 1], None, ALU.mult)
                                if c < DC - 1:
                                    link(last)
                        last.then_inc(s_free, 1)
                    elif base == "mix":
                        c = 2 * half + b // 2
                        if c == 0 and b == 0:
                            dve.wait_ge(s_bias, NT)
                        if b % 2 == 0:
                            bank_filled(dve, j, b + 1)
                            dn = ps[4 * j["set"] + b + 1]
                            nc.vector.tensor_scalar(sq[:, 0:N], dn[:, 0:N], EPS_MIX, None, ALU.add).then_inc(s_free, 1)
                            dve.wait_ge(s_free, j["first"] + b + 1)
                            quotients += 1
                            link(nc.vector.reciprocal(sq[:, 0:N], sq[:, 0:N]))
                            link_q(dve, nc.vector.tensor_tensor(etmp[:, c % 2, 0:N], pb[:, 0:N], sq[:, 0:N], ALU.mult), quotients)
                            ahi += 1
                            dve.wait_ge(s_ahi, ahi)
                            nc.vector.tensor_tensor(mbl[:, c, :], etmp[:, c % 2, 0:N], mbh[:, c, :].bitcast(F32), ALU.subtract)\
                                .then_inc(s_free, 1)
                if name == "lin":
                    edge_mask(link)
                if name == "o1":
                    dve.wait_ge(s_free, j["first"] + j["banks"] + att_units)
            def split_expert(k, j):
                dve.wait_ge(s_hi, SUBS + k + 1 + 16 * j)
                nc.vector.tensor_tensor(wl_of[k % XSUB], raw_of[(k // 2) % XRAW][:, 2 * (k % 2):2 * (k % 2) + 2, :],
                                        wh_of[k % XSUB].bitcast(F32), ALU.subtract).then_inc(s_lo, 1)

            norms(xt, s_xt)
            for k in range(XLEAD):
                split_expert(k, 0)
            for b in range(8):
                dve.wait_ge(s_t, H * NT + b + 1)
                nc.vector.tensor_copy(xtT[:, b, :], ps[b][:, 0:N]).then_inc(s_rv, 1)
            rv = [8]

            def rlink(ins):
                rv[0] += 1
                ins.then_inc(s_rv, 1)
                dve.wait_ge(s_rv, rv[0])

            dve.wait_ge(s_ra, 2)
            rlink(nc.vector.tensor_scalar(gates[:, :, :], gates[:, :, :], 1.0, None, ALU.add))
            rlink(nc.vector.reciprocal(gates[:, :, :], gates[:, :, :]))
            iota = cst["iota"]
            for t in range(NT):
                rlink(nc.vector.max(m8[:, t, :], gates[:, t, :]))
                rlink(nc.vector.max_index(i8[:, t, :], m8[:, t, :], gates[:, t, :]))
            rlink(nc.vector.tensor_copy(i8f[:, :, :], i8[:, :, :]))
            for t in range(NT):
                for k in range(TOPK):
                    rlink(nc.vector.tensor_scalar(oh[:, t * TOPK + k, :], iota[:, 0:NE], i8f[:, t, k:k + 1], None, ALU.is_equal))
            rlink(nc.vector.tensor_reduce(member[:, :, :], oh[:, :, :].rearrange("p (t k) e -> p t e k", k=TOPK), AX_X, ALU.add))
            members_ready = rv[0]
            assert members_ready == MEMBERS_READY
            dve.wait_ge(s_r, 2)
            rlink(nc.vector.tensor_copy(rank[:, :, :], ps[1][:, 0:(NT + 1) * NE].rearrange("p (t e) -> p t e", e=NE)))
            tot = rank[:, NT, :]
            rlink(nc.vector.memset(small[:, 1, :], 1.0))
            for t in range(1, NT):
                rlink(nc.vector.scalar_tensor_tensor(small[:, 1, :], tot, t * P + 0.5, small[:, 1, :], ALU.is_gt, ALU.add))
            rlink(nc.vector.memset(small[:, 2, :], 0.0))
            rlink(nc.vector.tensor_tensor_scan(small[:, 3, :], small[:, 1, :], small[:, 2, :], 0.0, ALU.add, ALU.add))
            rlink(nc.vector.tensor_tensor(small[:, 4, :], small[:, 3, :], small[:, 1, :], ALU.subtract))
            for t in range(NT):
                rlink(nc.vector.scalar_tensor_tensor(rank[:, t, :], small[:, 4, :], float(P), rank[:, t, :], ALU.mult, ALU.add))
            for t in range(NT):
                for k in range(TOPK):
                    q = t * TOPK + k
                    rlink(nc.vector.tensor_tensor_reduce(out=small[:, 5, :], in0=oh[:, q, :], in1=rank[:, t, :], scale=1.0, scalar=0.0,
                                                         op0=ALU.mult, op1=ALU.add, accum_out=pos[:, 0, q:q + 1]))
            posi = pos[:, 3, :].bitcast(I32)
            rlink(nc.vector.tensor_copy(posi, pos[:, 0, :]))
            rlink(nc.vector.tensor_single_scalar(pos[:, 1, :].bitcast(I32), posi, P - 1, ALU.bitwise_and))
            rlink(nc.vector.tensor_single_scalar(pos[:, 2, :].bitcast(I32), posi, 7, ALU.logical_shift_right))
            rlink(nc.vector.tensor_copy(pos[:, 0, :], pos[:, 1, :].bitcast(I32)))
            rlink(nc.vector.tensor_copy(pos[:, 3, :], pos[:, 2, :].bitcast(I32)))
            own = cst["own"]
            for q in range(NT * TOPK):
                if q >= 2:
                    dve.wait_ge(s_r, 3 + q - 2)
                rlink(nc.vector.tensor_scalar(lane1h[:, q % 2, :], iota[:, 0:P], pos[:, 0, q:q + 1], None, ALU.is_equal))
                for m in range(2):
                    rlink(nc.vector.tensor_scalar(slot1h[:, q % 2, m, :], iota[:, 0:SLOTS], pos[:, 3, q:q + 1],
                                                  own[:, m * NT * TOPK + q:m * NT * TOPK + q + 1], ALU.is_equal, ALU.mult))
                rlink(nc.vector.tensor_scalar(slot1h[:, q % 2, 2, :], iota[:, 0:SLOTS], pos[:, 3, q:q + 1],
                                              m8[:, q // TOPK, q % TOPK:q % TOPK + 1], ALU.is_equal, ALU.mult))
            rlink(nc.vector.tensor_tensor(cmp[:, :, :], small[:, 3, None, :].to_broadcast([P, SLOTS, NE]),
                                          iota[:, 0:SLOTS, None].to_broadcast([P, SLOTS, NE]), ALU.is_le))
            rlink(nc.vector.tensor_reduce(tabf[:, 0, :], cmp[:, :, :], AX_X, ALU.add))
            rlink(nc.vector.tensor_scalar(slotx[:, :], tabf[:, 0, :], float(NE - 1), None, ALU.min))
            rlink(nc.vector.tensor_scalar(slots[:, :], small[:, 3, NE - 1:NE], -1.0, None, ALU.add))
            rlink(nc.vector.tensor_single_scalar(slots[:, :], slots[:, :], 1, ALU.logical_shift_right))
            dve.wait_ge(s_r, 2 + NT * TOPK)
            tab = ps[2][:, 0:3 * SLOTS].rearrange("p (m s) -> p m s", s=SLOTS)
            rlink(nc.vector.tensor_scalar(gidx[:, :], tab[:, 0, :], -1.0, FAR, ALU.mult, ALU.add))
            rlink(nc.vector.tensor_scalar(pidx[:, :], tab[:, 1, :], -1.0, FAR, ALU.mult, ALU.add))
            nc.vector.tensor_copy(tabf[:, 2, :], tab[:, 2, :]).then_inc(s_tab, 1)

            def x_lo(count, p):
                dve.wait_ge(s_xhi, count)
                for b in range(2):
                    ins = nc.vector.tensor_tensor(xgTl[p][:, 4 * b:4 * b + 4, :], ps[2 + b][:, :].rearrange("p (c t) -> p c t", t=P),
                                                  xgTh[p][:, 4 * b:4 * b + 4, :].bitcast(F32), ALU.subtract)
                ins.then_inc(s_xlo, 1)

            def h_lo(count, p):
                dve.wait_ge(s_hhi, count)
                nc.vector.tensor_tensor(hTl[p][:, :, :], ps[1][:, :].rearrange("p (c t) -> p c t", t=P),
                                        hTh[p][:, :, :].bitcast(F32), ALU.subtract).then_inc(s_hlo, 1)

            def y_first(j, p, used):
                dve.wait_ge(s_used, used)
                dve.wait_ge(s_scd, 2 * j + p + 1)
                nc.vector.tensor_copy(ysb[p][:, 0:HALF], ps[4 + 2 * p][:, :]).then_inc(s_ye0, 1)

            def dve_slot(j, p, ahead):
                k = 8 * p
                for q in range(8, 11):
                    split_expert(k + q, j)
                if ahead:
                    x_lo(2 * j + p + 3, p)
                split_expert(k + 11, j)
                y_first(j, p, SUBS + 10 + 8 * p + 16 * j)
                h_lo(2 * j + p + 2, 1 - p)
                for q in range(12, 16):
                    split_expert(k + q, j)

            dve.wait_ge(s_tab, 1)
            last = dve.value_load(slots[0:1, 0:1], min_val=PAIRS_MIN - 1, max_val=PAIRS_MAX - 1)
            dve.sem_inc(s_ye0, 2)
            x_lo(1, 0)
            for k in range(4, 6):
                split_expert(k, 0)
            x_lo(2, 1)
            for k in range(6, 4 + XLEAD):
                split_expert(k, 0)
            h_lo(1, 0)
            with dve.Fori(0, last) as j:
                for p in range(2):
                    dve_slot(j, p, True)
            dve_slot(last, 0, False)
            y_first(last, 1, SUBS + 14 + 16 * last)
            for t in range(NT):
                dve.wait_ge(s_yl[t], 16)
                for k in range(TOPK):
                    ins = nc.vector.tensor_tensor(acc[:, t, :], acc[:, t, :], yk[t][:, k, :], ALU.add)
                    if k < TOPK - 1:
                        link(ins)
                ins.then_inc(s_fin, 1)

        @block.tensor
        def _(pe):
            def mm3(o, ah, al, bh_, bl_, start, stop):
                nc.tensor.matmul(o, ah, bh_, start=start, stop=False)
                nc.tensor.matmul(o, ah, bl_, start=False, stop=False)
                return nc.tensor.matmul(o, al, bh_, start=False, stop=stop)

            src_of = {"mq": (xnh, xnl), "mk": (xnh, xnl), "mv": (xnh, xnl), "v": (xnh, xnl), "q": (xnh, xnl), "k": (xnh, xnl),
                      "mo": (mbh, mbl), "v2": (mah, mal), "q2": (mbh, mbl), "k2": (mah, mal), "o": (mbh, mbl)}
            needs = {"mo": "mix3", "v2": "v1", "q2": "q1", "k2": "k1", "mq": "xT1"}
            end = {n: jobs[n]["first"] + jobs[n]["banks"] for n in order}
            pe.wait_ge(s_const, 16 * n_const)
            for name in order:
                j = jobs[name]
                if name == "att":
                    attention_pe(pe)
                    continue
                half = int(name[-1]) if name[-1].isdigit() else 0
                base = j["base"]
                shift = att_units if name in ("o0", "o1") else 0
                if j["free"]:
                    pe.wait_ge(s_free, j["free"] + shift)
                if base in needs and half == 0:
                    pe.wait_ge(s_free, end[needs[base]])
                if name == "o0":
                    pe.wait_ge(s_o, H)
                bk = [ps[4 * j["set"] + b] for b in range(4)]
                if name.startswith("dup"):
                    pe.wait_ge(s_key, 1)
                    for b in range(4):
                        for q in range(4):
                            g = 16 * half + 4 * b + q
                            last = nc.tensor.transpose(bk[b][:, q * P:(q + 1) * P], ef[:, 3, g:g + 1].to_broadcast([P, P]), ident[:, :])
                        last.then_inc(s_bank, 1)
                elif name.startswith("xT"):
                    pe.wait_ge(s_xn, NT)
                    for b in range(4):
                        for t in range(NT):
                            o = 4 * half + b
                            last = nc.tensor.transpose(bk[b][:, t * P:(t + 1) * P], xn[:, t, o * P:(o + 1) * P], ident[:, :])
                        last.then_inc(s_bank, 1)
                elif name.startswith("edge"):
                    for c in range(LAYERS):
                        g = half * LAYERS + c
                        pe.wait_ge(s_oh, g + 1)
                        for t in range(NT):
                            last = nc.tensor.matmul(bk[t][:, 0:N], ohs[:, g % 4, t * P:(t + 1) * P], ohd[:, g % 4, :],
                                                    start=(c == 0), stop=(c == LAYERS - 1))
                            if c == LAYERS - 1 and t < NT - 1:
                                last.then_inc(s_bank, 1)
                        last.then_inc(s_ohu, 1)
                elif name == "lin":
                    pe.wait_ge(s_free, end["mv1"])
                    for c in range(DC):
                        cs = slice(c * P, (c + 1) * P)
                        for t in range(NT):
                            last = nc.tensor.matmul(bk[c // 4][:, (c % 4) * P:(c % 4 + 1) * P], mk[:, t, cs], mv[:, t, cs],
                                                    start=(t == 0), stop=(t == NT - 1))
                        if c % 4 == 3:
                            last.then_inc(s_bank, 1)
                    for c in range(DC):
                        cs = slice(c * P, (c + 1) * P)
                        for t in range(NT):
                            last = nc.tensor.matmul(bk[2][:, c:c + 1], mk[:, t, cs], ones[:, 0:1], start=(t == 0), stop=(t == NT - 1))
                    last.then_inc(s_bank, 1)
                elif base == "mix":
                    if half == 0:
                        pe.wait_ge(s_free, end["lin"])
                    for b in range(4):
                        c = 2 * half + b // 2
                        w = (kvbd, ksbd)[b % 2]
                        nc.tensor.matmul(bk[b][:, 0:N], w[:, c, :], mq[:, c, :], start=True, stop=True).then_inc(s_bank, 1)
                else:
                    xh, xl = src_of[base]
                    for q in range(4):
                        s = j["sub"] + q
                        pe.wait_ge(s_lo, s + 1)
                        for kb in range(2):
                            i = 2 * q + kb
                            first, fin = q == 0 and kb == 0, q == 3 and kb == 1
                            for b in range(j["banks"]):
                                if j["kind"] == "F":
                                    bs = slice(b * P, (b + 1) * P)
                                    last = mm3(bk[b][:, 0:N], wh[:, s % SUB, kb, bs], wl[:, s % SUB, kb, bs],
                                               xh[:, i, :], xl[:, i, :], first, fin)
                                else:
                                    bs = slice(b * P, (b + 1) * P)
                                    last = mm3(bk[b][:, :], xh[:, i, bs], xl[:, i, bs],
                                               wh[:, s % SUB, kb, :], wl[:, s % SUB, kb, :], first, fin)
                                if fin and b < j["banks"] - 1:
                                    last.then_inc(s_bank, 1)
                        last.then_inc(s_used, 1)

            for b in range(8):
                pe.wait_ge(s_xt, NT)
                for t in range(NT):
                    last = nc.tensor.transpose(ps[b][:, t * P:(t + 1) * P], xt[:, t, b * P:(b + 1) * P], ident[:, :])
                last.then_inc(s_t, 1)
            pe.wait_ge(s_rv, 8)
            for t in range(NT):
                for b in range(DC):
                    last = nc.tensor.matmul(ps[0][:, t * NE:(t + 1) * NE], xtT[:, b, t * P:(t + 1) * P], sel[:, b, :],
                                            start=(b == 0), stop=(b == DC - 1))
            last.then_inc(s_r, 1)
            pe.wait_ge(s_rv, MEMBERS_READY)
            for t in range(NT + 1):
                o = ps[1][:, t * NE:(t + 1) * NE]
                for u in range(min(t, NT)):
                    last = nc.tensor.matmul(o, ones[:, :], member[:, u, :], start=(u == 0), stop=(t == NT and u == NT - 1))
                if t < NT:
                    last = nc.tensor.matmul(o, after[:, :], member[:, t, :], start=(t == 0), stop=True)
            last.then_inc(s_r, 1)
            for q in range(NT * TOPK):
                pe.wait_ge(s_rv, POS_READY + 4 * (q + 1))
                nc.tensor.matmul(ps[2][:, 0:3 * SLOTS], lane1h[:, q % 2, :], slot1h[:, q % 2, :, :].rearrange("p m s -> p (m s)"),
                                 start=(q == 0), stop=(q == NT * TOPK - 1)).then_inc(s_r, 1)

            def half_chunk(k, j, lhs, q, o, first, fin):
                pe.wait_ge(s_lo, SUBS + k + 1 + 16 * j)
                for kb in range(2):
                    b = 2 * q + kb
                    last = mm3(o, lhs[0][:, b, :], lhs[1][:, b, :], wh_of[k % XSUB][:, kb, :], wl_of[k % XSUB][:, kb, :],
                               first and kb == 0, fin and kb == 1)
                last.then_inc(s_used, 1)

            def do_keys(k, j, p, count):
                pe.wait_ge(s_xlo, count)
                for q in range(4):
                    half_chunk(k + q, j, (xgTh[p], xgTl[p]), q, ps[0][:, :], q == 0, q == 3)

            def do_values(k, j, p, v):
                if v == 0:
                    pe.wait_ge(s_hlo, 2 * j + p + 1)
                pe.wait_ge((s_ye0, s_ye1)[v], 2 * j + p + 1)
                for q in range(2):
                    half_chunk(k + q, j, (hTh[p], hTl[p]), q, ps[4 + 2 * p + v][:, :], q == 0, q == 1)

            def x_T(p, landed):
                pe.wait_ge(s_g[p], landed)
                for b in range(DC):
                    last = nc.tensor.transpose(ps[2 + b // 4][:, (b % 4) * P:(b % 4 + 1) * P], xg[p][:, b * P:(b + 1) * P], ident[:, :])
                last.then_inc(s_xT, 1)

            def h_T(count):
                pe.wait_ge(s_h, count)
                for b in range(EF):
                    last = nc.tensor.transpose(ps[1][:, b * P:(b + 1) * P], hsb[:, b * P:(b + 1) * P], ident[:, :])
                last.then_inc(s_hT, 1)

            def pe_slot(j, p, ahead):
                do_keys(4 + 8 * p, j, 1 - p, 2 * j + p + 2)
                if ahead:
                    x_T(p, 16 * j + 32)
                do_values(8 + 8 * p, j, p, 0)
                h_T(2 * j + p + 2)
                do_values(10 + 8 * p, j, p, 1)

            pe.wait_ge(s_tab, 1)
            last_round = pe.value_load(slots[0:1, 0:1], min_val=PAIRS_MIN - 1, max_val=PAIRS_MAX - 1)
            x_T(0, 16)
            do_keys(0, 0, 0, 1)
            x_T(1, 16)
            h_T(1)
            with pe.Fori(0, last_round) as j:
                for p in range(2):
                    pe_slot(j, p, True)
            pe_slot(last_round, 0, False)
            do_values(12, last_round, 1, 0)
            do_values(14, last_round, 1, 1)


def kernel(**inputs):
    import numpy as _np
    import concourse.bacc as _bacc
    from concourse import mybir as _mybir
    from concourse.bass_utils import run_bass_kernel_spmd as _run

    nc = _bacc.Bacc("TRN2", target_bir_lowering=False, num_devices=1)
    arrays = {}

    def given(name, a):
        a = _np.ascontiguousarray(a)
        arrays["in_" + name] = a
        return nc.dram_tensor("in_" + name, a.shape, _mybir.dt.from_np(a.dtype), kind="ExternalInput").ap()

    a = {k: _np.asarray(v) for k, v in inputs.items()}

    def edge_layout(v):
        return v.reshape(EC, P).T

    def weight_layout(w):
        return w.T.reshape(2, 4, P, 2, HALF).transpose(3, 0, 2, 1, 4).reshape(4, P, 4, HALF)

    gnn, mix, ffn = "L0_gnn_", "L0_mix_", "L0_ffn_"
    names = {"mq": mix + "wq", "mk": mix + "wk", "mv": mix + "wv", "mo": mix + "wo", "q": gnn + "wq", "k": gnn + "wk",
             "v": gnn + "wv", "q2": gnn + "wiq", "k2": gnn + "wik", "v2": gnn + "wiv", "o": gnn + "wo"}
    W = {n: given("w_" + n, weight_layout(a[names[n]])) for n, _ in PROJ}
    cols = {n: given("col_" + n, a[gnn + n].reshape(DC, P).T) for n in ("bq", "bk", "bv", "biq", "bik")}
    rows = {n: given("row_" + n, a[k].reshape(1, D)) for n, k in (("bo", gnn + "bo"), ("mbo", mix + "bo"), ("biv", gnn + "biv"))}
    selT = given("sel", a[ffn + "expert_sel"].reshape(NE, DC, P).transpose(2, 1, 0))
    keys = given("keys", a[ffn + "keys"].reshape(NE, 2, 4, P, ES).transpose(0, 1, 3, 2, 4))
    values = given("values", a[ffn + "values"].reshape(NE, EF, P, 2, HALF).transpose(0, 3, 2, 1, 4))
    f4 = _np.float32
    p = _np.arange(P)
    tok = _np.arange(NT)[None, :, None] * P + p[:, None, None] + _np.zeros((1, 1, TOPK))
    row = tok + _np.arange(TOPK)[None, None, :] * N
    own = _np.concatenate([(FAR - tok).reshape(P, -1), (FAR - row).reshape(P, -1), tok[:, :, 0]], axis=1)
    consts = {
        "ident": _np.eye(P), "after": p[None, :] > p[:, None], "ones": _np.ones((P, P)),
        "pair": (p[None, :] // HD) == (p[:, None] // HD), "iota": _np.tile(_np.arange(N), (P, 1)),
        "layer": _np.tile(4 * (_np.arange(EC) % LAYERS) + 32, (P, 1)), "own": own,
    }
    C = {n: given("c_" + n, v.astype(f4)) for n, v in consts.items() if n != "iotah"}
    C["iotah"] = given("c_iotah", consts["iota"].astype(_np.float16))
    xt_dram = nc.dram_tensor("xt_dram", (N, D), F32).ap()
    y_dram = nc.dram_tensor("y_dram", (TOPK * N, D), F32).ap()
    out = nc.dram_tensor("out_dram", (N, D), F32, kind="ExternalOutput").ap()
    gps_layer_kernel(nc, given("x", a["x"]), given("src", edge_layout(a["src"])), given("dst", edge_layout(a["dst"])),
                     given("typ", edge_layout(a["edge_type_5"])), given("etw", a[gnn + "edge_type_weights"].reshape(1, 4)),
                     W, cols, rows, selT, keys, values, C, xt_dram, y_dram, out)
    r = _run(nc, [arrays], core_ids=[0])
    return r.results[0]["out_dram"]
```

```python
from contextlib import ExitStack

import concourse.bass as bass
from concourse import mybir

F32 = mybir.dt.float32
FR = mybir.dt.float32r
BF16 = mybir.dt.bfloat16
F16 = mybir.dt.float16
I32 = mybir.dt.int32
U32 = mybir.dt.uint32
ACT = mybir.ActivationFunctionType
ALU = mybir.AluOpType
AX_X = mybir.AxisListType.X

P = 128
N = 384
NT = N // P
D = 1024
DC = D // P
H = 16
HD = D // H
E = 12288
EC = E // P
LAYERS = EC // 2
NE = 32
ES = 512
EF = ES // P
TOPK = 4
HALF = 512
SLOTS_MAX = (N * TOPK) // P + NE - 1
PAIRS_MIN, PAIRS_MAX = NE // 2, (SLOTS_MAX + 1) // 2
SLOTS = 2 * PAIRS_MAX + 1
FAR = 4096.0
NEG = -1.0e30
EPS_LN = 1e-5
EPS_MIX = 1e-6
RAW = 4
SUB = 4
RING = 5
XRAW = 8
XSUB = 8
XLEAD = 4
LEAD = 3

PROJ = [("mq", "F"), ("mk", "T"), ("mv", "T"), ("v", "F"), ("mo", "T"), ("q", "F"), ("v2", "T"),
        ("k", "F"), ("q2", "F"), ("k2", "F"), ("o", "T")]
CHUNKS = 4 * len(PROJ)
SUBS = 2 * CHUNKS
COLS = ["bq", "bk", "bv", "biq", "bik"]
CONSTS_AT = [("ident", P), ("after", P), ("ones", P), ("pair", P), ("iota", N), ("layer", EC), ("own", 2 * NT * TOPK + NT)]
N_CONST = 6
N_ROWS = 3


def plan_jobs():
    names = ["xT0", "xT1", "mq0", "dup0", "mq1", "dup1", "mk0", "dup2", "mk1", "dup3", "mv0", "dup4", "dup5",
             "mv1", "edge0", "lin", "v0", "mix0", "mix1", "mix2", "edge1", "mT0", "mT1", "v1", "mo0", "mo1",
             "q0", "q1", "v20", "v21", "k0", "k1", "q20", "q21", "k20", "k21", "att", "o0", "o1"]
    proj = [n for n, _ in PROJ]
    kind = dict(PROJ)
    jobs, bank, signalled, sub, at = {}, 0, 0, 0, 0
    for n in names:
        base = n[:-1]
        if base in proj:
            banks = 4 if kind[base] == "F" else NT
        else:
            banks = {"edge": NT, "at": 0, "li": 3, "mix": 3}.get(base, 4)
        subs = 4 if base in proj else 0
        jobs[n] = dict(set=at % 2, first=bank, signals=signalled, banks=banks, sub=sub, sub_end=sub + subs, kind=kind.get(base), base=base,
                       half=int(n[-1]) if n[-1].isdigit() else 0)
        bank += banks
        signalled += banks - 1 if subs or base == "edge" else banks
        sub += subs
        at += 1
    order = list(jobs)
    for k, n in enumerate(order):
        prev = order[k - 2] if k >= 2 else None
        jobs[n]["free"] = jobs[prev]["first"] + jobs[prev]["banks"] if prev else 0
    return jobs, order


def gps_layer_kernel(nc, x, edges, etw, W, cols, rows, selT, keys, values, C, xt_dram, y_dram, out):
    jobs, order = plan_jobs()
    assert jobs["o1"]["sub_end"] == SUBS
    ctx = ExitStack()
    with ctx:
        def sb(name, shape, dt):
            return ctx.enter_context(nc.sbuf_tensor(name, shape, dt))

        def sem(name):
            return ctx.enter_context(nc.semaphore(name))

        arena0 = (nc.sbuf_base + 31) // 32 * 32
        arena = sb("arena", [P, 3 * 6144 + 3 * 3072], F32)

        def at(name, shape, dt, off):
            return nc.alloc_sbuf_tensor_at(name, shape, dt, offset=arena0 + off)

        KB = 1024
        A0, A1, A2, F0, F1, F2 = 0, 24 * KB, 48 * KB, 72 * KB, 84 * KB, 96 * KB
        xnh, xnl = at("xnh", [P, DC, N], FR, A0), at("xnl", [P, DC, N], FR, A0 + 12 * KB)
        mah, mal = at("mah", [P, DC, N], FR, A1), at("mal", [P, DC, N], FR, A1 + 12 * KB)
        mbh, mbl = at("mbh", [P, DC, N], FR, A2), at("mbl", [P, DC, N], FR, A2 + 12 * KB)
        xn = at("xn", [P, NT, D], F32, F0)
        mq = at("mq", [P, DC, N], F32, F0)
        q2 = at("q2", [P, DC, N], F32, F0)
        mk = at("mk", [P, NT, D], F32, F1)
        kvks = at("kvks", [P, DC, P + 2], F32, F1)
        k2 = at("k2", [P, DC, N], F32, F1)
        mv = at("mv", [P, NT, D], F32, F2)
        v2 = at("v2", [P, NT, D], F32, F2)
        bo_b = at("bo_b", [P, D], F32, A2)
        mbo_b = at("mbo_b", [P, D], F32, A2 + 4 * KB)
        ohs = at("ohs", [P, 4, N], BF16, A2 + 8 * KB)
        ohd = at("ohd", [P, 4, N], BF16, A2 + 11 * KB)
        mixed = at("mixed", [P, NT, D], F32, F2)
        mtyp, mval, mtmp, mdef = (at(f"mask_tmp{k}", [P, N], F32, F1 + 6 * KB + 1536 * k) for k in range(4))
        pT = at("pT", [P, 2, NT, N], F32, A0)
        sm = at("sm", [P, RING, N], F32, A0 + 9 * KB)
        pr = at("pr", [P, RING, N], F32, A0 + 9 * KB + RING * 1536)
        raw_x = [at(f"raw_x{r}", [P, 4, HALF], F32, A1 + 8 * KB * r) for r in range(3)] + [at("raw_x3", [P, 4, HALF], F32, F2)]
        sub_x = [A0 + 8 * KB * r for r in range(3)] + [F1]
        wh_x = [at(f"wh_x{r}", [P, 2, HALF], FR, o) for r, o in enumerate(sub_x)]
        wl_x = [at(f"wl_x{r}", [P, 2, HALF], FR, o + 4 * KB) for r, o in enumerate(sub_x)]
        xgTh = [at(f"xgTh{p}", [P, DC, P], FR, A2 + 8 * KB * p) for p in range(2)]
        xgTl = [at(f"xgTl{p}", [P, DC, P], FR, A2 + 8 * KB * p + 4 * KB) for p in range(2)]
        hTh = [at(f"hTh{p}", [P, EF, P], FR, A2 + 16 * KB + 4 * KB * p) for p in range(2)]
        hTl = [at(f"hTl{p}", [P, EF, P], FR, A2 + 18 * KB + 4 * KB * p) for p in range(2)]
        xg = [at(f"xg{p}", [P, D], F32, F0 + 4 * KB * p) for p in range(2)]
        hsb = at("hsb", [P, ES], F32, F0 + 8 * KB)
        yk = [at(f"yk{t}", [P, TOPK, D], F32, A0 + 16 * KB * t) for t in range(NT)]
        xt = at("xt", [P, NT, D], F32, F0)
        xtT = at("xtT", [P, DC, N], F32, F1)
        route = A2
        gates = at("gates", [P, NT, NE], F32, route)
        oh = at("oh", [P, NT * TOPK, NE], F32, route + 1 * KB)
        member = at("member", [P, NT, NE], F32, route + 2560)
        rank = at("rank", [P, NT, NE], F32, route + 3 * KB)
        m8 = at("m8", [P, NT, 8], F32, route + 3584)
        i8 = at("i8", [P, NT, 8], U32, route + 3680)
        i8f = at("i8f", [P, NT, 8], F32, route + 3776)
        small = at("small", [P, 8, NE], F32, route + 4 * KB)
        pos = at("pos", [P, 4, NT * TOPK], F32, route + 5 * KB)
        lane1h = at("lane1h", [P, NT * TOPK, P], F32, route + 5632)
        slot1h = at("slot1h", [P, NT * TOPK, 3, SLOTS], F32, route + 11776)
        inslot = at("inslot", [P, NT * TOPK, SLOTS], F32, route + 18432)
        logit = at("logit", [NE, N], F32, route + 21 * KB)
        picked = at("picked", [P, NT * TOPK, NE], F32, route + 22 * KB + 512)
        cmp = at("cmp", [P, SLOTS, NE], F32, F1)
        tabf = at("tabf", [P, 3, SLOTS], F32, F2 + 8 * KB)
        gidx, pidx = at("gidx", [P, SLOTS], I32, F2 + 9 * KB), at("pidx", [P, SLOTS], I32, F2 + 9 * KB + 512)
        acc = sb("acc", [P, NT, D], F32)
        raw = sb("raw", [P, RAW, 4, HALF], F32)
        wh = sb("wh", [P, SUB, 2, HALF], FR)
        wl = sb("wl", [P, SUB, 2, HALF], FR)
        mask = sb("mask", [P, NT, N], F32)
        etmp = sb("etmp", [P, 2, HALF], F32)
        biv_b = sb("biv_b", [P, D], F32)
        ysb = [at("ysb0", [P, D], F32, F1 + 8 * KB), etmp[:, :, :].rearrange("p a b -> p (a b)")]
        call = sb("c_all", [P, sum(w for _, w in CONSTS_AT)], F32)
        cst, width = {}, 0
        for n, w in CONSTS_AT:
            cst[n] = call[:, width:width + w]
            width += w
        iotah = sb("iotah", [P, N], F16)
        ident, after, ones = cst["ident"], cst["after"], cst["ones"]
        col = sb("col", [P, len(COLS), DC], F32)
        sel = sb("sel", [P, DC, NE], F32)
        ei = sb("ei", [P, 3, EC], I32)
        ef = sb("ef", [P, 4, EC], F32)
        code = sb("code", [P, EC], F32)
        dup = sb("dup", [P, EC], F32)
        junk = sb("junk", [P, P], F32)
        w4 = sb("w4", [P, 5, 4], F32)
        stats = sb("stats", [P, NT, 2, 6], F32)
        mv2 = sb("mv2", [P, NT, 4], F32)
        kss = sb("kss", [P, DC], F32)
        qden = sb("qden", [P, 2, 8], F32)
        mx = sb("mx", [P, 4, H * NT], F32)
        gcol = [sb(f"gcol{p}", [P, 1], I32) for p in range(2)]
        pcol = sb("pcol", [P, 1], I32)
        slotx = sb("slotx", [P, SLOTS], I32)
        slots = sb("slots", [P, 1], I32)

        ps = [ctx.enter_context(nc.psum_tensor(f"ps{b}", [P, 512], F32)) for b in range(8)]

        s_x = [sem(f"s_x{t}") for t in range(NT)]
        s_const = sem("s_const")
        s_rows = sem("s_rows")
        s_load = [sem(f"s_load{r}") for r in range(XRAW)]
        s_hi = sem("s_hi")
        s_lo = sem("s_lo")
        s_used = sem("s_used")
        s_bank = sem("s_bank")
        s_free = sem("s_free")
        s_ahi = sem("s_ahi")
        s_dch = sem("s_dch")
        s_ach = sem("s_ach")
        s_pch = sem("s_pch")
        s_seen = sem("s_seen")
        s_bias = sem("s_bias")
        s_xn = sem("s_xn")
        s_spl = sem("s_spl")
        s_oh = sem("s_oh")
        s_ohu = sem("s_ohu")
        s_key = sem("s_key")
        s_s = sem("s_s")
        s_sm = sem("s_sm")
        s_e = sem("s_e")
        s_p = sem("s_p")
        s_t = sem("s_t")
        s_pt = sem("s_pt")
        s_pv = sem("s_pv")
        s_oh_hi = sem("s_oh_hi")
        s_o = sem("s_o")
        s_xt = sem("s_xt")
        s_xtd = sem("s_xtd")
        s_r = sem("s_r")
        s_r_t = sem("s_r_t")
        s_rv = sem("s_rv")
        s_lg = sem("s_lg")
        s_lga = sem("s_lga")
        s_mem = sem("s_mem")
        s_1h = sem("s_1h")
        s_ra = sem("s_ra")
        s_slots = sem("s_slots")
        s_tab = sem("s_tab")
        s_g = [sem("s_g0"), sem("s_g1")]
        s_xT = sem("s_xT")
        s_xhi = sem("s_xhi")
        s_xlo = sem("s_xlo")
        s_h = sem("s_h")
        s_hT = sem("s_hT")
        s_hhi = sem("s_hhi")
        s_hlo = sem("s_hlo")
        s_ye0, s_ye1 = sem("s_ye0"), sem("s_ye1")
        s_sc = sem("s_sc")
        s_scd = sem("s_scd")
        s_end = sem("s_end")
        s_yl = [sem(f"s_yl{t}") for t in range(NT)]
        s_fin = sem("s_fin")
        s_out = sem("s_out")

        s_rv_a = sem("s_rv_a")
        att_units = H * NT
        att_free = jobs["att"]["first"]
        elu_banks = []

        def attention_act(act):
            units = H * NT
            for t in range(units + 7):
                u = t - 1
                if 0 <= u < units:
                    act.wait_ge(s_sm, u + 1)
                    if u >= RING:
                        act.wait_ge(s_t, u - RING + 1)
                    nc.scalar.activation(pr[:, u % RING, :], sm[:, u % RING, :], ACT.Exp, bias=mx[:, 1, u:u + 1],
                                         accum_out=mx[:, 2, u:u + 1]).then_inc(s_e, 1)
                u = t - 4
                if 0 <= u < units:
                    h, n = u // NT, u % NT
                    act.wait_ge(s_t, u + 1)
                    if h >= 2:
                        act.wait_ge(s_pv, h - 1)
                    nc.scalar.activation(pT[:, h % 2, :, n * P:(n + 1) * P],
                                         ps[3 + u % 3][:, 0:N].rearrange("p (c n) -> p c n", n=P), ACT.Copy).then_inc(s_pt, 1)
                u = t - 6
                if u >= 0 and u % NT == NT - 1:
                    h = u // NT
                    r = slice(HD * (h % 2), HD * (h % 2) + HD)
                    act.wait_ge(s_pv, h + 1)
                    nc.scalar.activation(mbh[r, h // 2, :], ps[6 + h % 2][r, 0:N], ACT.Copy).then_inc(s_oh_hi, 1)

        def edge_mask(link, t, stage):
            code_t = mask[:, t, :]
            if stage == 0:
                link(nc.vector.tensor_single_scalar(mval[:, :].bitcast(I32), code_t.bitcast(I32), 23, ALU.logical_shift_right))
                link(nc.vector.tensor_single_scalar(mval[:, :].bitcast(I32), mval[:, :].bitcast(I32), 3, ALU.bitwise_and))
                link(nc.vector.tensor_copy(mtyp[:, :], mval[:, :].bitcast(I32)))
                link(nc.vector.tensor_scalar(mval[:, :], mtyp[:, :], 0.0, w4[:, 4, 0:1], ALU.is_equal, ALU.mult))
            elif stage == 1:
                for k in range(1, 4):
                    link(nc.vector.tensor_scalar(mtmp[:, :], mtyp[:, :], float(k), w4[:, 4, k:k + 1], ALU.is_equal, ALU.mult))
                    link(nc.vector.tensor_tensor(mval[:, :], mval[:, :], mtmp[:, :], ALU.add))
            else:
                own_t = cst["own"][:, 2 * NT * TOPK + t:2 * NT * TOPK + t + 1]
                link(nc.vector.tensor_scalar(mtmp[:, :], cst["iota"][:, :], own_t, None, ALU.is_equal))
                link(nc.vector.tensor_scalar(mtyp[:, :], mtmp[:, :], w4[:, 4, 3:4], None, ALU.mult))
                link(nc.vector.memset(mdef[:, :], NEG))
                link(nc.vector.copy_predicated(mdef[:, :], mtmp[:, :].bitcast(U32), mtyp[:, :]))
                link(nc.vector.copy_predicated(mdef[:, :], code_t.bitcast(U32), mval[:, :]))
                link(nc.vector.tensor_copy(code_t, mdef[:, :]))

        def attention_dve(dve):
            units = H * NT
            for t in range(units + 7):
                if t < units:
                    u = t
                    dve.wait_ge(s_s, u + 1)
                    if u >= RING:
                        dve.wait_ge(s_e, u - RING + 1)
                    nc.vector.tensor_tensor_reduce(out=sm[:, u % RING, :], in0=ps[u % 3][:, 0:N], in1=mask[:, u % NT, :], scale=1.0,
                                                   scalar=-3.0e38, op0=ALU.add, op1=ALU.max, accum_out=mx[:, 0, u:u + 1])\
                        .then_inc(s_free, 1)
                    dve.wait_ge(s_free, att_free + u + 1)
                    nc.vector.tensor_scalar(mx[:, 1, u:u + 1], mx[:, 0, u:u + 1], -1.0, None, ALU.mult).then_inc(s_sm, 1)
                u = t - 2
                if 0 <= u < units:
                    dve.wait_ge(s_e, u + 1)
                    nc.vector.reciprocal(mx[:, 3, u:u + 1], mx[:, 2, u:u + 1]).then_inc(s_rv_a, 1)
                    dve.wait_ge(s_rv_a, u + 1)
                    nc.vector.tensor_scalar(pr[:, u % RING, :], pr[:, u % RING, :], mx[:, 3, u:u + 1], None, ALU.mult).then_inc(s_p, 1)
                u = t - 6
                if u >= 0 and u % NT == NT - 1:
                    h = u // NT
                    r = slice(HD * (h % 2), HD * (h % 2) + HD)
                    dve.wait_ge(s_oh_hi, h + 1)
                    nc.vector.tensor_tensor(mbl[r, h // 2, :], ps[6 + h % 2][r, 0:N], mbh[r, h // 2, :].bitcast(F32), ALU.subtract)\
                        .then_inc(s_o, 1)

        def attention_pe(pe):
            units = H * NT
            pe.wait_ge(s_free, att_free)
            for t in range(units + 6):
                if t < units:
                    h, n = t // NT, t % NT
                    r = slice(HD * (h % 2), HD * (h % 2) + HD)
                    if t >= 3:
                        pe.wait_ge(s_free, att_free + t - 2)
                    nc.tensor.matmul(ps[t % 3][:, 0:N], q2[r, h // 2, n * P:(n + 1) * P], k2[r, h // 2, :],
                                     start=True, stop=True).then_inc(s_s, 1)
                u = t - 4
                if 0 <= u < units:
                    pe.wait_ge(s_p, u + 1)
                    if u >= 3:
                        pe.wait_ge(s_pt, u - 2)
                    for c in range(NT):
                        last = nc.tensor.transpose(ps[3 + u % 3][:, c * P:(c + 1) * P], pr[:, u % RING, c * P:(c + 1) * P], ident[:, :])
                    last.then_inc(s_t, 1)
                u = t - 5
                if u >= 0 and u % NT == NT - 1:
                    h = u // NT
                    pe.wait_ge(s_pt, u + 1)
                    if h >= 2:
                        pe.wait_ge(s_o, h - 1)
                    for c in range(NT):
                        last = nc.tensor.matmul(ps[6 + h % 2][:, 0:N], v2[:, c, (h // 2) * P:(h // 2 + 1) * P], pT[:, h % 2, c, :],
                                                start=(c == 0), stop=(c == NT - 1))
                    last.then_inc(s_pv, 1)

        block = ctx.enter_context(nc.Block())

        def bank_filled(eng, j, b):
            if b == j["banks"] - 1 and j["sub_end"] > j["sub"]:
                eng.wait_ge(s_used, j["sub_end"])
            elif b == j["banks"] - 1 and j["base"] == "edge":
                eng.wait_ge(s_ohu, (j["half"] + 1) * LAYERS)
            else:
                eng.wait_ge(s_bank, j["signals"] + b + 1)

        def load_done(c):
            return 16 * (c // RAW + 1)

        raw_of = [raw[:, r, :, :] for r in range(RAW)] + [t[:, :, :] for t in raw_x]
        wh_of = [wh[:, r, :, :] for r in range(SUB)] + [t[:, :, :] for t in wh_x]
        wl_of = [wl[:, r, :, :] for r in range(SUB)] + [t[:, :, :] for t in wl_x]

        def x_load_done(c, j):
            r = c % XRAW
            return 16 * ((CHUNKS // RAW if r < RAW else 0) + c // XRAW + 1) + 16 * j

        @block.sync
        def _(sp):
            for t in range(NT):
                sp.dma_start(acc[:, t, :], x[t * P:(t + 1) * P, :]).then_inc(s_x[t], 16)
            sp.wait_ge(s_const, 16 * N_CONST)
            for c in range(CHUNKS):
                if c >= RAW:
                    sp.wait_ge(s_lo, 2 * (c - RAW + 1))
                n = PROJ[c // 4][0]
                sp.dma_start(raw[:, c % RAW, :, :], W[n][c % 4]).then_inc(s_load[c % RAW], 16)
                if c == RAW - 1:
                    for to, n in ((bo_b, "bo"), (mbo_b, "mbo"), (biv_b, "biv")):
                        sp.dma_start(to[:, :], rows[n].to_broadcast([P, D])).then_inc(s_rows, 16)

            def expert_half(src_ap, e, half, c):
                sp.dma_start(raw_of[c % XRAW], src_ap[bass.ds(e, 1), half].rearrange("a p k n -> p (a k) n"))\
                    .then_inc(s_load[c % XRAW], 16)

            def expert_chunks(src_ap, e, c, j):
                for half in range(2):
                    sp.wait_ge(s_lo, SUBS + 2 * (c + half - XRAW + 1) + 16 * j)
                    expert_half(src_ap, e, half, c + half)

            for half in range(2):
                sp.wait_ge(s_lo, 2 * (CHUNKS + half - RAW + 1))
                sp.dma_start(raw_of[half], keys[0, half]).then_inc(s_load[half], 16)
            sp.wait_ge(s_slots, 1)
            last = sp.value_load(slots[0:1, 0:1], min_val=PAIRS_MIN - 1, max_val=PAIRS_MAX - 1)
            with sp.Fori(0, last) as j:
                e = [sp.value_load(slotx[0:1, bass.ds(2 * j + q, 1)], min_val=0, max_val=NE - 1) for q in range(3)]
                for p in range(2):
                    expert_chunks(keys, e[p + 1], 2 + 4 * p, j)
                    expert_chunks(values, e[p], 4 + 4 * p, j)
            e = [sp.value_load(slotx[0:1, bass.ds(2 * last + q, 1)], min_val=0, max_val=NE - 1) for q in range(2)]
            expert_chunks(keys, e[1], 2, last)
            expert_chunks(values, e[0], 4, last)
            expert_chunks(values, e[1], 6, last)
            sp.wait_ge(s_end, 1)
            for t in range(NT):
                sp.dma_start(yk[t][:, :, :], y_dram.rearrange("(k t p) d -> t p k d", k=TOPK, t=NT)[t]).then_inc(s_yl[t], 16)
            for t in range(NT):
                sp.wait_ge(s_fin, t + 1)
                sp.dma_start(out[t * P:(t + 1) * P, :], acc[:, t, :]).then_inc(s_out, 16)
            sp.wait_ge(s_out, 16 * NT)

        @block.gpsimd
        def _(pool):
            pool.wait_ge(s_rows, 16 * N_ROWS)
            pool.wait_ge(s_xn, NT)
            for t in range(NT):
                nc.gpsimd.tensor_tensor(acc[:, t, :], acc[:, t, :], bo_b[:, :], ALU.add).then_inc(s_pch, 1)
                pool.wait_ge(s_pch, t + 1)
            for t in range(NT):
                nc.gpsimd.tensor_tensor(acc[:, t, :], acc[:, t, :], mbo_b[:, :], ALU.add).then_inc(s_bias, 1)

            def pool_wait(s, value):
                pool.wait_ge(s, value)
                pool.sem_inc(s_seen, 1)

            def gather(s, p, count):
                nc.gpsimd.tensor_copy(gcol[p][:, :], gidx[:, bass.ds(s, 1)]).then_inc(s_pch, 1)
                pool_wait(s_pch, count)
                nc.gpsimd.indirect_dma_start(xg[p][:, :], None, xt_dram, bass.IndirectOffsetOnAxis(gcol[p][:, :].bitcast(U32), 0),
                                             bounds_check=N - 1, oob_is_err=False).then_inc(s_g[p], 16)

            def pool_slot(j, p, count, ahead):
                s = 2 * j + p
                if ahead:
                    pool_wait(s_xT, s + 2)
                    gather(s + 3, 1 - p, count + 1)
                nc.gpsimd.tensor_copy(pcol[:, :], pidx[:, bass.ds(s, 1)]).then_inc(s_pch, 1)
                pool_wait(s_pch, count + (2 if ahead else 1))
                pool_wait(s_ye0, s + 3)
                pool_wait(s_ye1, s + 3)
                nc.gpsimd.indirect_dma_start(y_dram, bass.IndirectOffsetOnAxis(pcol[:, :].bitcast(U32), 0), ysb[p][:, :], None,
                                             bounds_check=TOPK * N - 1, oob_is_err=False).then_inc(s_sc, 16)
                pool_wait(s_sc, 16 * s + 16)
                pool.sem_inc(s_scd, 1)

            pool.wait_ge(s_xtd, 16 * NT)
            pool.wait_ge(s_t, H * NT + 8)
            for p in range(2):
                nc.gpsimd.memset(xg[p][:, :], 0.0).then_inc(s_pch, 1)
            pool.wait_ge(s_tab, 1)
            last = pool.value_load(slots[0:1, 0:1], min_val=PAIRS_MIN - 1, max_val=PAIRS_MAX - 1)
            pool.sem_inc(s_scd, 2)
            gather(0, 0, NT + 3)
            gather(1, 1, NT + 4)
            pool.wait_ge(s_xT, 1)
            gather(2, 0, NT + 5)
            with pool.Fori(0, last) as j:
                for p in range(2):
                    pool_slot(j, p, 4 * j + 2 * p + NT + 5, True)
            for p in range(2):
                pool_slot(last, p, 4 * last + p + NT + 5, False)
            pool_wait(s_g[0], 16 * last + 32)
            pool.sem_inc(s_end, 1)

        @block.scalar
        def _(act):
            act.dma_start(ei[:, :, :], edges).then_inc(s_const, 16)
            act.dma_start(call[:, :], C["all"]).then_inc(s_const, 16)
            act.dma_start(w4[:, 0, :], etw.to_broadcast([P, 4])).then_inc(s_const, 16)
            act.dma_start(col[:, :, :], cols).then_inc(s_const, 16)
            act.dma_start(iotah[:, :], C["iotah"]).then_inc(s_const, 16)
            act.dma_start(sel[:, :, :], selT).then_inc(s_const, 16)

            done = [0]
            chain = [0]

            def link(ins):
                chain[0] += 1
                ins.then_inc(s_ach, 1)
                act.wait_ge(s_ach, chain[0])

            def split(upto):
                for s in range(done[0], min(upto, SUBS)):
                    c = s // 2
                    act.wait_ge(s_load[c % RAW], load_done(c))
                    if s >= SUB:
                        act.wait_ge(s_used, s - SUB + 1)
                    nc.scalar.activation(wh[:, s % SUB], raw[:, c % RAW, 2 * (s % 2):2 * (s % 2) + 2, :], ACT.Copy)\
                        .then_inc(s_hi, 1)
                done[0] = max(done[0], min(upto, SUBS))

            def bank_of(j, b):
                return ps[4 * j["set"] + b]

            colno = {n: k for k, n in enumerate(COLS)}
            bias_of = {"v": "bv", "q": "bq", "k": "bk"}
            into = {"v": mah, "q": mbh, "k": mah}
            ahi = [0]
            act.wait_ge(s_spl, 1)
            link(nc.scalar.activation(w4[:, 2, :], w4[:, 1, :], ACT.Exp, scale=-1.0))
            nc.scalar.activation(w4[:, 3, :], w4[:, 2, :], ACT.Ln, bias=1.0).then_inc(s_ra, 1)
            split(2)
            for name in order:
                j = jobs[name]
                if name == "att":
                    attention_act(act)
                    continue
                split(j["sub_end"] + LEAD)
                oh_ = int(name[-1]) if name[-1].isdigit() else 0
                for b in range(j["banks"]):
                    pb = bank_of(j, b)
                    if b == 1:
                        split(j["sub_end"] + LEAD + 1)
                    base = j["base"]
                    if base in ("xT", "mT"):
                        bank_filled(act, j, b)
                        if name == "mT0" and b == 0:
                            act.wait_ge(s_bias, NT)
                        nc.scalar.activation((xnh if base == "xT" else mbh)[:, 4 * oh_ + b, :], pb[:, 0:N], ACT.Copy).then_inc(s_ahi, 1)
                    elif base in into:
                        bank_filled(act, j, b)
                        o = 4 * oh_ + b
                        nc.scalar.activation(into[base][:, o, :], pb[:, 0:N], ACT.Identity,
                                             bias=col[:, colno[bias_of[base]], o:o + 1]).then_inc(s_ahi, 1)
                    elif base in ("mq", "mk"):
                        width = N if base == "mq" else HALF
                        bank_filled(act, j, b)
                        if len(elu_banks) >= 2:
                            act.wait_ge(s_free, elu_banks[-2] + 1)
                        t = etmp[:, len(elu_banks) % 2, 0:width]
                        link(nc.scalar.activation(t, pb[:, 0:width], ACT.Relu, scale=-1.0))
                        nc.scalar.activation(t, t, ACT.Exp, scale=-1.0).then_inc(s_ahi, 1)
                        elu_banks.append(j["first"] + b)
            for t in range(NT):
                act.wait_ge(s_xt, t + 1)
                act.dma_start(xt_dram[t * P:(t + 1) * P, :], xt[:, t, :]).then_inc(s_xtd, 16)
            def split_expert(k, j):
                c = k // 2
                act.wait_ge(s_load[c % XRAW], x_load_done(c, j))
                if k >= XSUB or k < SUB:
                    act.wait_ge(s_used, SUBS + k + 1 - (XSUB if k >= XSUB else SUB) + 16 * j)
                nc.scalar.activation(wh_of[k % XSUB], raw_of[c % XRAW][:, 2 * (k % 2):2 * (k % 2) + 2, :], ACT.Copy)\
                    .then_inc(s_hi, 1)

            for k in range(XLEAD):
                split_expert(k, 0)
            for b in range(1, DC, 2):
                act.wait_ge(s_t, H * NT + b + 1)
                nc.scalar.activation(xtT[:, b, :], ps[b][:, 0:N], ACT.Copy).then_inc(s_lga, 1)
            act.wait_ge(s_r_t, 1)
            nc.scalar.activation(gates[:, :, :], ps[2][:, 0:NT * NE].rearrange("p (t e) -> p t e", e=NE), ACT.Exp,
                                 scale=-1.0).then_inc(s_ra, 1)

            def x_hi(count, p):
                act.wait_ge(s_xT, count)
                for b in range(2):
                    ins = nc.scalar.activation(xgTh[p][:, 4 * b:4 * b + 4, :], ps[2 + b][:, :].rearrange("p (c t) -> p c t", t=P), ACT.Copy)
                ins.then_inc(s_xhi, 1)

            def h_out(used, s):
                act.wait_ge(s_used, used)
                nc.scalar.activation(hsb[:, :], ps[0][:, :], ACT.Relu, scale=tabf[:, 2, bass.ds(s, 1)]).then_inc(s_h, 1)

            def h_hi(count, p):
                act.wait_ge(s_hT, count)
                nc.scalar.activation(hTh[p][:, :, :], ps[1][:, :].rearrange("p (c t) -> p c t", t=P), ACT.Copy).then_inc(s_hhi, 1)

            def y_second(j, p, used):
                act.wait_ge(s_used, used)
                act.wait_ge(s_scd, 2 * j + p + 1)
                nc.scalar.activation(ysb[p][:, HALF:D], ps[5 + 2 * p][:, :], ACT.Copy).then_inc(s_ye1, 1)

            def act_slot(j, p, ahead):
                k = 8 * p
                used = SUBS + 8 * p + 16 * j
                for q in range(8, 10):
                    split_expert(k + q, j)
                h_out(used + 8, 2 * j + p + 1)
                split_expert(k + 10, j)
                if ahead:
                    x_hi(2 * j + p + 3, p)
                split_expert(k + 11, j)
                h_hi(2 * j + p + 2, 1 - p)
                for q in range(12, 14):
                    split_expert(k + q, j)
                y_second(j, p, used + 12)
                for q in range(14, 16):
                    split_expert(k + q, j)

            act.wait_ge(s_tab, 1)
            last = act.value_load(slots[0:1, 0:1], min_val=PAIRS_MIN - 1, max_val=PAIRS_MAX - 1)
            act.sem_inc(s_ye1, 2)
            x_hi(1, 0)
            for k in range(4, 6):
                split_expert(k, 0)
            x_hi(2, 1)
            for k in range(6, 4 + XLEAD):
                split_expert(k, 0)
            h_out(SUBS + 4, 0)
            h_hi(1, 0)
            with act.Fori(0, last) as j:
                for p in range(2):
                    act_slot(j, p, True)
            act_slot(last, 0, False)
            y_second(last, 1, SUBS + 16 + 16 * last)

        @block.vector
        def _(dve):
            chain = [0]

            def link(ins):
                chain[0] += 1
                ins.then_inc(s_dch, 1)
                dve.wait_ge(s_dch, chain[0])

            done = [0]

            def split(upto):
                for s in range(done[0], min(upto, SUBS)):
                    dve.wait_ge(s_hi, s + 1)
                    nc.vector.tensor_tensor(wl[:, s % SUB], raw[:, (s // 2) % RAW, 2 * (s % 2):2 * (s % 2) + 2, :],
                                            wh[:, s % SUB].bitcast(F32), ALU.subtract).then_inc(s_lo, 1)
                done[0] = max(done[0], min(upto, SUBS))

            def row_stats(t, k):
                link(nc.vector.bn_stats(stats[:, t, k, :], acc[:, t, k * 512:(k + 1) * 512]))

            def norms(out_tile, done_sem):
                for t in range(NT):
                    link(nc.vector.bn_aggr(mv2[:, t, 0:2], stats[:, t, :, :].rearrange("p a b -> p (a b)")))
                v, y, z = mv2[:, :, 1], mv2[:, :, 2], mv2[:, :, 3]
                link(nc.vector.tensor_scalar(v, v, EPS_LN, None, ALU.add))
                link(nc.vector.tensor_single_scalar(z.bitcast(I32), v.bitcast(I32), 1, ALU.logical_shift_right))
                link(nc.vector.tensor_scalar(y.bitcast(I32), z.bitcast(I32), -1.0, float(0x5F3759DF), ALU.mult, ALU.add))
                for _ in range(3):
                    link(nc.vector.tensor_tensor(z, y, y, ALU.mult))
                    link(nc.vector.tensor_tensor(z, z, v, ALU.mult))
                    link(nc.vector.tensor_scalar(z, z, -0.5, 1.5, ALU.mult, ALU.add))
                    link(nc.vector.tensor_tensor(y, y, z, ALU.mult))
                for t in range(NT):
                    nc.vector.tensor_scalar(out_tile[:, t, :], acc[:, t, :], mv2[:, t, 0:1], mv2[:, t, 2:3],
                                            ALU.subtract, ALU.mult).then_inc(done_sem, 1)

            dve.wait_ge(s_const, 16 * N_CONST)
            link(nc.vector.tensor_copy(ef[:, 0:3, :], ei[:, :, :]))
            nc.vector.scalar_tensor_tensor(ef[:, 3, :], ef[:, 0, :], float(N), ef[:, 1, :], ALU.mult, ALU.add).then_inc(s_key, 1)
            dve.wait_ge(s_key, 1)
            link(nc.vector.tensor_scalar(ei[:, 2, :], ef[:, 2, :], 3.0, None, ALU.add))
            link(nc.vector.tensor_single_scalar(ei[:, 2, :], ei[:, 2, :], 3, ALU.bitwise_and))
            link(nc.vector.tensor_tensor(ei[:, 2, :], ei[:, 2, :], cst["layer"][:, :], ALU.add))
            link(nc.vector.tensor_single_scalar(code[:, :].bitcast(I32), ei[:, 2, :], 23, ALU.logical_shift_left))
            nc.vector.scalar_tensor_tensor(w4[:, 1, :], w4[:, 0, :], -1.0, w4[:, 0, :], ALU.mult, ALU.max).then_inc(s_spl, 1)
            for t in range(NT):
                dve.wait_ge(s_x[t], 16)
                for k in range(2):
                    row_stats(t, k)
            norms(xn, s_xn)
            dve.wait_ge(s_ra, 1)
            link(nc.vector.scalar_tensor_tensor(w4[:, 4, :], w4[:, 0, :], 0.0, w4[:, 3, :], ALU.max, ALU.add))

            colno = {n: k for k, n in enumerate(COLS)}
            bias_of = {"v": "bv", "q": "bq", "k": "bk", "q2": "biq", "k2": "bik"}
            parts = {"v": (mah, mal), "q": (mbh, mbl), "k": (mah, mal)}
            ahi = 0
            elus = 0
            decode_at = ["v1", "mo0", "mo1", "q0", "q1", "v20", "v21", "k0", "k1"]
            for name in order:
                j = jobs[name]
                if name == "att":
                    attention_dve(dve)
                    continue
                if not name.startswith("xT"):
                    split(j["sub_end"] + LEAD)
                half = int(name[-1]) if name[-1].isdigit() else 0
                base = j["base"]
                if name.startswith("edge"):
                    for c in range(LAYERS):
                        g = half * LAYERS + c
                        if g >= 4:
                            dve.wait_ge(s_ohu, g - 3)
                        nc.vector.tensor_scalar(ohs[:, g % 4, :], iotah[:, :], ef[:, 0, g:g + 1], None, ALU.is_equal)
                        nc.vector.tensor_scalar(ohd[:, g % 4, :], iotah[:, :], ef[:, 1, g:g + 1], ef[:, 2, g:g + 1],
                                                ALU.is_equal, ALU.mult).then_inc(s_oh, 1)
                for b in range(j["banks"]):
                    if b == 1:
                        split(half if name.startswith("xT") else j["sub_end"] + LEAD + 1)
                    pb = ps[4 * j["set"] + b]
                    if name != "lin":
                        bank_filled(dve, j, b)
                    if name.startswith("dup"):
                        for q in range(4):
                            g = 16 * half + 4 * b + q
                            last = nc.vector.scalar_tensor_tensor(junk[:, :], pb[:, q * P:(q + 1) * P], ef[:, 3, g:g + 1],
                                                                  after[:, :], ALU.is_equal, ALU.mult, accum_out=dup[:, g:g + 1])
                            if q < 3:
                                link(last)
                        last.then_inc(s_free, 1)
                        dve.wait_ge(s_free, j["first"] + b + 1)
                        if name == "dup5" and b == 3:
                            link(nc.vector.scalar_tensor_tensor(ef[:, 2, :], dup[:, :], 0.5, code[:, :], ALU.is_lt, ALU.mult))
                    elif base in ("xT", "mT"):
                        hi, lo = (xnh, xnl) if base == "xT" else (mbh, mbl)
                        ahi += 1
                        dve.wait_ge(s_ahi, ahi)
                        nc.vector.tensor_tensor(lo[:, 4 * half + b, :], pb[:, 0:N], hi[:, 4 * half + b, :].bitcast(F32),
                                                ALU.subtract).then_inc(s_free, 1)
                    elif base in parts:
                        hi, lo = parts[base]
                        o = 4 * half + b
                        ahi += 1
                        dve.wait_ge(s_ahi, ahi)
                        nc.vector.scalar_tensor_tensor(lo[:, o, :], pb[:, 0:N], col[:, colno[bias_of[base]], o:o + 1],
                                                       hi[:, o, :].bitcast(F32), ALU.add, ALU.subtract).then_inc(s_free, 1)
                    elif base in ("mq", "mk"):
                        width = N if base == "mq" else HALF
                        to = mq[:, 4 * half + b, :] if base == "mq" else mk[:, b, half * HALF:(half + 1) * HALF]
                        t = etmp[:, elus % 2, 0:width]
                        ahi += 1
                        dve.wait_ge(s_ahi, ahi)
                        elus += 1
                        nc.vector.scalar_tensor_tensor(to, pb[:, 0:width], 0.0, t, ALU.max, ALU.add).then_inc(s_free, 1)
                    elif base in ("q2", "k2"):
                        o = 4 * half + b
                        to = q2 if base == "q2" else k2
                        nc.vector.tensor_scalar(to[:, o, :], pb[:, 0:N], col[:, colno[bias_of[base]], o:o + 1],
                                                float(HD) ** -0.5 if base == "q2" else 1.0, ALU.add, ALU.mult).then_inc(s_free, 1)
                    elif base == "mv":
                        nc.vector.tensor_copy(mv[:, b, half * HALF:(half + 1) * HALF], pb[:, :]).then_inc(s_free, 1)
                    elif base == "v2":
                        if half == 0 and b == 0:
                            dve.wait_ge(s_rows, 16 * N_ROWS)
                        cs = slice(half * HALF, (half + 1) * HALF)
                        nc.vector.tensor_tensor(v2[:, b, cs], pb[:, :], biv_b[:, cs], ALU.add).then_inc(s_free, 1)
                    elif base in ("mo", "o"):
                        cs = slice(half * HALF, (half + 1) * HALF)
                        nc.vector.tensor_tensor(acc[:, b, cs], pb[:, :], acc[:, b, cs], ALU.add).then_inc(s_free, 1)
                    elif name.startswith("edge"):
                        if half == 0:
                            nc.vector.tensor_copy(mask[:, b, :], pb[:, 0:N]).then_inc(s_free, 1)
                        else:
                            nc.vector.tensor_copy(mtmp[:, :], pb[:, 0:N]).then_inc(s_free, 1)
                            dve.wait_ge(s_free, j["first"] + b + 1)
                            link(nc.vector.copy_predicated(mask[:, b, :], mtmp[:, :].bitcast(U32), mtmp[:, :]))
                    elif name == "lin":
                        if b == 0:
                            bank_filled(dve, j, 2)
                            link(nc.vector.tensor_copy(kss[:, :], ps[4 * j["set"] + 2][:, 0:DC]))
                        if b < 2:
                            last = nc.vector.tensor_tensor(kvks[:, 4 * b:4 * b + 4, 0:P], pb[:, :].rearrange("p (c e) -> p c e", e=P),
                                                           cst["pair"][:, None, :].to_broadcast([P, 4, P]), ALU.mult)
                        else:
                            for k in range(2):
                                last = nc.vector.tensor_scalar(kvks[:, :, P + k], kss[:, :], cst["pair"][:, k * HD:k * HD + 1], None, ALU.mult)
                        last.then_inc(s_free, 1)
                    elif base == "mix":
                        n = min(3, DC - 3 * b)
                        view = pb[:, 0:n * (P + 2)].rearrange("p (c e) -> p c e", e=P + 2)
                        den, inv = qden[:, 0, 0:2 * n], qden[:, 1, 0:2 * n]
                        link(nc.vector.tensor_scalar(den.rearrange("p (c k) -> p c k", k=2), view[:, :, P:P + 2], EPS_MIX, None, ALU.add))
                        link(nc.vector.reciprocal(inv, den))
                        last = nc.vector.tensor_tensor(mixed[:, half, 3 * b * P:(3 * b + n) * P].rearrange("p (c k e) -> p c k e", k=2, e=HD),
                                                       view[:, :, 0:P].rearrange("p c (k e) -> p c k e", k=2),
                                                       inv.rearrange("p (c k) -> p c k", k=2)[:, :, :, None].to_broadcast([P, n, 2, HD]), ALU.mult)
                        last.then_inc(s_free, 1)
                        dve.wait_ge(s_free, j["first"] + b + 1)
                if name in decode_at:
                    edge_mask(link, decode_at.index(name) // 3, decode_at.index(name) % 3)
                if name == "o0":
                    for t in range(NT):
                        dve.wait_ge(s_free, j["first"] + t + 1 + att_units)
                        row_stats(t, 0)
                if name == "o1":
                    dve.wait_ge(s_free, j["first"] + j["banks"] + att_units)
            def split_expert(k, j):
                dve.wait_ge(s_hi, SUBS + k + 1 + 16 * j)
                nc.vector.tensor_tensor(wl_of[k % XSUB], raw_of[(k // 2) % XRAW][:, 2 * (k % 2):2 * (k % 2) + 2, :],
                                        wh_of[k % XSUB].bitcast(F32), ALU.subtract).then_inc(s_lo, 1)

            for t in range(NT):
                row_stats(t, 1)
            norms(xt, s_xt)
            for b in range(0, DC, 2):
                dve.wait_ge(s_t, H * NT + b + 1)
                nc.vector.tensor_copy(xtT[:, b, :], ps[b][:, 0:N]).then_inc(s_lg, 1)
            for k in range(XLEAD):
                split_expert(k, 0)
            rv = [0]

            def step(ins):
                rv[0] += 1
                ins.then_inc(s_rv, 1)

            def steps_done():
                dve.wait_ge(s_rv, rv[0])

            def rlink(ins):
                step(ins)
                steps_done()

            iota, own = cst["iota"], cst["own"]
            pairs = NT * TOPK
            dve.wait_ge(s_r, 1)
            nc.vector.tensor_copy(logit[:, :], ps[0][0:NE, 0:N]).then_inc(s_lg, 1)
            rlink(nc.vector.memset(small[:, 1, :], 1.0))
            rlink(nc.vector.memset(small[:, 2, :], 0.0))
            dve.wait_ge(s_ra, 2)
            rlink(nc.vector.tensor_scalar(gates[:, :, :], gates[:, :, :], 1.0, None, ALU.add))
            rlink(nc.vector.reciprocal(gates[:, :, :], gates[:, :, :]))
            for t in range(NT):
                step(nc.vector.max(m8[:, t, :], gates[:, t, :]))
            steps_done()
            for t in range(NT):
                step(nc.vector.max_index(i8[:, t, :], m8[:, t, :], gates[:, t, :]))
            steps_done()
            rlink(nc.vector.tensor_copy(i8f[:, :, :], i8[:, :, :]))
            for t in range(NT):
                step(nc.vector.tensor_tensor(oh[:, t * TOPK:(t + 1) * TOPK, :], iota[:, None, 0:NE].to_broadcast([P, TOPK, NE]),
                                             i8f[:, t, 0:TOPK, None].to_broadcast([P, TOPK, NE]), ALU.is_equal))
            steps_done()
            nc.vector.tensor_reduce(member[:, :, :], oh[:, :, :].rearrange("p (t k) e -> p t e k", k=TOPK), AX_X, ALU.add)\
                .then_inc(s_mem, 1)
            dve.wait_ge(s_r, 2)
            ranks = ps[1][:, 0:NT * NE].rearrange("p (t e) -> p t e", e=NE)
            tot = ps[1][:, NT * NE:(NT + 1) * NE]
            for t in range(1, NT):
                rlink(nc.vector.scalar_tensor_tensor(small[:, 1, :], tot, t * P + 0.5, small[:, 1, :], ALU.is_gt, ALU.add))
            rlink(nc.vector.tensor_tensor_scan(small[:, 3, :], small[:, 1, :], small[:, 2, :], 0.0, ALU.add, ALU.add))
            rlink(nc.vector.tensor_tensor(small[:, 4, :], small[:, 3, :], small[:, 1, :], ALU.subtract))
            rlink(nc.vector.tensor_scalar(small[:, 5, :], small[:, 4, :], float(P), None, ALU.mult))
            rlink(nc.vector.tensor_tensor(rank[:, :, :], ranks, small[:, 5, None, :].to_broadcast([P, NT, NE]), ALU.add))
            for t in range(NT):
                step(nc.vector.tensor_tensor(picked[:, t * TOPK:(t + 1) * TOPK, :], oh[:, t * TOPK:(t + 1) * TOPK, :],
                                             rank[:, t, None, :].to_broadcast([P, TOPK, NE]), ALU.mult))
            steps_done()
            rlink(nc.vector.tensor_reduce(pos[:, 0, :], picked[:, :, :], AX_X, ALU.add))
            posi = pos[:, 3, :].bitcast(I32)
            rlink(nc.vector.tensor_copy(posi, pos[:, 0, :]))
            step(nc.vector.tensor_single_scalar(pos[:, 1, :].bitcast(I32), posi, P - 1, ALU.bitwise_and))
            step(nc.vector.tensor_single_scalar(pos[:, 2, :].bitcast(I32), posi, 7, ALU.logical_shift_right))
            steps_done()
            step(nc.vector.tensor_copy(pos[:, 0, :], pos[:, 1, :].bitcast(I32)))
            step(nc.vector.tensor_copy(pos[:, 3, :], pos[:, 2, :].bitcast(I32)))
            steps_done()
            for t in range(NT):
                ks = slice(t * TOPK, (t + 1) * TOPK)
                step(nc.vector.tensor_tensor(inslot[:, ks, :], iota[:, None, 0:SLOTS].to_broadcast([P, TOPK, SLOTS]),
                                             pos[:, 3, ks, None].to_broadcast([P, TOPK, SLOTS]), ALU.is_equal))
                step(nc.vector.tensor_tensor(lane1h[:, ks, :], iota[:, None, 0:P].to_broadcast([P, TOPK, P]),
                                             pos[:, 0, ks, None].to_broadcast([P, TOPK, P]), ALU.is_equal))
                steps_done()
                for m in range(2):
                    step(nc.vector.tensor_tensor(slot1h[:, ks, m, :], inslot[:, ks, :],
                                                 own[:, m * pairs + t * TOPK:m * pairs + (t + 1) * TOPK, None].to_broadcast([P, TOPK, SLOTS]),
                                                 ALU.mult))
                step(nc.vector.tensor_tensor(slot1h[:, ks, 2, :], inslot[:, ks, :],
                                             m8[:, t, 0:TOPK, None].to_broadcast([P, TOPK, SLOTS]), ALU.mult))
                steps_done()
                dve.sem_inc(s_1h, 1)
            rlink(nc.vector.tensor_tensor(cmp[:, :, :], small[:, 3, None, :].to_broadcast([P, SLOTS, NE]),
                                          iota[:, 0:SLOTS, None].to_broadcast([P, SLOTS, NE]), ALU.is_le))
            rlink(nc.vector.tensor_reduce(tabf[:, 0, :], cmp[:, :, :], AX_X, ALU.add))
            rlink(nc.vector.tensor_scalar(slotx[:, :], tabf[:, 0, :], float(NE - 1), None, ALU.min))
            rlink(nc.vector.tensor_scalar(slots[:, :], small[:, 3, NE - 1:NE], -1.0, None, ALU.add))
            nc.vector.tensor_single_scalar(slots[:, :], slots[:, :], 1, ALU.logical_shift_right).then_inc(s_slots, 1)
            dve.wait_ge(s_slots, 1)
            dve.wait_ge(s_r, 3)
            tab = ps[2][:, 0:3 * SLOTS].rearrange("p (m s) -> p m s", s=SLOTS)
            step(nc.vector.tensor_scalar(gidx[:, :], tab[:, 0, :], -1.0, FAR, ALU.mult, ALU.add))
            step(nc.vector.tensor_scalar(pidx[:, :], tab[:, 1, :], -1.0, FAR, ALU.mult, ALU.add))
            step(nc.vector.tensor_copy(tabf[:, 2, :], tab[:, 2, :]))
            steps_done()
            dve.sem_inc(s_tab, 1)

            def x_lo(count, p):
                dve.wait_ge(s_xhi, count)
                for b in range(2):
                    ins = nc.vector.tensor_tensor(xgTl[p][:, 4 * b:4 * b + 4, :], ps[2 + b][:, :].rearrange("p (c t) -> p c t", t=P),
                                                  xgTh[p][:, 4 * b:4 * b + 4, :].bitcast(F32), ALU.subtract)
                ins.then_inc(s_xlo, 1)

            def h_lo(count, p):
                dve.wait_ge(s_hhi, count)
                nc.vector.tensor_tensor(hTl[p][:, :, :], ps[1][:, :].rearrange("p (c t) -> p c t", t=P),
                                        hTh[p][:, :, :].bitcast(F32), ALU.subtract).then_inc(s_hlo, 1)

            def y_first(j, p, used):
                dve.wait_ge(s_used, used)
                dve.wait_ge(s_scd, 2 * j + p + 1)
                nc.vector.tensor_copy(ysb[p][:, 0:HALF], ps[4 + 2 * p][:, :]).then_inc(s_ye0, 1)

            def dve_slot(j, p, ahead):
                k = 8 * p
                for q in range(8, 11):
                    split_expert(k + q, j)
                if ahead:
                    x_lo(2 * j + p + 3, p)
                split_expert(k + 11, j)
                y_first(j, p, SUBS + 10 + 8 * p + 16 * j)
                h_lo(2 * j + p + 2, 1 - p)
                for q in range(12, 16):
                    split_expert(k + q, j)

            dve.wait_ge(s_tab, 1)
            last = dve.value_load(slots[0:1, 0:1], min_val=PAIRS_MIN - 1, max_val=PAIRS_MAX - 1)
            dve.sem_inc(s_ye0, 2)
            x_lo(1, 0)
            for k in range(4, 6):
                split_expert(k, 0)
            x_lo(2, 1)
            for k in range(6, 4 + XLEAD):
                split_expert(k, 0)
            h_lo(1, 0)
            with dve.Fori(0, last) as j:
                for p in range(2):
                    dve_slot(j, p, True)
            dve_slot(last, 0, False)
            y_first(last, 1, SUBS + 14 + 16 * last)
            for t in range(NT):
                dve.wait_ge(s_yl[t], 16)
                for k in range(TOPK):
                    ins = nc.vector.tensor_tensor(acc[:, t, :], acc[:, t, :], yk[t][:, k, :], ALU.add)
                    if k < TOPK - 1:
                        link(ins)
                ins.then_inc(s_fin, 1)

        @block.tensor
        def _(pe):
            def mm3(o, ah, al, bh_, bl_, start, stop):
                nc.tensor.matmul(o, ah, bh_, start=start, stop=False)
                nc.tensor.matmul(o, ah, bl_, start=False, stop=False)
                return nc.tensor.matmul(o, al, bh_, start=False, stop=stop)

            src_of = {"mq": (xnh, xnl), "mk": (xnh, xnl), "mv": (xnh, xnl), "v": (xnh, xnl), "q": (xnh, xnl), "k": (xnh, xnl),
                      "mo": (mbh, mbl), "v2": (mah, mal), "q2": (mbh, mbl), "k2": (mah, mal), "o": (mbh, mbl)}
            needs = {"mo": "mT1", "v2": "v1", "q2": "q1", "k2": "k1", "mq": "xT1"}
            end = {n: jobs[n]["first"] + jobs[n]["banks"] for n in order}
            pe.wait_ge(s_const, 16 * N_CONST)
            for name in order:
                j = jobs[name]
                if name == "att":
                    attention_pe(pe)
                    continue
                half = int(name[-1]) if name[-1].isdigit() else 0
                base = j["base"]
                shift = att_units if name in ("o0", "o1") else 0
                if j["free"]:
                    pe.wait_ge(s_free, j["free"] + shift)
                if base in needs and half == 0:
                    pe.wait_ge(s_free, end[needs[base]])
                if name == "o0":
                    pe.wait_ge(s_o, H)
                bk = [ps[4 * j["set"] + b] for b in range(4)]
                if name.startswith("dup"):
                    pe.wait_ge(s_key, 1)
                    for b in range(4):
                        for q in range(4):
                            g = 16 * half + 4 * b + q
                            last = nc.tensor.transpose(bk[b][:, q * P:(q + 1) * P], ef[:, 3, g:g + 1].to_broadcast([P, P]), ident[:, :])
                        last.then_inc(s_bank, 1)
                elif base in ("xT", "mT"):
                    if base == "mT":
                        pe.wait_ge(s_free, end["mix2"])
                    for t in range(NT):
                        if base == "xT":
                            pe.wait_ge(s_xn, t + 1)
                        for b in range(4):
                            o = 4 * half + b
                            last = nc.tensor.transpose(bk[b][:, t * P:(t + 1) * P], (xn if base == "xT" else mixed)[:, t, o * P:(o + 1) * P],
                                                       ident[:, :])
                            if t == NT - 1:
                                last.then_inc(s_bank, 1)
                elif name.startswith("edge"):
                    for c in range(LAYERS):
                        g = half * LAYERS + c
                        pe.wait_ge(s_oh, g + 1)
                        for t in range(NT):
                            last = nc.tensor.matmul(bk[t][:, 0:N], ohs[:, g % 4, t * P:(t + 1) * P], ohd[:, g % 4, :],
                                                    start=(c == 0), stop=(c == LAYERS - 1))
                            if c == LAYERS - 1 and t < NT - 1:
                                last.then_inc(s_bank, 1)
                        last.then_inc(s_ohu, 1)
                elif name == "lin":
                    pe.wait_ge(s_free, end["mv1"])
                    for c in range(DC):
                        cs = slice(c * P, (c + 1) * P)
                        for t in range(NT):
                            last = nc.tensor.matmul(bk[c // 4][:, (c % 4) * P:(c % 4 + 1) * P], mk[:, t, cs], mv[:, t, cs],
                                                    start=(t == 0), stop=(t == NT - 1))
                        if c % 4 == 3:
                            last.then_inc(s_bank, 1)
                    for c in range(DC):
                        cs = slice(c * P, (c + 1) * P)
                        for t in range(NT):
                            last = nc.tensor.matmul(bk[2][:, c:c + 1], mk[:, t, cs], ones[:, 0:1], start=(t == 0), stop=(t == NT - 1))
                    last.then_inc(s_bank, 1)
                elif base == "mix":
                    if half == 0:
                        pe.wait_ge(s_free, end["lin"])
                    for c in range(DC):
                        last = nc.tensor.matmul(bk[c // 3][:, (c % 3) * (P + 2):(c % 3 + 1) * (P + 2)], mq[:, c, half * P:(half + 1) * P],
                                                kvks[:, c, :], start=True, stop=True)
                        if c % 3 == 2 or c == DC - 1:
                            last.then_inc(s_bank, 1)
                else:
                    xh, xl = src_of[base]
                    for q in range(4):
                        s = j["sub"] + q
                        pe.wait_ge(s_lo, s + 1)
                        for kb in range(2):
                            i = 2 * q + kb
                            first, fin = q == 0 and kb == 0, q == 3 and kb == 1
                            for b in range(j["banks"]):
                                if j["kind"] == "F":
                                    bs = slice(b * P, (b + 1) * P)
                                    last = mm3(bk[b][:, 0:N], wh[:, s % SUB, kb, bs], wl[:, s % SUB, kb, bs],
                                               xh[:, i, :], xl[:, i, :], first, fin)
                                else:
                                    bs = slice(b * P, (b + 1) * P)
                                    last = mm3(bk[b][:, :], xh[:, i, bs], xl[:, i, bs],
                                               wh[:, s % SUB, kb, :], wl[:, s % SUB, kb, :], first, fin)
                                if fin and b < j["banks"] - 1:
                                    last.then_inc(s_bank, 1)
                        last.then_inc(s_used, 1)

            for t in range(NT):
                pe.wait_ge(s_xt, t + 1)
                for b in range(DC):
                    if t == 0 and b == 4:
                        pe.wait_ge(s_free, end["o1"] + att_units)
                    last = nc.tensor.transpose(ps[b][:, t * P:(t + 1) * P], xt[:, t, b * P:(b + 1) * P], ident[:, :])
                    if t == NT - 1:
                        last.then_inc(s_t, 1)
            for b in range(DC):
                pe.wait_ge((s_lg, s_lga)[b % 2], b // 2 + 1)
                last = nc.tensor.matmul(ps[0][0:NE, 0:N], sel[:, b, :], xtT[:, b, :], start=(b == 0), stop=(b == DC - 1))
            last.then_inc(s_r, 1)
            pe.wait_ge(s_lg, DC // 2 + 1)
            for t in range(NT):
                last = nc.tensor.transpose(ps[2][:, t * NE:(t + 1) * NE], logit[:, t * P:(t + 1) * P], ident[0:NE, 0:NE])
            last.then_inc(s_r_t, 1)
            pe.wait_ge(s_mem, 1)
            for t in range(NT + 1):
                o = ps[1][:, t * NE:(t + 1) * NE]
                for u in range(min(t, NT)):
                    last = nc.tensor.matmul(o, ones[:, :], member[:, u, :], start=(u == 0), stop=(t == NT and u == NT - 1))
                if t < NT:
                    last = nc.tensor.matmul(o, after[:, :], member[:, t, :], start=(t == 0), stop=True)
            last.then_inc(s_r, 1)
            for q in range(NT * TOPK):
                if q % TOPK == 0:
                    pe.wait_ge(s_1h, q // TOPK + 1)
                last = nc.tensor.matmul(ps[2][:, 0:3 * SLOTS], lane1h[:, q, :], slot1h[:, q, :, :].rearrange("p m s -> p (m s)"),
                                        start=(q == 0), stop=(q == NT * TOPK - 1))
            last.then_inc(s_r, 1)

            def half_chunk(k, j, lhs, q, o, first, fin):
                pe.wait_ge(s_lo, SUBS + k + 1 + 16 * j)
                for kb in range(2):
                    b = 2 * q + kb
                    last = mm3(o, lhs[0][:, b, :], lhs[1][:, b, :], wh_of[k % XSUB][:, kb, :], wl_of[k % XSUB][:, kb, :],
                               first and kb == 0, fin and kb == 1)
                last.then_inc(s_used, 1)

            def do_keys(k, j, p, count):
                pe.wait_ge(s_xlo, count)
                for q in range(4):
                    half_chunk(k + q, j, (xgTh[p], xgTl[p]), q, ps[0][:, :], q == 0, q == 3)

            def do_values(k, j, p, v):
                if v == 0:
                    pe.wait_ge(s_hlo, 2 * j + p + 1)
                pe.wait_ge((s_ye0, s_ye1)[v], 2 * j + p + 1)
                for q in range(2):
                    half_chunk(k + q, j, (hTh[p], hTl[p]), q, ps[4 + 2 * p + v][:, :], q == 0, q == 1)

            def x_T(p, landed):
                pe.wait_ge(s_g[p], landed)
                for b in range(DC):
                    last = nc.tensor.transpose(ps[2 + b // 4][:, (b % 4) * P:(b % 4 + 1) * P], xg[p][:, b * P:(b + 1) * P], ident[:, :])
                last.then_inc(s_xT, 1)

            def h_T(count):
                pe.wait_ge(s_h, count)
                for b in range(EF):
                    last = nc.tensor.transpose(ps[1][:, b * P:(b + 1) * P], hsb[:, b * P:(b + 1) * P], ident[:, :])
                last.then_inc(s_hT, 1)

            def pe_slot(j, p, ahead):
                do_keys(4 + 8 * p, j, 1 - p, 2 * j + p + 2)
                if ahead:
                    x_T(p, 16 * j + 32)
                do_values(8 + 8 * p, j, p, 0)
                h_T(2 * j + p + 2)
                do_values(10 + 8 * p, j, p, 1)

            pe.wait_ge(s_tab, 1)
            last_round = pe.value_load(slots[0:1, 0:1], min_val=PAIRS_MIN - 1, max_val=PAIRS_MAX - 1)
            x_T(0, 16)
            do_keys(0, 0, 0, 1)
            x_T(1, 16)
            h_T(1)
            with pe.Fori(0, last_round) as j:
                for p in range(2):
                    pe_slot(j, p, True)
            pe_slot(last_round, 0, False)
            do_values(12, last_round, 1, 0)
            do_values(14, last_round, 1, 1)


def kernel(**inputs):
    import numpy as _np
    import concourse.bacc as _bacc
    from concourse import mybir as _mybir
    from concourse.bass_utils import run_bass_kernel_spmd as _run

    nc = _bacc.Bacc("TRN2", target_bir_lowering=False, num_devices=1)
    arrays = {}

    def given(name, a):
        a = _np.ascontiguousarray(a)
        arrays["in_" + name] = a
        return nc.dram_tensor("in_" + name, a.shape, _mybir.dt.from_np(a.dtype), kind="ExternalInput").ap()

    a = {k: _np.asarray(v) for k, v in inputs.items()}

    def edge_layout(v):
        return v.reshape(EC, P).T

    def weight_layout(w):
        return w.T.reshape(2, 4, P, 2, HALF).transpose(3, 0, 2, 1, 4).reshape(4, P, 4, HALF)

    gnn, mix, ffn = "L0_gnn_", "L0_mix_", "L0_ffn_"
    names = {"mq": mix + "wq", "mk": mix + "wk", "mv": mix + "wv", "mo": mix + "wo", "q": gnn + "wq", "k": gnn + "wk",
             "v": gnn + "wv", "q2": gnn + "wiq", "k2": gnn + "wik", "v2": gnn + "wiv", "o": gnn + "wo"}
    W = {n: given("w_" + n, weight_layout(a[names[n]])) for n, _ in PROJ}
    cols = given("cols", _np.stack([a[gnn + n].reshape(DC, P).T for n in COLS], axis=1))
    rows = {n: given("row_" + n, a[k].reshape(1, D)) for n, k in (("bo", gnn + "bo"), ("mbo", mix + "bo"), ("biv", gnn + "biv"))}
    selT = given("sel", a[ffn + "expert_sel"].reshape(NE, DC, P).transpose(2, 1, 0))
    keys = given("keys", a[ffn + "keys"].reshape(NE, 2, 4, P, ES).transpose(0, 1, 3, 2, 4))
    values = given("values", a[ffn + "values"].reshape(NE, EF, P, 2, HALF).transpose(0, 3, 2, 1, 4))
    f4 = _np.float32
    p = _np.arange(P)
    tok = _np.arange(NT)[None, :, None] * P + p[:, None, None] + _np.zeros((1, 1, TOPK))
    row = tok + _np.arange(TOPK)[None, None, :] * N
    own = _np.concatenate([(FAR - tok).reshape(P, -1), (FAR - row).reshape(P, -1), tok[:, :, 0]], axis=1)
    consts = {
        "ident": _np.eye(P), "after": p[None, :] > p[:, None], "ones": _np.ones((P, P)),
        "pair": (p[None, :] // HD) == (p[:, None] // HD), "iota": _np.tile(_np.arange(N), (P, 1)),
        "layer": _np.tile(4 * (_np.arange(EC) % LAYERS) + 32, (P, 1)), "own": own,
    }
    C = {"all": given("c_all", _np.concatenate([_np.asarray(consts[n]).astype(f4) for n, _ in CONSTS_AT], axis=1))}
    C["iotah"] = given("c_iotah", consts["iota"].astype(_np.float16))
    xt_dram = nc.dram_tensor("xt_dram", (N, D), F32).ap()
    y_dram = nc.dram_tensor("y_dram", (TOPK * N, D), F32).ap()
    out = nc.dram_tensor("out_dram", (N, D), F32, kind="ExternalOutput").ap()
    gps_layer_kernel(nc, given("x", a["x"]), given("edges", _np.stack([edge_layout(a[n]) for n in ("src", "dst", "edge_type_5")], axis=1)),
                     given("etw", a[gnn + "edge_type_weights"].reshape(1, 4)),
                     W, cols, rows, selT, keys, values, C, xt_dram, y_dram, out)
    r = _run(nc, [arrays], core_ids=[0])
    return r.results[0]["out_dram"]
```

```python
from contextlib import ExitStack

import concourse.bass as bass
from concourse import mybir

F32 = mybir.dt.float32
FR = mybir.dt.float32r
BF16 = mybir.dt.bfloat16
F16 = mybir.dt.float16
I32 = mybir.dt.int32
U32 = mybir.dt.uint32
ACT = mybir.ActivationFunctionType
ALU = mybir.AluOpType
AX_X = mybir.AxisListType.X

P = 128
N = 384
NT = N // P
D = 1024
DC = D // P
H = 16
HD = D // H
E = 12288
EC = E // P
LAYERS = EC // 2
NE = 32
ES = 512
EF = ES // P
TOPK = 4
HALF = 512
SLOTS_MAX = (N * TOPK) // P + NE - 1
PAIRS_MIN, PAIRS_MAX = NE // 2, (SLOTS_MAX + 1) // 2
SLOTS = 2 * PAIRS_MAX + 1
FAR = 4096.0
NEG = -1.0e30
EPS_LN = 1e-5
EPS_MIX = 1e-6
RAW = 4
SUB = 4
RING = 5
XRAW = 8
XSUB = 8
XLEAD = 4
LEAD = 3

PROJ = [("mq", "F"), ("mk", "T"), ("mv", "T"), ("v", "F"), ("mo", "T"), ("q", "F"), ("v2", "T"),
        ("k", "F"), ("q2", "F"), ("k2", "F"), ("o", "T")]
CHUNKS = 4 * len(PROJ)
SUBS = 2 * CHUNKS
COLS = ["bq", "bk", "bv", "biq", "bik"]
CONSTS_AT = [("ident", P), ("after", P), ("ones", P), ("pair", P), ("iota", N), ("layer", EC), ("own", 2 * NT), ("first", NE)]
N_CONST = 6
N_ROWS = 3


def plan_jobs():
    names = ["xT0", "xT1", "mq0", "dup0", "mq1", "dup1", "mk0", "dup2", "mk1", "dup3", "mv0", "dup4",
             "mv1", "dup5", "lin", "edge0", "v0", "mix0", "edge1", "mix1", "mix2", "v1", "mT0", "mT1", "mo0", "mo1",
             "q0", "q1", "v20", "v21", "k0", "k1", "q20", "q21", "k20", "k21", "att", "o0", "o1"]
    proj = [n for n, _ in PROJ]
    kind = dict(PROJ)
    jobs, bank, signalled, sub, at = {}, 0, 0, 0, 0
    for n in names:
        base = n[:-1]
        if base in proj:
            banks = 4 if kind[base] == "F" else NT
        else:
            banks = {"edge": NT, "at": 0, "li": 3, "mix": 3}.get(base, 4)
        subs = 4 if base in proj else 0
        jobs[n] = dict(set=at % 2, first=bank, signals=signalled, banks=banks, sub=sub, sub_end=sub + subs, kind=kind.get(base), base=base,
                       half=int(n[-1]) if n[-1].isdigit() else 0)
        bank += banks
        signalled += banks - 1 if subs or base == "edge" else banks
        sub += subs
        at += 1
    order = list(jobs)
    for k, n in enumerate(order):
        prev = order[k - 2] if k >= 2 else None
        jobs[n]["free"] = jobs[prev]["first"] + jobs[prev]["banks"] if prev else 0
        jobs[n]["bank_free"] = [jobs[prev]["first"] + min(b + 1, jobs[prev]["banks"]) if prev else 0 for b in range(4)]
    return jobs, order


def gps_layer_kernel(nc, x, edges, etw, W, cols, rows, selT, keys, values, C, xt_dram, out):
    jobs, order = plan_jobs()
    assert jobs["o1"]["sub_end"] == SUBS
    ctx = ExitStack()
    with ctx:
        def sb(name, shape, dt):
            return ctx.enter_context(nc.sbuf_tensor(name, shape, dt))

        def sem(name):
            return ctx.enter_context(nc.semaphore(name))

        arena0 = (nc.sbuf_base + 31) // 32 * 32
        arena = sb("arena", [P, 3 * 6144 + 3 * 3072 + 32 + NT * N + D], F32)

        def at(name, shape, dt, off):
            return nc.alloc_sbuf_tensor_at(name, shape, dt, offset=arena0 + off)

        KB = 1024
        A0, A1, A2, F0, F1, F2 = 0, 24 * KB, 48 * KB, 72 * KB, 84 * KB, 96 * KB
        MASK = 108 * KB + 128
        BIV = MASK + NT * N * 4
        xnh, xnl = at("xnh", [P, DC, N], FR, A0), at("xnl", [P, DC, N], FR, A0 + 12 * KB)
        mah, mal = at("mah", [P, DC, N], FR, A1), at("mal", [P, DC, N], FR, A1 + 12 * KB)
        mbh, mbl = at("mbh", [P, DC, N], FR, A2), at("mbl", [P, DC, N], FR, A2 + 12 * KB)
        xn = at("xn", [P, NT, D], F32, F0)
        mq = at("mq", [P, DC, N], F32, F0)
        q2 = at("q2", [P, DC, N], F32, F0)
        mk = at("mk", [P, NT, D], F32, F1)
        kvks = at("kvks", [P, DC, P + 2], F32, F1)
        k2 = at("k2", [P, DC, N], F32, F1)
        mv = at("mv", [P, NT, DC, P + 1], F32, F2)
        v2 = at("v2", [P, NT, D], F32, F2)
        bo_b = at("bo_b", [P, D], F32, A2)
        mbo_b = at("mbo_b", [P, D], F32, A2 + 4 * KB)
        ohs = at("ohs", [P, 4, N], BF16, A2 + 8 * KB)
        ohd = at("ohd", [P, 4, N], BF16, A2 + 11 * KB)
        mixed = at("mixed", [P, NT, D], F32, F2)
        mtyp, mval, mtmp, mdef = (at(f"mask_tmp{k}", [P, N], F32, F1 + 6 * KB + 1536 * k) for k in range(4))
        pT = at("pT", [P, 2, NT, N], F32, A0)
        sm = at("sm", [P, RING, N], F32, A0 + 9 * KB)
        pr = at("pr", [P, RING, N], F32, A0 + 9 * KB + RING * 1536)
        raw_x = [at(f"raw_x{r}", [P, 4, HALF], F32, A1 + 8 * KB * r) for r in range(3)] + [at("raw_x3", [P, 4, HALF], F32, F2)]
        wh_x = [at(f"wh_x{r}", [P, 2, HALF], FR, A0 + 8 * KB * r)[:, :, :] for r in range(3)]
        wl_x = [at(f"wl_x{r}", [P, 2, HALF], FR, A0 + 8 * KB * r + 4 * KB)[:, :, :] for r in range(3)]
        xgTh = [at(f"xgTh{p}", [P, DC, P], FR, A2 + 8 * KB * p) for p in range(2)]
        xgTl = [at(f"xgTl{p}", [P, DC, P], FR, A2 + 8 * KB * p + 4 * KB) for p in range(2)]
        hTh = [at(f"hTh{p}", [P, EF, P], FR, A2 + 16 * KB + 4 * KB * p) for p in range(2)]
        hTl = [at(f"hTl{p}", [P, EF, P], FR, A2 + 18 * KB + 4 * KB * p) for p in range(2)]
        xg = [at(f"xg{p}", [P, D], F32, F0 + 4 * KB * p) for p in range(2)]
        hsb = at("hsb", [P, ES], F32, F0 + 8 * KB)
        xt = at("xt", [P, NT, D], F32, F0)
        xtT = at("xtT", [P, DC, N], F32, F1)
        route = A2
        gates = at("gates", [P, NT, NE], F32, route)
        oh = at("oh", [P, NT * TOPK, NE], F32, route + 1 * KB)
        member = at("member", [P, NT, NE], F32, route + 2560)
        rank = at("rank", [P, NT, NE], F32, route + 3 * KB)
        further = at("further", [P, NT, NE], F32, route + 5248)
        m8 = at("m8", [P, NT, 8], F32, route + 3584)
        i8 = at("i8", [P, NT, 8], U32, route + 3680)
        i8f = at("i8f", [P, NT, 8], F32, route + 3776)
        small = at("small", [P, 8, NE], F32, route + 4 * KB)
        pos = at("pos", [P, 4, NT * TOPK], F32, route + 5 * KB)
        lane1h = at("lane1h", [P, NT * TOPK, P], F32, route + 5632)
        slot1h = at("slot1h", [P, NT * TOPK, 2, SLOTS], F32, route + 11776)
        inslot = at("inslot", [P, NT * TOPK, SLOTS], F32, route + 18432)
        logit = at("logit", [NE, N], F32, route + 21 * KB)
        picked = at("picked", [P, NT * TOPK, NE], F32, route + 22 * KB + 512)
        cmp = at("cmp", [P, SLOTS - NE, NE], F32, F1)
        tabf = at("tabf", [P, 2, SLOTS], F32, F2 + 8 * KB)
        gidx = at("gidx", [P, SLOTS], I32, F2 + 9 * KB)
        slotx = at("slotx", [P, SLOTS], I32, F2 + 9 * KB + 512)
        acc = sb("acc", [P, NT, D], F32)
        raw = sb("raw", [P, RAW, 4, HALF], F32)
        wh = sb("wh", [P, SUB, 2, HALF], FR)
        wl = sb("wl", [P, SUB, 2, HALF], FR)
        mask = at("mask", [P, NT, N], F32, MASK)
        etmp = sb("etmp", [P, 2, HALF], F32)
        biv_b = at("biv_b", [P, D], F32, BIV)
        wh_x.append(at("wh_x3", [P, 2, HALF], FR, MASK)[:, :, :])
        wl_x.append(at("wl_x3", [P, 2, HALF], FR, BIV)[:, :, :])
        ysb = [at("ysb0", [P, D], F32, F1 + 8 * KB), etmp[:, :, :].rearrange("p a b -> p (a b)")]
        call = sb("c_all", [P, sum(w for _, w in CONSTS_AT)], F32)
        cst, width = {}, 0
        for n, w in CONSTS_AT:
            cst[n] = call[:, width:width + w]
            width += w
        iotah = sb("iotah", [P, N], F16)
        ident, after, ones = cst["ident"], cst["after"], cst["ones"]
        col = sb("col", [P, len(COLS), DC], F32)
        sel = sb("sel", [P, DC, NE], F32)
        ei = sb("ei", [P, 3, EC], I32)
        ef = sb("ef", [P, 4, EC], F32)
        code = sb("code", [P, EC], F32)
        dup = sb("dup", [P, EC], F32)
        junk = sb("junk", [P, P], F32)
        w4 = sb("w4", [P, 5, 4], F32)
        stats = sb("stats", [P, NT, 2, 6], F32)
        mv2 = sb("mv2", [P, NT, 4], F32)
        qden = sb("qden", [P, 2, 8], F32)
        mx = sb("mx", [P, 4, H * NT], F32)
        gcol = [sb(f"gcol{p}", [P, 1], I32) for p in range(2)]
        pcol = sb("pcol", [P, 1], I32)
        slots = sb("slots", [P, 1], I32)

        ps = [ctx.enter_context(nc.psum_tensor(f"ps{b}", [P, 512], F32)) for b in range(8)]

        s_x = [sem(f"s_x{t}") for t in range(NT)]
        s_const = sem("s_const")
        s_rows = sem("s_rows")
        s_load = [sem(f"s_load{r}") for r in range(XRAW)]
        s_hi = sem("s_hi")
        s_lo = sem("s_lo")
        s_used = sem("s_used")
        s_bank = sem("s_bank")
        s_free = sem("s_free")
        s_ahi = sem("s_ahi")
        s_dch = sem("s_dch")
        s_ach = sem("s_ach")
        s_pch = sem("s_pch")
        s_seen = sem("s_seen")
        s_bias = sem("s_bias")
        s_xn = sem("s_xn")
        s_spl = sem("s_spl")
        s_oh = sem("s_oh")
        s_ohu = sem("s_ohu")
        s_key = sem("s_key")
        s_s = sem("s_s")
        s_sm = sem("s_sm")
        s_e = sem("s_e")
        s_p = sem("s_p")
        s_t = sem("s_t")
        s_pt = sem("s_pt")
        s_pv = sem("s_pv")
        s_oh_hi = sem("s_oh_hi")
        s_o = sem("s_o")
        s_xt = sem("s_xt")
        s_xtd = sem("s_xtd")
        s_r = sem("s_r")
        s_r_t = sem("s_r_t")
        s_rv = sem("s_rv")
        s_lg = sem("s_lg")
        s_lga = sem("s_lga")
        s_mem = sem("s_mem")
        s_1h = sem("s_1h")
        s_ra = sem("s_ra")
        s_slots = sem("s_slots")
        s_tab = sem("s_tab")
        s_g = [sem("s_g0"), sem("s_g1")]
        s_xT = sem("s_xT")
        s_xhi = sem("s_xhi")
        s_xlo = sem("s_xlo")
        s_h = sem("s_h")
        s_hT = sem("s_hT")
        s_hhi = sem("s_hhi")
        s_hlo = sem("s_hlo")
        s_ye0, s_ye1 = sem("s_ye0"), sem("s_ye1")
        s_sc = sem("s_sc")
        s_scd = sem("s_scd")
        s_out = sem("s_out")

        s_rv_a = sem("s_rv_a")
        att_units = H * NT
        att_free = jobs["att"]["first"]
        elu_banks = []

        def attention_act(act):
            units = H * NT
            for t in range(units + 7):
                u = t - 1
                if 0 <= u < units:
                    act.wait_ge(s_sm, u + 1)
                    if u >= RING:
                        act.wait_ge(s_t, u - RING + 1)
                    nc.scalar.activation(pr[:, u % RING, :], sm[:, u % RING, :], ACT.Exp, bias=mx[:, 1, u:u + 1],
                                         accum_out=mx[:, 2, u:u + 1]).then_inc(s_e, 1)
                u = t - 4
                if 0 <= u < units:
                    h, n = u // NT, u % NT
                    act.wait_ge(s_t, u + 1)
                    if h >= 2:
                        act.wait_ge(s_pv, h - 1)
                    nc.scalar.activation(pT[:, h % 2, :, n * P:(n + 1) * P],
                                         ps[3 + u % 3][:, 0:N].rearrange("p (c n) -> p c n", n=P), ACT.Copy).then_inc(s_pt, 1)
                u = t - 6
                if u >= 0 and u % NT == NT - 1:
                    h = u // NT
                    r = slice(HD * (h % 2), HD * (h % 2) + HD)
                    act.wait_ge(s_pv, h + 1)
                    nc.scalar.activation(mbh[r, h // 2, :], ps[6 + h % 2][r, 0:N], ACT.Copy).then_inc(s_oh_hi, 1)

        def edge_mask(link, t, stage):
            code_t = mask[:, t, :]
            if stage == 0:
                link(nc.vector.tensor_single_scalar(mval[:, :].bitcast(I32), code_t.bitcast(I32), 23, ALU.logical_shift_right))
                link(nc.vector.tensor_single_scalar(mval[:, :].bitcast(I32), mval[:, :].bitcast(I32), 3, ALU.bitwise_and))
                link(nc.vector.tensor_copy(mtyp[:, :], mval[:, :].bitcast(I32)))
                link(nc.vector.tensor_scalar(mval[:, :], mtyp[:, :], 0.0, w4[:, 4, 0:1], ALU.is_equal, ALU.mult))
            elif stage == 1:
                for k in range(1, 4):
                    link(nc.vector.tensor_scalar(mtmp[:, :], mtyp[:, :], float(k), w4[:, 4, k:k + 1], ALU.is_equal, ALU.mult))
                    link(nc.vector.tensor_tensor(mval[:, :], mval[:, :], mtmp[:, :], ALU.add))
            else:
                own_t = cst["own"][:, t:t + 1]
                link(nc.vector.tensor_scalar(mtmp[:, :], cst["iota"][:, :], own_t, None, ALU.is_equal))
                link(nc.vector.tensor_scalar(mtyp[:, :], mtmp[:, :], w4[:, 4, 3:4], None, ALU.mult))
                link(nc.vector.memset(mdef[:, :], NEG))
                link(nc.vector.copy_predicated(mdef[:, :], mtmp[:, :].bitcast(U32), mtyp[:, :]))
                link(nc.vector.copy_predicated(mdef[:, :], code_t.bitcast(U32), mval[:, :]))
                link(nc.vector.tensor_copy(code_t, mdef[:, :]))

        def attention_dve(dve):
            units = H * NT
            for t in range(units + 7):
                if t < units:
                    u = t
                    dve.wait_ge(s_s, u + 1)
                    if u >= RING:
                        dve.wait_ge(s_e, u - RING + 1)
                    nc.vector.tensor_tensor_reduce(out=sm[:, u % RING, :], in0=ps[u % 3][:, 0:N], in1=mask[:, u % NT, :], scale=1.0,
                                                   scalar=-3.0e38, op0=ALU.add, op1=ALU.max, accum_out=mx[:, 0, u:u + 1])\
                        .then_inc(s_free, 1)
                    dve.wait_ge(s_free, att_free + u + 1)
                    nc.vector.tensor_scalar(mx[:, 1, u:u + 1], mx[:, 0, u:u + 1], -1.0, None, ALU.mult).then_inc(s_sm, 1)
                u = t - 2
                if 0 <= u < units:
                    dve.wait_ge(s_e, u + 1)
                    nc.vector.reciprocal(mx[:, 3, u:u + 1], mx[:, 2, u:u + 1]).then_inc(s_rv_a, 1)
                    dve.wait_ge(s_rv_a, u + 1)
                    nc.vector.tensor_scalar(pr[:, u % RING, :], pr[:, u % RING, :], mx[:, 3, u:u + 1], None, ALU.mult).then_inc(s_p, 1)
                u = t - 6
                if u >= 0 and u % NT == NT - 1:
                    h = u // NT
                    r = slice(HD * (h % 2), HD * (h % 2) + HD)
                    dve.wait_ge(s_oh_hi, h + 1)
                    nc.vector.tensor_tensor(mbl[r, h // 2, :], ps[6 + h % 2][r, 0:N], mbh[r, h // 2, :].bitcast(F32), ALU.subtract)\
                        .then_inc(s_o, 1)

        def attention_pe(pe):
            units = H * NT
            pe.wait_ge(s_free, att_free)
            for t in range(units + 6):
                if t < units:
                    h, n = t // NT, t % NT
                    r = slice(HD * (h % 2), HD * (h % 2) + HD)
                    if t >= 3:
                        pe.wait_ge(s_free, att_free + t - 2)
                    nc.tensor.matmul(ps[t % 3][:, 0:N], q2[r, h // 2, n * P:(n + 1) * P], k2[r, h // 2, :],
                                     start=True, stop=True).then_inc(s_s, 1)
                u = t - 4
                if 0 <= u < units:
                    pe.wait_ge(s_p, u + 1)
                    if u >= 3:
                        pe.wait_ge(s_pt, u - 2)
                    for c in range(NT):
                        last = nc.tensor.transpose(ps[3 + u % 3][:, c * P:(c + 1) * P], pr[:, u % RING, c * P:(c + 1) * P], ident[:, :])
                    last.then_inc(s_t, 1)
                u = t - 5
                if u >= 0 and u % NT == NT - 1:
                    h = u // NT
                    pe.wait_ge(s_pt, u + 1)
                    if h >= 2:
                        pe.wait_ge(s_o, h - 1)
                    for c in range(NT):
                        last = nc.tensor.matmul(ps[6 + h % 2][:, 0:N], v2[:, c, (h // 2) * P:(h // 2 + 1) * P], pT[:, h % 2, c, :],
                                                start=(c == 0), stop=(c == NT - 1))
                    last.then_inc(s_pv, 1)

        block = ctx.enter_context(nc.Block())

        def bank_filled(eng, j, b):
            if b == j["banks"] - 1 and j["sub_end"] > j["sub"]:
                eng.wait_ge(s_used, j["sub_end"])
            elif b == j["banks"] - 1 and j["base"] == "edge":
                eng.wait_ge(s_ohu, (j["half"] + 1) * LAYERS)
            else:
                eng.wait_ge(s_bank, j["signals"] + b + 1)

        def split_early(name):
            k = order.index(name)
            return k + 1 == len(order) or jobs[order[k + 1]]["kind"] is not None

        def load_done(c):
            return 16 * (c // RAW + 1)

        raw_of = [raw[:, r, :, :] for r in range(RAW)] + [t[:, :, :] for t in raw_x]
        wh_of = wh_x + [wh[:, r, :, :] for r in range(SUB)]
        wl_of = wl_x + [wl[:, r, :, :] for r in range(SUB)]

        def xt_bank(b):
            return (b + NT) % 8

        def x_load_done(c, j):
            r = c % XRAW
            return 16 * ((CHUNKS // RAW if r < RAW else 0) + c // XRAW + 1) + 16 * j

        @block.sync
        def _(sp):
            for t in range(NT):
                sp.dma_start(acc[:, t, :], x[t * P:(t + 1) * P, :]).then_inc(s_x[t], 16)
            sp.wait_ge(s_const, 16 * N_CONST)
            for c in range(CHUNKS):
                if c >= RAW:
                    sp.wait_ge(s_lo, 2 * (c - RAW + 1))
                n = PROJ[c // 4][0]
                sp.dma_start(raw[:, c % RAW, :, :], W[n][c % 4]).then_inc(s_load[c % RAW], 16)
                if c == RAW - 1:
                    for to, n in ((bo_b, "bo"), (mbo_b, "mbo"), (biv_b, "biv")):
                        sp.dma_start(to[:, :], rows[n].to_broadcast([P, D])).then_inc(s_rows, 16)

            def expert_half(src_ap, e, half, c):
                sp.dma_start(raw_of[c % XRAW], src_ap[bass.ds(e, 1), half].rearrange("a p k n -> p (a k) n"))\
                    .then_inc(s_load[c % XRAW], 16)

            def expert_chunks(src_ap, e, c, j):
                for half in range(2):
                    sp.wait_ge(s_lo, SUBS + 2 * (c + half - XRAW + 1) + 16 * j)
                    expert_half(src_ap, e, half, c + half)

            ahead = [src_ap[e, half] for src_ap, e in ((keys, 0), (keys, 1), (values, 0), (keys, 2), (values, 1), (keys, 3))
                     for half in range(2)]
            for c, chunk in enumerate(ahead):
                if c < RAW:
                    sp.wait_ge(s_lo, 2 * (CHUNKS + c - RAW + 1))
                elif c == RAW:
                    sp.wait_ge(s_pv, H)
                elif c >= XRAW:
                    sp.wait_ge(s_lo, SUBS + 2 * (c - XRAW + 1))
                sp.dma_start(raw_of[c % XRAW], chunk).then_inc(s_load[c % XRAW], 16)
            sp.wait_ge(s_slots, 1)
            last = sp.value_load(slots[0:1, 0:1], min_val=PAIRS_MIN - 1, max_val=PAIRS_MAX - 1)
            c = len(ahead)
            with sp.Fori(0, last - 1) as j:
                e = [sp.value_load(slotx[0:1, bass.ds(2 * j + q, 1)], min_val=0, max_val=NE - 1) for q in range(2, 6)]
                expert_chunks(values, e[0], c, j)
                expert_chunks(keys, e[2], c + 2, j)
                expert_chunks(values, e[1], c + 4, j)
                expert_chunks(keys, e[3], c + 6, j)
            e = [sp.value_load(slotx[0:1, bass.ds(2 * last + q, 1)], min_val=0, max_val=NE - 1) for q in range(2)]
            expert_chunks(values, e[0], c, last - 1)
            expert_chunks(values, e[1], c + 2, last - 1)

        @block.gpsimd
        def _(pool):
            pool.wait_ge(s_rows, 16 * N_ROWS)
            pool.wait_ge(s_xn, NT)
            for t in range(NT):
                nc.gpsimd.tensor_tensor(acc[:, t, :], acc[:, t, :], bo_b[:, :], ALU.add).then_inc(s_pch, 1)
                pool.wait_ge(s_pch, t + 1)
            for t in range(NT):
                nc.gpsimd.tensor_tensor(acc[:, t, :], acc[:, t, :], mbo_b[:, :], ALU.add).then_inc(s_bias, 1)

            def pool_wait(s, value):
                pool.wait_ge(s, value)
                pool.sem_inc(s_seen, 1)

            def gather(s, p, count):
                nc.gpsimd.tensor_copy(gcol[p][:, :], gidx[:, bass.ds(s, 1)]).then_inc(s_pch, 1)
                pool_wait(s_pch, count)
                nc.gpsimd.indirect_dma_start(xg[p][:, :], None, xt_dram, bass.IndirectOffsetOnAxis(gcol[p][:, :].bitcast(U32), 0),
                                             bounds_check=N - 1, oob_is_err=False).then_inc(s_g[p], 16)

            def pool_slot(j, p, count, ahead):
                s = 2 * j + p
                if ahead:
                    pool_wait(s_xT, s + 2)
                    gather(s + 3, 1 - p, count + 1)
                nc.gpsimd.tensor_copy(pcol[:, :], gidx[:, bass.ds(s, 1)]).then_inc(s_pch, 1)
                pool_wait(s_pch, count + (2 if ahead else 1))
                pool_wait(s_ye0, s + 3)
                pool_wait(s_ye1, s + 3)
                nc.gpsimd.indirect_dma_start(out, bass.IndirectOffsetOnAxis(pcol[:, :].bitcast(U32), 0), ysb[p][:, :], None,
                                             bounds_check=N - 1, oob_is_err=False, compute_op=ALU.add).then_inc(s_sc, 16)
                pool_wait(s_sc, 16 * s + 16)
                pool.sem_inc(s_scd, 1)

            pool.wait_ge(s_xtd, 16 * NT)
            pool.wait_ge(s_t, H * NT + 8)
            for p in range(2):
                nc.gpsimd.memset(xg[p][:, :], 0.0).then_inc(s_pch, 1)
            pool.wait_ge(s_tab, 1)
            last = pool.value_load(slots[0:1, 0:1], min_val=PAIRS_MIN - 1, max_val=PAIRS_MAX - 1)
            pool.sem_inc(s_scd, 2)
            pool.wait_ge(s_out, 16 * NT)
            gather(0, 0, NT + 3)
            gather(1, 1, NT + 4)
            pool.wait_ge(s_xT, 1)
            gather(2, 0, NT + 5)
            with pool.Fori(0, last) as j:
                for p in range(2):
                    pool_slot(j, p, 4 * j + 2 * p + NT + 5, True)
            for p in range(2):
                pool_slot(last, p, 4 * last + p + NT + 5, False)
            pool_wait(s_g[0], 16 * last + 32)

        @block.scalar
        def _(act):
            act.dma_start(ei[:, :, :], edges).then_inc(s_const, 16)
            act.dma_start(w4[:, 0, :], etw.to_broadcast([P, 4])).then_inc(s_const, 16)
            act.dma_start(col[:, :, :], cols).then_inc(s_const, 16)
            act.dma_start(iotah[:, :], C["iotah"]).then_inc(s_const, 16)
            act.dma_start(sel[:, :, :], selT).then_inc(s_const, 16)
            act.dma_start(call[:, :], C["all"]).then_inc(s_const, 16)

            done = [0]
            chain = [0]

            def link(ins):
                chain[0] += 1
                ins.then_inc(s_ach, 1)
                act.wait_ge(s_ach, chain[0])

            def split(upto):
                for s in range(done[0], min(upto, SUBS)):
                    c = s // 2
                    act.wait_ge(s_load[c % RAW], load_done(c))
                    if s >= SUB:
                        act.wait_ge(s_used, s - SUB + 1)
                    nc.scalar.activation(wh[:, s % SUB], raw[:, c % RAW, 2 * (s % 2):2 * (s % 2) + 2, :], ACT.Copy)\
                        .then_inc(s_hi, 1)
                done[0] = max(done[0], min(upto, SUBS))

            def split_expert(k, j):
                c = k // 2
                act.wait_ge(s_load[c % XRAW], x_load_done(c, j))
                if k >= SUB:
                    act.wait_ge(s_used, SUBS + k + 1 - XSUB + 16 * j)
                nc.scalar.activation(wh_of[k % XSUB], raw_of[c % XRAW][:, 2 * (k % 2):2 * (k % 2) + 2, :], ACT.Copy)\
                    .then_inc(s_hi, 1)

            def bank_of(j, b):
                return ps[4 * j["set"] + b]

            colno = {n: k for k, n in enumerate(COLS)}
            bias_of = {"v": "bv", "q": "bq", "k": "bk"}
            into = {"v": mah, "q": mbh, "k": mah}
            ahi = [0]
            split(2)
            for name in order:
                j = jobs[name]
                if name == "att":
                    attention_act(act)
                    continue
                if name == "dup0":
                    act.wait_ge(s_spl, 1)
                    link(nc.scalar.activation(w4[:, 2, :], w4[:, 1, :], ACT.Exp, scale=-1.0))
                    nc.scalar.activation(w4[:, 3, :], w4[:, 2, :], ACT.Ln, bias=1.0).then_inc(s_ra, 1)
                if not name.startswith("xT"):
                    split(j["sub_end"] + LEAD)
                if name == "o1":
                    for k in range(4):
                        split_expert(k, 0)
                oh_ = int(name[-1]) if name[-1].isdigit() else 0
                for b in range(j["banks"]):
                    pb = bank_of(j, b)
                    if b == 1 and split_early(name) and not name.startswith("xT"):
                        split(j["sub_end"] + LEAD + 1)
                    base = j["base"]
                    if base in ("xT", "mT"):
                        bank_filled(act, j, b)
                        if name == "mT0" and b == 0:
                            act.wait_ge(s_bias, NT)
                        nc.scalar.activation((xnh if base == "xT" else mbh)[:, 4 * oh_ + b, :], pb[:, 0:N], ACT.Copy).then_inc(s_ahi, 1)
                    elif base in into:
                        bank_filled(act, j, b)
                        o = 4 * oh_ + b
                        nc.scalar.activation(into[base][:, o, :], pb[:, 0:N], ACT.Identity,
                                             bias=col[:, colno[bias_of[base]], o:o + 1]).then_inc(s_ahi, 1)
                    elif base in ("mq", "mk"):
                        width = N if base == "mq" else HALF
                        bank_filled(act, j, b)
                        if len(elu_banks) >= 2:
                            act.wait_ge(s_free, elu_banks[-2] + 1)
                        t = etmp[:, len(elu_banks) % 2, 0:width]
                        link(nc.scalar.activation(t, pb[:, 0:width], ACT.Relu, scale=-1.0))
                        nc.scalar.activation(t, t, ACT.Exp, scale=-1.0).then_inc(s_ahi, 1)
                        elu_banks.append(j["first"] + b)
            act.wait_ge(s_free, jobs["o1"]["first"] + jobs["o1"]["banks"] + att_units)
            for t in range(NT):
                act.dma_start(out[t * P:(t + 1) * P, :], acc[:, t, :]).then_inc(s_out, 16)
            for t in range(NT):
                act.wait_ge(s_xt, t + 1)
                act.dma_start(xt_dram[t * P:(t + 1) * P, :], xt[:, t, :]).then_inc(s_xtd, 16)
            for b in range(1, DC, 2):
                act.wait_ge(s_t, H * NT + b + 1)
                nc.scalar.activation(xtT[:, b, :], ps[xt_bank(b)][:, 0:N], ACT.Copy).then_inc(s_lga, 1)
            for k in range(4, 4 + XLEAD):
                split_expert(k, 0)
            act.wait_ge(s_r_t, 1)
            nc.scalar.activation(gates[:, :, :], ps[2][:, 0:NT * NE].rearrange("p (t e) -> p t e", e=NE), ACT.Exp,
                                 scale=-1.0).then_inc(s_ra, 1)

            def x_hi(count, p):
                act.wait_ge(s_xT, count)
                for b in range(2):
                    ins = nc.scalar.activation(xgTh[p][:, 4 * b:4 * b + 4, :], ps[2 + b][:, :].rearrange("p (c t) -> p c t", t=P), ACT.Copy)
                ins.then_inc(s_xhi, 1)

            def h_out(used, s):
                act.wait_ge(s_used, used)
                nc.scalar.activation(hsb[:, :], ps[0][:, :], ACT.Relu, scale=tabf[:, 1, bass.ds(s, 1)]).then_inc(s_h, 1)

            def h_hi(count, p):
                act.wait_ge(s_hT, count)
                nc.scalar.activation(hTh[p][:, :, :], ps[1][:, :].rearrange("p (c t) -> p c t", t=P), ACT.Copy).then_inc(s_hhi, 1)

            def y_second(j, p, used):
                act.wait_ge(s_used, used)
                act.wait_ge(s_scd, 2 * j + p + 1)
                nc.scalar.activation(ysb[p][:, HALF:D], ps[5 + 2 * p][:, :], ACT.Copy).then_inc(s_ye1, 1)

            def act_slot(j, p, ahead):
                k = 8 * p
                used = SUBS + 8 * p + 16 * j
                for q in range(8, 10):
                    split_expert(k + q, j)
                h_out(used + 8, 2 * j + p + 1)
                split_expert(k + 10, j)
                if ahead:
                    x_hi(2 * j + p + 3, p)
                split_expert(k + 11, j)
                h_hi(2 * j + p + 2, 1 - p)
                for q in range(12, 14):
                    split_expert(k + q, j)
                y_second(j, p, used + 12)
                for q in range(14, 16):
                    split_expert(k + q, j)

            act.wait_ge(s_tab, 1)
            last = act.value_load(slots[0:1, 0:1], min_val=PAIRS_MIN - 1, max_val=PAIRS_MAX - 1)
            act.sem_inc(s_ye1, 2)
            x_hi(1, 0)
            x_hi(2, 1)
            h_out(SUBS + 4, 0)
            h_hi(1, 0)
            with act.Fori(0, last) as j:
                for p in range(2):
                    act_slot(j, p, True)
            act_slot(last, 0, False)
            y_second(last, 1, SUBS + 16 + 16 * last)

        @block.vector
        def _(dve):
            chain = [0]

            def link(ins):
                chain[0] += 1
                ins.then_inc(s_dch, 1)
                dve.wait_ge(s_dch, chain[0])

            done = [0]

            def split(upto):
                for s in range(done[0], min(upto, SUBS)):
                    dve.wait_ge(s_hi, s + 1)
                    nc.vector.tensor_tensor(wl[:, s % SUB], raw[:, (s // 2) % RAW, 2 * (s % 2):2 * (s % 2) + 2, :],
                                            wh[:, s % SUB].bitcast(F32), ALU.subtract).then_inc(s_lo, 1)
                done[0] = max(done[0], min(upto, SUBS))

            def row_stats(t, k):
                link(nc.vector.bn_stats(stats[:, t, k, :], acc[:, t, k * 512:(k + 1) * 512]))

            def norms(t0, t1, out_tile, done_sem):
                for t in range(t0, t1):
                    link(nc.vector.bn_aggr(mv2[:, t, 0:2], stats[:, t, :, :].rearrange("p a b -> p (a b)")))
                v, y, z = mv2[:, t0:t1, 1], mv2[:, t0:t1, 2], mv2[:, t0:t1, 3]
                link(nc.vector.tensor_scalar(v, v, EPS_LN, None, ALU.add))
                link(nc.vector.tensor_single_scalar(z.bitcast(I32), v.bitcast(I32), 1, ALU.logical_shift_right))
                link(nc.vector.tensor_scalar(y.bitcast(I32), z.bitcast(I32), -1.0, float(0x5F3759DF), ALU.mult, ALU.add))
                for _ in range(3):
                    link(nc.vector.tensor_tensor(z, y, y, ALU.mult))
                    link(nc.vector.tensor_tensor(z, z, v, ALU.mult))
                    link(nc.vector.tensor_scalar(z, z, -0.5, 1.5, ALU.mult, ALU.add))
                    link(nc.vector.tensor_tensor(y, y, z, ALU.mult))
                for t in range(t0, t1):
                    nc.vector.tensor_scalar(out_tile[:, t, :], acc[:, t, :], mv2[:, t, 0:1], mv2[:, t, 2:3],
                                            ALU.subtract, ALU.mult).then_inc(done_sem, 1)

            for t in range(NT):
                dve.wait_ge(s_x[t], 16)
                for k in range(2):
                    row_stats(t, k)
            norms(0, NT, xn, s_xn)
            colno = {n: k for k, n in enumerate(COLS)}
            bias_of = {"v": "bv", "q": "bq", "k": "bk", "q2": "biq", "k2": "bik"}
            parts = {"v": (mah, mal), "q": (mbh, mbl), "k": (mah, mal)}
            ahi = 0
            elus = 0

            def split_expert(k, j):
                dve.wait_ge(s_hi, SUBS + k + 1 + 16 * j)
                nc.vector.tensor_tensor(wl_of[k % XSUB], raw_of[(k // 2) % XRAW][:, 2 * (k % 2):2 * (k % 2) + 2, :],
                                        wh_of[k % XSUB].bitcast(F32), ALU.subtract).then_inc(s_lo, 1)

            decode_at = ["mT1", "mo0", "mo1", "q0", "q1", "v20", "v21", "k0", "k1"]
            for name in order:
                j = jobs[name]
                if name == "att":
                    attention_dve(dve)
                    continue
                if not name.startswith("xT"):
                    split(j["sub_end"] + LEAD)
                half = int(name[-1]) if name[-1].isdigit() else 0
                base = j["base"]
                if name == "mq0":
                    dve.wait_ge(s_const, 16 * N_CONST)
                    link(nc.vector.tensor_copy(ef[:, 0:3, :], ei[:, :, :]))
                    nc.vector.scalar_tensor_tensor(ef[:, 3, :], ef[:, 0, :], float(N), ef[:, 1, :], ALU.mult, ALU.add).then_inc(s_key, 1)
                    dve.wait_ge(s_key, 1)
                    link(nc.vector.tensor_scalar(ei[:, 2, :], ef[:, 2, :], 3.0, None, ALU.add))
                    link(nc.vector.tensor_single_scalar(ei[:, 2, :], ei[:, 2, :], 3, ALU.bitwise_and))
                    link(nc.vector.tensor_tensor(ei[:, 2, :], ei[:, 2, :], cst["layer"][:, :], ALU.add))
                    link(nc.vector.tensor_single_scalar(code[:, :].bitcast(I32), ei[:, 2, :], 23, ALU.logical_shift_left))
                    nc.vector.scalar_tensor_tensor(w4[:, 1, :], w4[:, 0, :], -1.0, w4[:, 0, :], ALU.mult, ALU.max).then_inc(s_spl, 1)
                    link(nc.vector.memset(mv[:, :, :, P], 1.0))
                if name == "mq1":
                    dve.wait_ge(s_ra, 1)
                    link(nc.vector.scalar_tensor_tensor(w4[:, 4, :], w4[:, 0, :], 0.0, w4[:, 3, :], ALU.max, ALU.add))
                if name.startswith("edge"):
                    for c in range(LAYERS):
                        g = half * LAYERS + c
                        if g >= 4:
                            dve.wait_ge(s_ohu, g - 3)
                        nc.vector.tensor_scalar(ohs[:, g % 4, :], iotah[:, :], ef[:, 0, g:g + 1], None, ALU.is_equal)
                        nc.vector.tensor_scalar(ohd[:, g % 4, :], iotah[:, :], ef[:, 1, g:g + 1], ef[:, 2, g:g + 1],
                                                ALU.is_equal, ALU.mult).then_inc(s_oh, 1)
                for b in range(j["banks"]):
                    if b == 1 and (name.startswith("xT") or split_early(name)):
                        split(half if name.startswith("xT") else j["sub_end"] + LEAD + 1)
                    pb = ps[4 * j["set"] + b]
                    if name != "lin":
                        bank_filled(dve, j, b)
                    if name.startswith("dup"):
                        for q in range(4):
                            g = 16 * half + 4 * b + q
                            last = nc.vector.scalar_tensor_tensor(junk[:, :], pb[:, q * P:(q + 1) * P], ef[:, 3, g:g + 1],
                                                                  after[:, :], ALU.is_equal, ALU.mult, accum_out=dup[:, g:g + 1])
                            if q < 3:
                                link(last)
                        last.then_inc(s_free, 1)
                        dve.wait_ge(s_free, j["first"] + b + 1)
                        if name == "dup5" and b == 3:
                            link(nc.vector.scalar_tensor_tensor(ef[:, 2, :], dup[:, :], 0.5, code[:, :], ALU.is_lt, ALU.mult))
                    elif base in ("xT", "mT"):
                        hi, lo = (xnh, xnl) if base == "xT" else (mbh, mbl)
                        ahi += 1
                        dve.wait_ge(s_ahi, ahi)
                        nc.vector.tensor_tensor(lo[:, 4 * half + b, :], pb[:, 0:N], hi[:, 4 * half + b, :].bitcast(F32),
                                                ALU.subtract).then_inc(s_free, 1)
                    elif base in parts:
                        hi, lo = parts[base]
                        o = 4 * half + b
                        ahi += 1
                        dve.wait_ge(s_ahi, ahi)
                        nc.vector.scalar_tensor_tensor(lo[:, o, :], pb[:, 0:N], col[:, colno[bias_of[base]], o:o + 1],
                                                       hi[:, o, :].bitcast(F32), ALU.add, ALU.subtract).then_inc(s_free, 1)
                    elif base in ("mq", "mk"):
                        width = N if base == "mq" else HALF
                        to = mq[:, 4 * half + b, :] if base == "mq" else mk[:, b, half * HALF:(half + 1) * HALF]
                        t = etmp[:, elus % 2, 0:width]
                        ahi += 1
                        dve.wait_ge(s_ahi, ahi)
                        elus += 1
                        nc.vector.scalar_tensor_tensor(to, pb[:, 0:width], 0.0, t, ALU.max, ALU.add).then_inc(s_free, 1)
                    elif base in ("q2", "k2"):
                        o = 4 * half + b
                        to = q2 if base == "q2" else k2
                        nc.vector.tensor_scalar(to[:, o, :], pb[:, 0:N], col[:, colno[bias_of[base]], o:o + 1],
                                                float(HD) ** -0.5 if base == "q2" else 1.0, ALU.add, ALU.mult).then_inc(s_free, 1)
                    elif base == "mv":
                        nc.vector.tensor_copy(mv[:, b, 4 * half:4 * half + 4, 0:P], pb[:, :].rearrange("p (c e) -> p c e", e=P)).then_inc(s_free, 1)
                    elif base == "v2":
                        if half == 0 and b == 0:
                            dve.wait_ge(s_rows, 16 * N_ROWS)
                        cs = slice(half * HALF, (half + 1) * HALF)
                        nc.vector.tensor_tensor(v2[:, b, cs], pb[:, :], biv_b[:, cs], ALU.add).then_inc(s_free, 1)
                    elif base in ("mo", "o"):
                        cs = slice(half * HALF, (half + 1) * HALF)
                        nc.vector.tensor_tensor(acc[:, b, cs], pb[:, :], acc[:, b, cs], ALU.add).then_inc(s_free, 1)
                        if name == "o1":
                            dve.wait_ge(s_free, j["first"] + b + 1 + att_units)
                            row_stats(b, 1)
                            norms(b, b + 1, xt, s_xt)
                    elif name.startswith("edge"):
                        if half == 0:
                            nc.vector.tensor_copy(mask[:, b, :], pb[:, 0:N]).then_inc(s_free, 1)
                        else:
                            nc.vector.tensor_copy(mtmp[:, :], pb[:, 0:N]).then_inc(s_free, 1)
                            dve.wait_ge(s_free, j["first"] + b + 1)
                            link(nc.vector.copy_predicated(mask[:, b, :], mtmp[:, :].bitcast(U32), mtmp[:, :]))
                    elif name == "lin":
                        if b == 0:
                            bank_filled(dve, j, 2)
                        n = min(3, DC - 3 * b)
                        view = pb[:, 0:n * (P + 1)].rearrange("p (c e) -> p c e", e=P + 1)
                        nc.vector.tensor_tensor(kvks[:, 3 * b:3 * b + n, 0:P], view[:, :, 0:P],
                                                cst["pair"][:, None, :].to_broadcast([P, n, P]), ALU.mult)
                        for k in range(2):
                            last = nc.vector.tensor_scalar(kvks[:, 3 * b:3 * b + n, P + k], view[:, :, P], cst["pair"][:, k * HD:k * HD + 1],
                                                           None, ALU.mult)
                        last.then_inc(s_free, 1)
                    elif base == "mix":
                        n = min(3, DC - 3 * b)
                        view = pb[:, 0:n * (P + 2)].rearrange("p (c e) -> p c e", e=P + 2)
                        den, inv = qden[:, 0, 0:2 * n], qden[:, 1, 0:2 * n]
                        link(nc.vector.tensor_scalar(den.rearrange("p (c k) -> p c k", k=2), view[:, :, P:P + 2], EPS_MIX, None, ALU.add))
                        link(nc.vector.reciprocal(inv, den))
                        last = nc.vector.tensor_tensor(mixed[:, half, 3 * b * P:(3 * b + n) * P].rearrange("p (c k e) -> p c k e", k=2, e=HD),
                                                       view[:, :, 0:P].rearrange("p c (k e) -> p c k e", k=2),
                                                       inv.rearrange("p (c k) -> p c k", k=2)[:, :, :, None].to_broadcast([P, n, 2, HD]), ALU.mult)
                        last.then_inc(s_free, 1)
                        dve.wait_ge(s_free, j["first"] + b + 1)
                if name in decode_at:
                    edge_mask(link, decode_at.index(name) // 3, decode_at.index(name) % 3)
                if name == "o0":
                    for t in range(NT):
                        dve.wait_ge(s_free, j["first"] + t + 1 + att_units)
                        row_stats(t, 0)
                if name == "o1":
                    dve.wait_ge(s_free, j["first"] + j["banks"] + att_units)
            for b in range(0, DC, 2):
                dve.wait_ge(s_t, H * NT + b + 1)
                nc.vector.tensor_copy(xtT[:, b, :], ps[xt_bank(b)][:, 0:N]).then_inc(s_lg, 1)
            for k in range(5):
                split_expert(k, 0)
            rv = [0]

            def step(ins):
                rv[0] += 1
                ins.then_inc(s_rv, 1)

            def steps_done():
                dve.wait_ge(s_rv, rv[0])

            def rlink(ins):
                step(ins)
                steps_done()

            iota, own = cst["iota"], cst["own"]
            dve.wait_ge(s_r, 1)
            nc.vector.tensor_copy(logit[:, :], ps[xt_bank(0)][0:NE, 0:N]).then_inc(s_lg, 1)
            rlink(nc.vector.memset(small[:, 2, :], 0.0))
            dve.wait_ge(s_ra, 2)
            rlink(nc.vector.tensor_scalar(gates[:, :, :], gates[:, :, :], 1.0, None, ALU.add))
            rlink(nc.vector.reciprocal(gates[:, :, :], gates[:, :, :]))
            for t in range(NT):
                step(nc.vector.max(m8[:, t, :], gates[:, t, :]))
            steps_done()
            for t in range(NT):
                step(nc.vector.max_index(i8[:, t, :], m8[:, t, :], gates[:, t, :]))
            steps_done()
            rlink(nc.vector.tensor_copy(i8f[:, :, :], i8[:, :, :]))
            for t in range(NT):
                step(nc.vector.tensor_tensor(oh[:, t * TOPK:(t + 1) * TOPK, :], iota[:, None, 0:NE].to_broadcast([P, TOPK, NE]),
                                             i8f[:, t, 0:TOPK, None].to_broadcast([P, TOPK, NE]), ALU.is_equal))
            steps_done()
            nc.vector.tensor_reduce(member[:, :, :], oh[:, :, :].rearrange("p (t k) e -> p t e k", k=TOPK), AX_X, ALU.add)\
                .then_inc(s_mem, 1)
            split_expert(5, 0)
            dve.wait_ge(s_r, 2)
            ranks = ps[1][:, 0:NT * NE].rearrange("p (t e) -> p t e", e=NE)
            tot = ps[3][:, 0:NE]
            rlink(nc.vector.tensor_scalar(small[:, 1, :], tot, P + 0.5, None, ALU.is_gt))
            for t in range(2, NT):
                rlink(nc.vector.scalar_tensor_tensor(small[:, 1, :], tot, t * P + 0.5, small[:, 1, :], ALU.is_gt, ALU.add))
            rlink(nc.vector.tensor_tensor_scan(small[:, 3, :], small[:, 1, :], small[:, 2, :], 0.0, ALU.add, ALU.add))
            rlink(nc.vector.tensor_tensor(small[:, 4, :], small[:, 3, :], small[:, 1, :], ALU.subtract))
            rlink(nc.vector.tensor_scalar(small[:, 4, :], small[:, 4, :], float(P), float(P * (NE - 1)), ALU.mult, ALU.add))
            rlink(nc.vector.tensor_tensor(small[:, 5, :], small[:, 4, :], cst["first"][:, :], ALU.subtract))
            rlink(nc.vector.tensor_tensor(rank[:, :, :], ranks, cst["first"][:, None, :].to_broadcast([P, NT, NE]), ALU.add))
            rlink(nc.vector.scalar_tensor_tensor(further[:, :, :], ranks, P - 0.5, small[:, 5, None, :].to_broadcast([P, NT, NE]),
                                                 ALU.is_gt, ALU.mult))
            rlink(nc.vector.tensor_tensor(rank[:, :, :], rank[:, :, :], further[:, :, :], ALU.add))
            for t in range(NT):
                step(nc.vector.tensor_tensor(picked[:, t * TOPK:(t + 1) * TOPK, :], oh[:, t * TOPK:(t + 1) * TOPK, :],
                                             rank[:, t, None, :].to_broadcast([P, TOPK, NE]), ALU.mult))
            steps_done()
            rlink(nc.vector.tensor_reduce(pos[:, 0, :], picked[:, :, :], AX_X, ALU.add))
            posi = pos[:, 3, :].bitcast(I32)
            rlink(nc.vector.tensor_copy(posi, pos[:, 0, :]))
            step(nc.vector.tensor_single_scalar(pos[:, 1, :].bitcast(I32), posi, P - 1, ALU.bitwise_and))
            step(nc.vector.tensor_single_scalar(pos[:, 2, :].bitcast(I32), posi, 7, ALU.logical_shift_right))
            steps_done()
            step(nc.vector.tensor_copy(pos[:, 0, :], pos[:, 1, :].bitcast(I32)))
            step(nc.vector.tensor_copy(pos[:, 3, :], pos[:, 2, :].bitcast(I32)))
            steps_done()
            for t in range(NT):
                ks = slice(t * TOPK, (t + 1) * TOPK)
                step(nc.vector.tensor_tensor(inslot[:, ks, :], iota[:, None, 0:SLOTS].to_broadcast([P, TOPK, SLOTS]),
                                             pos[:, 3, ks, None].to_broadcast([P, TOPK, SLOTS]), ALU.is_equal))
                step(nc.vector.tensor_tensor(lane1h[:, ks, :], iota[:, None, 0:P].to_broadcast([P, TOPK, P]),
                                             pos[:, 0, ks, None].to_broadcast([P, TOPK, P]), ALU.is_equal))
                steps_done()
                step(nc.vector.tensor_tensor(slot1h[:, ks, 0, :], inslot[:, ks, :],
                                             own[:, NT + t, None, None].to_broadcast([P, TOPK, SLOTS]), ALU.mult))
                step(nc.vector.tensor_tensor(slot1h[:, ks, 1, :], inslot[:, ks, :],
                                             m8[:, t, 0:TOPK, None].to_broadcast([P, TOPK, SLOTS]), ALU.mult))
                steps_done()
                dve.sem_inc(s_1h, 1)
            rlink(nc.vector.tensor_tensor(cmp[:, :, :], small[:, 3, None, :].to_broadcast([P, SLOTS - NE, NE]),
                                          iota[:, 0:SLOTS - NE, None].to_broadcast([P, SLOTS - NE, NE]), ALU.is_le))
            rlink(nc.vector.tensor_reduce(tabf[:, 0, NE:SLOTS], cmp[:, :, :], AX_X, ALU.add))
            rlink(nc.vector.tensor_scalar(slotx[:, NE:SLOTS], tabf[:, 0, NE:SLOTS], float(NE - 1), None, ALU.min))
            rlink(nc.vector.tensor_copy(slotx[:, 0:NE], iota[:, 0:NE]))
            rlink(nc.vector.tensor_scalar(slots[:, :], small[:, 3, NE - 1:NE], float(NE - 1), None, ALU.add))
            nc.vector.tensor_single_scalar(slots[:, :], slots[:, :], 1, ALU.logical_shift_right).then_inc(s_slots, 1)
            dve.wait_ge(s_slots, 1)
            dve.wait_ge(s_r, 3)
            tab = ps[2][:, 0:2 * SLOTS].rearrange("p (m s) -> p m s", s=SLOTS)
            step(nc.vector.tensor_scalar(gidx[:, :], tab[:, 0, :], -1.0, FAR, ALU.mult, ALU.add))
            step(nc.vector.tensor_copy(tabf[:, 1, :], tab[:, 1, :]))
            steps_done()
            dve.sem_inc(s_tab, 1)

            def x_lo(count, p):
                dve.wait_ge(s_xhi, count)
                for b in range(2):
                    ins = nc.vector.tensor_tensor(xgTl[p][:, 4 * b:4 * b + 4, :], ps[2 + b][:, :].rearrange("p (c t) -> p c t", t=P),
                                                  xgTh[p][:, 4 * b:4 * b + 4, :].bitcast(F32), ALU.subtract)
                ins.then_inc(s_xlo, 1)

            def h_lo(count, p):
                dve.wait_ge(s_hhi, count)
                nc.vector.tensor_tensor(hTl[p][:, :, :], ps[1][:, :].rearrange("p (c t) -> p c t", t=P),
                                        hTh[p][:, :, :].bitcast(F32), ALU.subtract).then_inc(s_hlo, 1)

            def y_first(j, p, used):
                dve.wait_ge(s_used, used)
                dve.wait_ge(s_scd, 2 * j + p + 1)
                nc.vector.tensor_copy(ysb[p][:, 0:HALF], ps[4 + 2 * p][:, :]).then_inc(s_ye0, 1)

            def dve_slot(j, p, ahead):
                k = 8 * p
                for q in range(8, 11):
                    split_expert(k + q, j)
                if ahead:
                    x_lo(2 * j + p + 3, p)
                split_expert(k + 11, j)
                y_first(j, p, SUBS + 10 + 8 * p + 16 * j)
                h_lo(2 * j + p + 2, 1 - p)
                for q in range(12, 16):
                    split_expert(k + q, j)

            dve.wait_ge(s_tab, 1)
            last = dve.value_load(slots[0:1, 0:1], min_val=PAIRS_MIN - 1, max_val=PAIRS_MAX - 1)
            dve.sem_inc(s_ye0, 2)
            for k in range(6, 8):
                split_expert(k, 0)
            x_lo(1, 0)
            x_lo(2, 1)
            h_lo(1, 0)
            with dve.Fori(0, last) as j:
                for p in range(2):
                    dve_slot(j, p, True)
            dve_slot(last, 0, False)
            y_first(last, 1, SUBS + 14 + 16 * last)

        @block.tensor
        def _(pe):
            def mm3(o, ah, al, bh_, bl_, start, stop):
                nc.tensor.matmul(o, ah, bh_, start=start, stop=False)
                nc.tensor.matmul(o, ah, bl_, start=False, stop=False)
                return nc.tensor.matmul(o, al, bh_, start=False, stop=stop)

            src_of = {"mq": (xnh, xnl), "mk": (xnh, xnl), "mv": (xnh, xnl), "v": (xnh, xnl), "q": (xnh, xnl), "k": (xnh, xnl),
                      "mo": (mbh, mbl), "v2": (mah, mal), "q2": (mbh, mbl), "k2": (mah, mal), "o": (mbh, mbl)}
            needs = {"mo": "mT", "v2": "v", "q2": "q", "k2": "k", "mq": "xT"}
            end = {n: jobs[n]["first"] + jobs[n]["banks"] for n in order}
            pe.wait_ge(s_const, 16 * N_CONST)
            for name in order:
                j = jobs[name]
                if name == "att":
                    attention_pe(pe)
                    continue
                half = int(name[-1]) if name[-1].isdigit() else 0
                base = j["base"]
                shift = att_units if name in ("o0", "o1") else 0
                bankwise = j["kind"] is not None and not name.startswith("o")
                if j["free"] and not bankwise:
                    pe.wait_ge(s_free, j["free"] + shift)
                if name == "o0":
                    pe.wait_ge(s_pt, att_units)
                    pe.wait_ge(s_o, H - 1)
                bk = [ps[4 * j["set"] + b] for b in range(4)]
                if name.startswith("dup"):
                    pe.wait_ge(s_key, 1)
                    for b in range(4):
                        for q in range(4):
                            g = 16 * half + 4 * b + q
                            last = nc.tensor.transpose(bk[b][:, q * P:(q + 1) * P], ef[:, 3, g:g + 1].to_broadcast([P, P]), ident[:, :])
                        last.then_inc(s_bank, 1)
                elif base in ("xT", "mT"):
                    if base == "mT":
                        pe.wait_ge(s_free, end["mix2"])
                    for t in range(NT):
                        if base == "xT":
                            pe.wait_ge(s_xn, t + 1)
                        for b in range(4):
                            o = 4 * half + b
                            last = nc.tensor.transpose(bk[b][:, t * P:(t + 1) * P], (xn if base == "xT" else mixed)[:, t, o * P:(o + 1) * P],
                                                       ident[:, :])
                            if t == NT - 1:
                                last.then_inc(s_bank, 1)
                elif name.startswith("edge"):
                    for c in range(LAYERS):
                        g = half * LAYERS + c
                        pe.wait_ge(s_oh, g + 1)
                        for t in range(NT):
                            last = nc.tensor.matmul(bk[t][:, 0:N], ohs[:, g % 4, t * P:(t + 1) * P], ohd[:, g % 4, :],
                                                    start=(c == 0), stop=(c == LAYERS - 1))
                            if c == LAYERS - 1 and t < NT - 1:
                                last.then_inc(s_bank, 1)
                        last.then_inc(s_ohu, 1)
                elif name == "lin":
                    pe.wait_ge(s_free, end["mv1"])
                    for c in range(DC):
                        for t in range(NT):
                            last = nc.tensor.matmul(bk[c // 3][:, (c % 3) * (P + 1):(c % 3 + 1) * (P + 1)], mk[:, t, c * P:(c + 1) * P],
                                                    mv[:, t, c, :], start=(t == 0), stop=(t == NT - 1))
                        if c % 3 == 2 or c == DC - 1:
                            last.then_inc(s_bank, 1)
                elif base == "mix":
                    if half == 0:
                        pe.wait_ge(s_free, end["lin"])
                    for c in range(DC):
                        last = nc.tensor.matmul(bk[c // 3][:, (c % 3) * (P + 2):(c % 3 + 1) * (P + 2)], mq[:, c, half * P:(half + 1) * P],
                                                kvks[:, c, :], start=True, stop=True)
                        if c % 3 == 2 or c == DC - 1:
                            last.then_inc(s_bank, 1)
                elif name == "o1":
                    for b in range(NT):
                        bs = slice(b * P, (b + 1) * P)
                        for q in range(4):
                            s = j["sub"] + q
                            if b == 0:
                                pe.wait_ge(s_lo, s + 1)
                            for kb in range(2):
                                i = 2 * q + kb
                                last = mm3(bk[b][:, :], mbh[:, i, bs], mbl[:, i, bs], wh[:, s % SUB, kb, :], wl[:, s % SUB, kb, :],
                                           i == 0, i == DC - 1)
                                if i == DC - 1 and b < NT - 1:
                                    last.then_inc(s_bank, 1)
                            if b == NT - 1:
                                last.then_inc(s_used, 1)
                else:
                    xh, xl = src_of[base]
                    for q in range(4):
                        s = j["sub"] + q
                        if base in needs and half == 0:
                            made_by = jobs[needs[base] + str(q // 2)]
                            pe.wait_ge(s_free, made_by["first"] + 2 * (q % 2) + 2)
                        if name == "o0":
                            pe.wait_ge(s_o, 4 * (q + 1))
                        pe.wait_ge(s_lo, s + 1)
                        for kb in range(2):
                            i = 2 * q + kb
                            first, fin = q == 0 and kb == 0, q == 3 and kb == 1
                            for b in range(j["banks"]):
                                if first and bankwise and j["free"]:
                                    pe.wait_ge(s_free, j["bank_free"][b])
                                if j["kind"] == "F":
                                    bs = slice(b * P, (b + 1) * P)
                                    last = mm3(bk[b][:, 0:N], wh[:, s % SUB, kb, bs], wl[:, s % SUB, kb, bs],
                                               xh[:, i, :], xl[:, i, :], first, fin)
                                else:
                                    bs = slice(b * P, (b + 1) * P)
                                    last = mm3(bk[b][:, :], xh[:, i, bs], xl[:, i, bs],
                                               wh[:, s % SUB, kb, :], wl[:, s % SUB, kb, :], first, fin)
                                if fin and b < j["banks"] - 1:
                                    last.then_inc(s_bank, 1)
                        last.then_inc(s_used, 1)

            for t in range(NT):
                pe.wait_ge(s_xt, t + 1)
                for b in range(DC):
                    if t == 0 and xt_bank(b) < NT:
                        pe.wait_ge(s_free, jobs["o1"]["first"] + xt_bank(b) + 1 + att_units)
                    last = nc.tensor.transpose(ps[xt_bank(b)][:, t * P:(t + 1) * P], xt[:, t, b * P:(b + 1) * P], ident[:, :])
                    if t == NT - 1:
                        last.then_inc(s_t, 1)
            for b in range(DC):
                pe.wait_ge((s_lg, s_lga)[b % 2], b // 2 + 1)
                last = nc.tensor.matmul(ps[xt_bank(0)][0:NE, 0:N], sel[:, b, :], xtT[:, b, :], start=(b == 0), stop=(b == DC - 1))
            last.then_inc(s_r, 1)
            pe.wait_ge(s_lg, DC // 2 + 1)
            for t in range(NT):
                last = nc.tensor.transpose(ps[2][:, t * NE:(t + 1) * NE], logit[:, t * P:(t + 1) * P], ident[0:NE, 0:NE])
            last.then_inc(s_r_t, 1)
            pe.wait_ge(s_mem, 1)
            nc.tensor.matmul(ps[1][:, 0:NT * NE], after[:, :], member[:, :, :].rearrange("p t e -> p (t e)"), start=True, stop=False)
            for t in range(1, NT):
                nc.tensor.matmul(ps[1][:, t * NE:NT * NE], ones[:, :], member[:, t - 1, None, :].to_broadcast([P, NT - t, NE]),
                                 start=False, stop=(t == NT - 1))
            for t in range(NT):
                last = nc.tensor.matmul(ps[3][:, 0:NE], ones[:, :], member[:, t, :], start=(t == 0), stop=(t == NT - 1))
            last.then_inc(s_r, 1)
            for q in range(NT * TOPK):
                if q % TOPK == 0:
                    pe.wait_ge(s_1h, q // TOPK + 1)
                last = nc.tensor.matmul(ps[2][:, 0:2 * SLOTS], lane1h[:, q, :], slot1h[:, q, :, :].rearrange("p m s -> p (m s)"),
                                        start=(q == 0), stop=(q == NT * TOPK - 1))
            last.then_inc(s_r, 1)

            def half_chunk(k, j, lhs, q, o, first, fin):
                pe.wait_ge(s_lo, SUBS + k + 1 + 16 * j)
                for kb in range(2):
                    b = 2 * q + kb
                    last = mm3(o, lhs[0][:, b, :], lhs[1][:, b, :], wh_of[k % XSUB][:, kb, :], wl_of[k % XSUB][:, kb, :],
                               first and kb == 0, fin and kb == 1)
                last.then_inc(s_used, 1)

            def do_keys(k, j, p, count, quarters=range(4)):
                pe.wait_ge(s_xlo, count)
                for q in quarters:
                    half_chunk(k + q, j, (xgTh[p], xgTl[p]), q, ps[0][:, :], q == 0, q == 3)

            def do_values(k, j, p, v):
                if v == 0:
                    pe.wait_ge(s_hlo, 2 * j + p + 1)
                pe.wait_ge((s_ye0, s_ye1)[v], 2 * j + p + 1)
                for q in range(2):
                    half_chunk(k + q, j, (hTh[p], hTl[p]), q, ps[4 + 2 * p + v][:, :], q == 0, q == 1)

            def x_T(p, landed):
                pe.wait_ge(s_g[p], landed)
                for b in range(DC):
                    last = nc.tensor.transpose(ps[2 + b // 4][:, (b % 4) * P:(b % 4 + 1) * P], xg[p][:, b * P:(b + 1) * P], ident[:, :])
                last.then_inc(s_xT, 1)

            def h_T(count):
                pe.wait_ge(s_h, count)
                for b in range(EF):
                    last = nc.tensor.transpose(ps[1][:, b * P:(b + 1) * P], hsb[:, b * P:(b + 1) * P], ident[:, :])
                last.then_inc(s_hT, 1)

            def pe_slot(j, p, ahead):
                do_keys(4 + 8 * p, j, 1 - p, 2 * j + p + 2)
                if ahead:
                    x_T(p, 16 * j + 32)
                do_values(8 + 8 * p, j, p, 0)
                h_T(2 * j + p + 2)
                do_values(10 + 8 * p, j, p, 1)

            pe.wait_ge(s_tab, 1)
            last_round = pe.value_load(slots[0:1, 0:1], min_val=PAIRS_MIN - 1, max_val=PAIRS_MAX - 1)
            x_T(0, 16)
            do_keys(0, 0, 0, 1, range(0, 1))
            x_T(1, 16)
            do_keys(0, 0, 0, 1, range(1, 4))
            h_T(1)
            with pe.Fori(0, last_round) as j:
                for p in range(2):
                    pe_slot(j, p, True)
            pe_slot(last_round, 0, False)
            do_values(12, last_round, 1, 0)
            do_values(14, last_round, 1, 1)


def kernel(**inputs):
    import numpy as _np
    import concourse.bacc as _bacc
    from concourse import mybir as _mybir
    from concourse.bass_utils import run_bass_kernel_spmd as _run

    nc = _bacc.Bacc("TRN2", target_bir_lowering=False, num_devices=1)
    arrays = {}

    def given(name, a):
        a = _np.ascontiguousarray(a)
        arrays["in_" + name] = a
        return nc.dram_tensor("in_" + name, a.shape, _mybir.dt.from_np(a.dtype), kind="ExternalInput").ap()

    a = {k: _np.asarray(v) for k, v in inputs.items()}

    def edge_layout(v):
        return v.reshape(EC, P).T

    def weight_layout(w):
        return w.T.reshape(2, 4, P, 2, HALF).transpose(3, 0, 2, 1, 4).reshape(4, P, 4, HALF)

    gnn, mix, ffn = "L0_gnn_", "L0_mix_", "L0_ffn_"
    names = {"mq": mix + "wq", "mk": mix + "wk", "mv": mix + "wv", "mo": mix + "wo", "q": gnn + "wq", "k": gnn + "wk",
             "v": gnn + "wv", "q2": gnn + "wiq", "k2": gnn + "wik", "v2": gnn + "wiv", "o": gnn + "wo"}
    W = {n: given("w_" + n, weight_layout(a[names[n]])) for n, _ in PROJ}
    cols = given("cols", _np.stack([a[gnn + n].reshape(DC, P).T for n in COLS], axis=1))
    rows = {n: given("row_" + n, a[k].reshape(1, D)) for n, k in (("bo", gnn + "bo"), ("mbo", mix + "bo"), ("biv", gnn + "biv"))}
    selT = given("sel", a[ffn + "expert_sel"].reshape(NE, DC, P).transpose(2, 1, 0))
    keys = given("keys", a[ffn + "keys"].reshape(NE, 2, 4, P, ES).transpose(0, 1, 3, 2, 4))
    values = given("values", a[ffn + "values"].reshape(NE, EF, P, 2, HALF).transpose(0, 3, 2, 1, 4))
    f4 = _np.float32
    p = _np.arange(P)
    tok = _np.arange(NT)[None, :] * P + p[:, None]
    consts = {
        "ident": _np.eye(P), "after": p[None, :] > p[:, None], "ones": _np.ones((P, P)),
        "pair": (p[None, :] // HD) == (p[:, None] // HD), "iota": _np.tile(_np.arange(N), (P, 1)),
        "layer": _np.tile(4 * (_np.arange(EC) % LAYERS) + 32, (P, 1)), "own": _np.concatenate([tok, FAR - tok], axis=1),
        "first": _np.tile(P * _np.arange(NE), (P, 1)),
    }
    C = {"all": given("c_all", _np.concatenate([_np.asarray(consts[n]).astype(f4) for n, _ in CONSTS_AT], axis=1))}
    C["iotah"] = given("c_iotah", consts["iota"].astype(_np.float16))
    xt_dram = nc.dram_tensor("xt_dram", (N, D), F32).ap()
    out = nc.dram_tensor("out_dram", (N, D), F32, kind="ExternalOutput").ap()
    gps_layer_kernel(nc, given("x", a["x"]), given("edges", _np.stack([edge_layout(a[n]) for n in ("src", "dst", "edge_type_5")], axis=1)),
                     given("etw", a[gnn + "edge_type_weights"].reshape(1, 4)),
                     W, cols, rows, selT, keys, values, C, xt_dram, out)
    r = _run(nc, [arrays], core_ids=[0])
    return r.results[0]["out_dram"]
```
